# Optimizing a Trainium2 kernel written in Bass

```python
import numpy as np
import jax
import jax.numpy as jnp

def _softmax(x, axis=-1):
    return jax.nn.softmax(x, axis=axis)
def _gelu(x):
    return jax.nn.gelu(x, approximate=True)
def _silu(x):
    return jax.nn.silu(x)
def _sigmoid(x):
    return jax.nn.sigmoid(x)
def _layernorm(x, axis=-1, eps=1e-5):
    m = jnp.mean(x, axis=axis, keepdims=True)
    v = jnp.var(x, axis=axis, keepdims=True)
    return (x - m) / jnp.sqrt(v + eps)
def _scatter_add(tgt, idx, src, axis=0):
    return tgt.at[idx].add(src)
def _segment_sum(src, seg, n):
    return jax.ops.segment_sum(src, seg, n)

kernel_name = 'mk_vit_tower_d1_tok_img256_3a817c'

def setup_inputs(seed: int = 0):
    np.random.seed(seed)
    _w = jnp.asarray
    def _rec_inputs():
        import jax
        import jax.numpy as jnp
        _rk = jax.random.key(seed)
        x = (-0.00016672 + 0.999947 * jax.random.normal(jax.random.fold_in(_rk, 1), (32, 3, 384, 384), jnp.float32))
        return x
    x = _rec_inputs()
    def _L0_tok_setup():
        import jax, jax.numpy as jnp
        import numpy as np
        PATCH = 16
        key = jax.random.key(seed)
        k1, k2, k3 = jax.random.split(key, 3)
        B, C, H, Wd = (64, 3, 384, 384)
        E = 256
        pdim = PATCH * PATCH * C
        x = jax.random.normal(k1, (B, C, H, Wd), dtype=jnp.float32)
        W = jax.random.normal(k2, (E, pdim), dtype=jnp.float32) * pdim ** (-0.5)
        b = jax.random.normal(k3, (E,), dtype=jnp.float32) * 0.01
        return {'x': x, 'W': W, 'b': b}
    _L0_tok_all = _L0_tok_setup()
    _L0_tok_in = {k: v for k, v in _L0_tok_all.items() if k in ('W', 'b', )}
    del _L0_tok_all

    def _L0_attn_setup():
        import jax, jax.numpy as jnp
        import numpy as np
        B, T, C = (16, 2048, 256)
        TT = T
        LAYER_ID, N_LAYER = (3, 6)
        key = jax.random.key(seed)
        ks = jax.random.split(key, 6)
        ratio_0_to_1 = LAYER_ID / (N_LAYER - 1)
        ratio_1_to_almost0 = 1.0 - LAYER_ID / N_LAYER
        h = np.arange(TT, dtype=np.float32)
        decay_speed = -5.0 + 8.0 * (h / (TT - 1)) ** (0.7 + 1.3 * ratio_0_to_1)
        curve = -(TT - 1 - h)
        time_w = jnp.asarray(np.exp(np.clip(curve * decay_speed, -30.0, 0.0)), dtype=jnp.float32)
        i = np.arange(C, dtype=np.float32) / C
        time_mix_k = jnp.asarray((i ** ratio_1_to_almost0).reshape(1, 1, C), dtype=jnp.float32)
        time_mix_v = jnp.asarray((i ** ratio_1_to_almost0 + 0.3 * ratio_0_to_1).reshape(1, 1, C), dtype=jnp.float32)
        time_mix_r = jnp.asarray((i ** (0.5 * ratio_1_to_almost0)).reshape(1, 1, C), dtype=jnp.float32)
        x = jax.random.normal(ks[0], (B, T, C), dtype=jnp.float32)
        scale = 0.02
        Wk = scale * jax.random.normal(ks[1], (C, C), dtype=jnp.float32)
        Wv = scale * jax.random.normal(ks[2], (C, C), dtype=jnp.float32)
        Wr = scale * jax.random.normal(ks[3], (C, C), dtype=jnp.float32)
        Wo = scale * jax.random.normal(ks[4], (C, C), dtype=jnp.float32)
        return {'x': x, 'time_w': time_w, 'time_mix_k': time_mix_k, 'time_mix_v': time_mix_v, 'time_mix_r': time_mix_r, 'Wk': Wk, 'Wv': Wv, 'Wr': Wr, 'Wo': Wo}
    _L0_attn_all = _L0_attn_setup()
    _L0_attn_in = {k: v for k, v in _L0_attn_all.items() if k in ('time_w', 'time_mix_k', 'time_mix_v', 'time_mix_r', 'Wk', 'Wv', 'Wr', 'Wo', )}
    del _L0_attn_all

    def _L0_ffn_setup():
        import jax, jax.numpy as jnp
        import numpy as np
        E, D, H, TOP_K = (6, 256, 256, 2)
        ROUTER_H = D // 2
        key = jax.random.key(seed)
        ks = jax.random.split(key, 12)
        s = 1.0 / np.sqrt(D)
        sh = 1.0 / np.sqrt(H)
        sr = 1.0 / np.sqrt(ROUTER_H)
        return {'features': jax.random.normal(ks[0], (8, 4096, D), dtype=jnp.float32), 'router_w1': jax.random.uniform(ks[1], (D, ROUTER_H), jnp.float32, -s, s), 'router_b1': jnp.zeros((ROUTER_H,), jnp.float32), 'router_w2': jax.random.uniform(ks[2], (ROUTER_H, E), jnp.float32, -sr, sr), 'router_b2': jnp.zeros((E,), jnp.float32), 'expert_w1': jax.random.uniform(ks[3], (E, D, H), jnp.float32, -s, s), 'expert_b1': jnp.zeros((E, H), jnp.float32), 'expert_w2': jax.random.uniform(ks[4], (E, H, H), jnp.float32, -sh, sh), 'expert_b2': jnp.zeros((E, H), jnp.float32), 'expert_w3': jax.random.uniform(ks[5], (E, H, D), jnp.float32, -sh, sh), 'expert_b3': jnp.zeros((E, D), jnp.float32)}
    _L0_ffn_all = _L0_ffn_setup()
    _L0_ffn_in = {k: v for k, v in _L0_ffn_all.items() if k in ('router_w1', 'router_b1', 'router_w2', 'router_b2', 'expert_w1', 'expert_b1', 'expert_w2', 'expert_b2', 'expert_w3', 'expert_b3', )}
    del _L0_ffn_all

    return {
        "x": x,
        "L0_tok_W": _L0_tok_in["W"],
        "L0_tok_b": _L0_tok_in["b"],
        "L0_attn_time_w": _L0_attn_in["time_w"],
        "L0_attn_time_mix_k": _L0_attn_in["time_mix_k"],
        "L0_attn_time_mix_v": _L0_attn_in["time_mix_v"],
        "L0_attn_time_mix_r": _L0_attn_in["time_mix_r"],
        "L0_attn_Wk": _L0_attn_in["Wk"],
        "L0_attn_Wv": _L0_attn_in["Wv"],
        "L0_attn_Wr": _L0_attn_in["Wr"],
        "L0_attn_Wo": _L0_attn_in["Wo"],
        "L0_ffn_router_w1": _L0_ffn_in["router_w1"],
        "L0_ffn_router_b1": _L0_ffn_in["router_b1"],
        "L0_ffn_router_w2": _L0_ffn_in["router_w2"],
        "L0_ffn_router_b2": _L0_ffn_in["router_b2"],
        "L0_ffn_expert_w1": _L0_ffn_in["expert_w1"],
        "L0_ffn_expert_b1": _L0_ffn_in["expert_b1"],
        "L0_ffn_expert_w2": _L0_ffn_in["expert_w2"],
        "L0_ffn_expert_b2": _L0_ffn_in["expert_b2"],
        "L0_ffn_expert_w3": _L0_ffn_in["expert_w3"],
        "L0_ffn_expert_b3": _L0_ffn_in["expert_b3"],
    }

def reference(x, L0_tok_W, L0_tok_b, L0_attn_time_w, L0_attn_time_mix_k, L0_attn_time_mix_v, L0_attn_time_mix_r, L0_attn_Wk, L0_attn_Wv, L0_attn_Wr, L0_attn_Wo, L0_ffn_router_w1, L0_ffn_router_b1, L0_ffn_router_w2, L0_ffn_router_b2, L0_ffn_expert_w1, L0_ffn_expert_b1, L0_ffn_expert_w2, L0_ffn_expert_b2, L0_ffn_expert_w3, L0_ffn_expert_b3):
    import jax
    import jax.numpy as jnp
    def _L0_tok_ref(x, W, b):
        import jax, jax.numpy as jnp
        import numpy as np
        PATCH = 16
        B, C, H, Wd = x.shape
        p = PATCH
        nH, nW = (H // p, Wd // p)
        patches = x.reshape(B, C, nH, p, nW, p)
        patches = patches.transpose(0, 2, 4, 1, 3, 5)
        patches = patches.reshape(B, nH * nW, C * p * p)
        return jnp.einsum('bnk,ek->bne', patches, W) + b

    def _L0_attn_ref(x, time_w, time_mix_k, time_mix_v, time_mix_r, Wk, Wv, Wr, Wo):
        import jax, jax.numpy as jnp
        import numpy as np
        B, T, C = (16, 2048, 256)
        TT = T
        LAYER_ID, N_LAYER = (3, 6)
        Bx, Tx, Cx = x.shape
        maxlen = time_w.shape[0]
        xx = jnp.pad(x, ((0, 0), (1, 0), (0, 0)))[:, :-1]
        xk = x * time_mix_k + xx * (1.0 - time_mix_k)
        xv = x * time_mix_v + xx * (1.0 - time_mix_v)
        xr = x * time_mix_r + xx * (1.0 - time_mix_r)
        k = jnp.exp(jnp.clip(xk @ Wk, -60.0, 30.0))
        v = xv @ Wv
        r = xr @ Wr
        sum_k = jnp.cumsum(k, axis=1)
        kv = k * v
        t_idx = jnp.arange(Tx)
        d = t_idx[:, None] - t_idx[None, :]
        W = jnp.where(d >= 0, time_w[jnp.clip(maxlen - 1 - d, 0, maxlen - 1)], 0.0)
        wkv = jnp.einsum('tu,buc->btc', W, kv)
        rwkv = jax.nn.sigmoid(r) * wkv / sum_k
        return rwkv @ Wo

    def _L0_ffn_ref(features, router_w1, router_b1, router_w2, router_b2, expert_w1, expert_b1, expert_w2, expert_b2, expert_w3, expert_b3):
        import jax, jax.numpy as jnp
        import numpy as np
        E, D, H, TOP_K = (6, 256, 256, 2)
        ROUTER_H = D // 2
        rh = jax.nn.relu(features @ router_w1 + router_b1)
        expert_logits = jax.nn.softmax(rh @ router_w2 + router_b2, axis=-1)
        top_w, top_i = jax.lax.top_k(expert_logits, TOP_K)
        routing_weights = jax.nn.softmax(top_w, axis=-1)
        h1 = jax.nn.relu(jnp.einsum('bsd,edh->bseh', features, expert_w1) + expert_b1)
        h2 = jax.nn.relu(jnp.einsum('bseh,ehf->bsef', h1, expert_w2) + expert_b2)
        expert_out = jnp.einsum('bsef,efo->bseo', h2, expert_w3) + expert_b3
        sel = jnp.take_along_axis(expert_out, top_i[:, :, :, None], axis=2)
        combined = jnp.sum(sel * routing_weights[..., None], axis=2)
        return combined

    h = _L0_tok_ref(x, L0_tok_W, L0_tok_b)
    h = h + _L0_attn_ref(_layernorm(h, axis=-1), L0_attn_time_w, L0_attn_time_mix_k, L0_attn_time_mix_v, L0_attn_time_mix_r, L0_attn_Wk, L0_attn_Wv, L0_attn_Wr, L0_attn_Wo)
    h = h + _L0_ffn_ref(_layernorm(h, axis=-1), L0_ffn_router_w1, L0_ffn_router_b1, L0_ffn_router_w2, L0_ffn_router_b2, L0_ffn_expert_w1, L0_ffn_expert_b1, L0_ffn_expert_w2, L0_ffn_expert_b2, L0_ffn_expert_w3, L0_ffn_expert_b3)
    return h


_drawn_inputs = setup_inputs


def setup_inputs(seed=0):
    import zlib

    import numpy as np

    out = dict(_drawn_inputs(seed))
    spreads = {'L0_ffn_router_b1': (0.0, 0.8),
     'L0_ffn_router_b2': (0.0, 0.8),
     'L0_ffn_expert_b1': (0.0, 2.0),
     'L0_ffn_expert_b2': (0.0, 2.0),
     'L0_ffn_expert_b3': (0.0, 2.0)}
    factors = {'L0_tok_b': 4.219,
     'L0_attn_time_w': 8.0,
     'L0_attn_time_mix_k': 8.0,
     'L0_attn_time_mix_v': 8.0,
     'L0_attn_time_mix_r': 8.0,
     'L0_attn_Wk': 8.0,
     'L0_attn_Wv': 8.0,
     'L0_attn_Wr': 8.0,
     'L0_attn_Wo': 8.0,
     'L0_ffn_router_w1': 8.0,
     'L0_ffn_router_w2': 8.0,
     'L0_ffn_expert_w1': 8.0,
     'L0_ffn_expert_w2': 8.0,
     'L0_ffn_expert_w3': 8.0}
    for name, (base, spread) in spreads.items():
        noise = np.random.default_rng([zlib.crc32(name.encode()), seed]).standard_normal(out[name].shape)
        drawn = base * np.exp(spread * noise) if base else spread * noise
        out[name] = jnp.asarray(drawn.astype(out[name].dtype))
    for name, factor in factors.items():
        out[name] = (out[name] * factor).astype(out[name].dtype)
    return out
```

```python
from contextlib import ExitStack

import numpy as np

import concourse.bass as bass
from concourse import mybir

F32, F16 = mybir.dt.float32, mybir.dt.float16
U32, I32 = mybir.dt.uint32, mybir.dt.int32
ALU = mybir.AluOpType
ACT = mybir.ActivationFunctionType
AX = mybir.AxisListType

P = 128
PATCH, SIDE, CH = 16, 24, 3
IMG = SIDE * SIDE
PAIR = 2 * IMG
TILES = PAIR // P
GROUP = 3 * P
D = 256
E = 6
QS = 8
KP = 2 * CH * PATCH
HALF = 288
BT = 512
ROW = 264
SLACK = 8192.0
LN_SCALE = 1024.0
EPS = 1e-5
EW_M, EW_B, EW_B3 = 0, 1536, 1540
EW = 1796
NEXT, THIS, LAST = 1, 0, -1

STEPS = (
    [("kv", 0), ("kv", 1), ("kv", 2), ("r", 0), ("tok", 0), ("rtt", 0), ("rtt", 1), ("rtt", 2), ("rh", 0)]
    + [("mix2", 2), ("kv", 3), ("kv", 4), ("kv", 5), ("r", 1), ("tok", 1), ("rtt", 3), ("rtt", 4), ("rtt", 5), ("rh", 1)]
    + [("kv", 6), ("kv", 7), ("kv", 8), ("r", 2), ("tok", 2), ("rtt", 6), ("rtt", 7), ("rtt", 8), ("rh", 2)]
    + [("norm1", 0), ("att", 0), ("top", 0), ("tok", 3), ("mix", 0), ("att", 1), ("rank", 0), ("scat", 0)]
    + [("tok", 4), ("scat", 1), ("att", 2), ("scat", 2), ("tok", 5), ("norm1", 1), ("scat", 3), ("att", 3)]
    + [("scat", 4), ("wo", 0), ("wo", 1), ("mix", 1), ("scat", 5), ("tok", 6), ("scat", 6), ("att", 4)]
    + [("scat", 7), ("wo", 2), ("scat", 8)]
    + [("norm2", 0), ("tok", 7), ("att", 5), ("wo", 3), ("tok", 8), ("att", 6)]
    + [("wo", 4), ("norm1", 2), ("wo", 5), ("norm2", 1), ("att", 7), ("wo", 6), ("wo", 7)]
    + [("wo", 8), ("norm2", 2)]
)
LEAD = {"tok": NEXT, "norm1": NEXT, "mix": NEXT, "mix2": THIS, "kv": THIS, "r": THIS, "att": THIS, "wo": THIS,
        "norm2": THIS, "rtt": LAST, "rh": LAST, "top": LAST, "rank": LAST, "scat": LAST}


class Signal:

    def __init__(self, sem, per, unit=1):
        self.sem, self.per, self.unit = sem, per, unit

    def after(self, pair, n=None):
        return (pair * self.per + (self.per if n is None else n + 1)) * self.unit


def wait(eng, signal, pair, n=None):
    v = signal.after(pair, n)
    if not isinstance(v, int) or v > 0:
        eng.wait_ge(signal.sem, v)


def hold(eng, spacer, signal, pair, n=None):
    wait(eng, signal, pair, n)
    eng.sem_inc(spacer, 1)


def iterations(eng, body, pairs, last=1):
    body(-1)
    body(0)
    with eng.Fori(1, pairs - last) as p:
        body(p)
    for p in range(pairs - last, pairs + 1):
        body(p)


def steps(p, pairs):
    for name, n in STEPS:
        q = p + LEAD[name]
        if not isinstance(p, int) or 0 <= q < pairs:
            yield name, n, q


def build(nc, x, tok_w, tok_b, decay, mix, wk, wv, wr, wo, rw1, rb1, rw2, rb2, ew1, eb1, ew2, eb2, ew3, eb3,
          out):
    images = x.shape[0]
    pairs = images // 2
    tokens = images * IMG
    region = tokens + BT
    btiles = (2 * tokens + E * (BT - 1)) // BT
    btiles += btiles % 2
    dummy = E * region
    assert pairs >= 4 and region * (E + 1) < 1 << 24

    ctx = ExitStack()
    with ctx:
        def sb(name, shape, dt=F32):
            return ctx.enter_context(nc.sbuf_tensor(name, shape, dt))

        def sem(name):
            return ctx.enter_context(nc.semaphore(name))

        def sig(name, per, unit=1):
            return Signal(sem(name), per, unit)

        lists = nc.dram_tensor("expert_lists", [dummy + BT, ROW], F32, kind="Internal").ap()
        packs = nc.dram_tensor("expert_packages", [E, P, EW], F32, kind="Internal").ap()
        skew = nc.dram_tensor("skewed_decay", [P * 800], F32, kind="Internal").ap()

        arena = sb("arena", [P, 2 * IMG * PATCH])
        embed_w = sb("embed_w", [KP, QS, D])
        embed_b = sb("embed_b", [P, D])
        h = sb("h", [P, 2, TILES, D])
        y1 = sb("y1", [P, 3, D])
        y1t = sb("y1t", [P, 2, 386])
        diff = sb("diff", [P, 2, GROUP])
        xf = sb("xf", [P, 2, 2, GROUP])
        xh = sb("xh", [P, 3, 2, 2 * GROUP], F16)
        xl = sb("xl", [P, 3, 2, 2 * GROUP], F16)
        k = sb("k", [P, TILES, D])
        kv = sb("kv", [P, TILES, D])
        gate = sb("gate", [P, 2, PAIR])
        rwh = sb("rwh", [P, 2, PAIR], F16)
        rwl = sb("rwl", [P, 2, PAIR], F16)
        h2 = sb("h2", [P, 3, D])
        y2 = sb("y2", [P, 3, D])
        row = sb("row", [P, TILES, ROW])
        y2t = sb("y2t", [P, 4, GROUP], F16)
        rh = sb("rh", [P, GROUP])
        wh = sb("wh", [P, 4, 2, D], F16)
        wl = sb("wl", [P, 4, 2, D], F16)
        rwa = sb("rwa", [P, 2, 2, P], F16)
        rw2s = sb("rw2s", [P, E])
        rb1s = sb("rb1s", [P, 1])
        rb2s = sb("rb2s", [P, E])
        mixs = sb("mixs", [P, 3, 2])
        dec = sb("dec", [P, 640])
        upto = sb("upto", [P, P])
        carry_w = sb("carry_w", [P, 5])
        before = sb("before", [P, P], F16)
        ones16 = sb("ones16", [P, P], F16)
        id16 = sb("id16", [P, P], F16)
        id32 = sb("id32", [P, P])
        half3 = sb("half3", [P, 3])
        zero2 = sb("zero2", [P, 2])
        st = sb("st", [P, 3, 6])
        mv1 = sb("mv1", [P, 3, 2])
        ve1 = sb("ve1", [P, 3])
        rs1 = sb("rs1", [P, 3])
        st2 = sb("st2", [P, 3, 6])
        mv2 = sb("mv2", [P, 3, 2])
        ve2 = sb("ve2", [P, 3])
        rs2 = sb("rs2", [P, 3])
        lg = sb("lg", [P, TILES, E])
        t1 = sb("t1", [P, TILES, E])
        oh1 = sb("oh1", [P, TILES, E])
        oh2 = sb("oh2", [P, TILES, E])
        t2 = sb("t2", [P, TILES, E])
        ex = sb("ex", [P, TILES, E])
        sel16 = sb("sel16", [P, TILES, E], F16)
        base = sb("base", [P, TILES + 1, E])
        rev = sb("rev", [P, TILES, E])
        m1 = sb("m1", [P, TILES, 1])
        m2 = sb("m2", [P, TILES, 1])
        g1 = sb("g1", [P, TILES, 1])
        g2 = sb("g2", [P, TILES, 1])
        posf = sb("posf", [P, 2, TILES])
        posu = sb("posu", [P, 2, TILES], U32)
        idf = sb("idf", [P, TILES])
        idi = sb("idi", [P, TILES], I32)
        mx = sb("mx", [P, 20])
        mxa = sb("mxa", [P, 20])
        omm = sb("omm", [P, 3, 2])
        bd = sb("bd", [P, 16])
        sc = sb("sc", [P, 16])
        isc = sb("isc", [P, 16])
        un = sb("un", [P, 16])
        cnt = sb("cnt", [P, E])
        nti = sb("nti", [P, E], I32)
        ntf = sb("ntf", [P, E])
        cum = sb("cum", [P, E + 1])
        tk = sb("tk", [1, btiles])
        tki = sb("tki", [1, btiles], I32)
        tge = sb("tge", [1, btiles])
        toff = sb("toff", [1, btiles])
        texp = sb("texp", [1, btiles])
        table = sb("table", [1, 2, btiles], I32)
        rbase = sb("rbase", [P, E])
        tails = sb("tails", [1, E], I32)
        fill_id = sb("fill_id", [P, 4], I32)

        def bank(name):
            return ctx.enter_context(nc.psum_tensor(name, [P, 512], F32))

        b_tok = [bank("b_tok0"), bank("b_tok1")]
        b_tr = bank("b_tr")
        b_rt = bank("b_rt")
        b_proj = [bank("b_proj0"), bank("b_proj1")]
        b_w = bank("b_w")
        b_s = bank("b_s")

        x_in = [sig("x_in0", 1, 96), sig("x_in1", 1, 96)]
        tok_done = sig("tok_done", TILES)
        h_ready = sig("h_ready", TILES)
        st1_ready = sig("st1_ready", TILES)
        mv1_ready = sig("mv1_ready", TILES)
        ve1_ready = sig("ve1_ready", 3)
        rs1_ready = sig("rs1_ready", 3)
        y1_ready = sig("y1_ready", TILES)
        tr_done = sig("tr_done", TILES)
        y1t_ready = sig("y1t_ready", TILES)
        diff_ready = sig("diff_ready", 3)
        xf_ready = sig("xf_ready", 9)
        xh_ready = sig("xh_ready", 9)
        xl_ready = sig("xl_ready", 3)
        xl_pool = sig("xl_pool", 6)
        kv_done = sig("kv_done", TILES)
        kc_ready = sig("kc_ready", TILES)
        k_ready = sig("k_ready", TILES)
        kv_ready = sig("kv_ready", TILES)
        r_done = sig("r_done", 6)
        rc_ready = sig("rc_ready", 6)
        e_ready = sig("e_ready", 6)
        gate_ready = sig("gate_ready", 6)
        sum_done = sig("sum_done", 8)
        wkv_done = sig("wkv_done", 8)
        den_ready = sig("den_ready", 8)
        inv_ready = sig("inv_ready", 8)
        rw_ready = sig("rw_ready", 8)
        rwh_ready = sig("rwh_ready", 8)
        rwl_ready = sig("rwl_ready", 8)
        wo_done = sig("wo_done", TILES)
        h2_ready = sig("h2_ready", TILES)
        h2_out = [sig(f"h2_out{i}", 3, 16) for i in range(3)]
        st2_ready = sig("st2_ready", TILES)
        mv2_ready = sig("mv2_ready", TILES)
        ve2_ready = sig("ve2_ready", 3)
        rs2_ready = sig("rs2_ready", 3)
        y2_ready = sig("y2_ready", TILES)
        yh_ready = sig("yh_ready", TILES)
        yl_ready = sig("yl_ready", TILES)
        rtt_done = sig("rtt_done", TILES)
        y2t_ready = sig("y2t_ready", TILES)
        rh_done = sig("rh_done", 3)
        rh_ready = sig("rh_ready", 3)
        lg_done = sig("lg_done", 3)
        lg_ready = sig("lg_ready", 3)
        TOP_LINKS = 20
        top_link = sig("top_link", TOP_LINKS)
        d_ready = sig("d_ready", 1)
        ex_ready = sig("ex_ready", 1)
        q_in = sig("q_in", 1)
        q_ready = sig("q_ready", 1)
        sel_ready = sig("sel_ready", 1)
        gw_ready = sig("gw_ready", 1)
        rank_done = sig("rank_done", 1)
        RANK_LINKS = 15
        rank_link = sig("rank_link", RANK_LINKS)
        pos_ready = sig("pos_ready", 1)
        scat = sig("rows_out", 2 * TILES, 16)

        dve_hold = sem("vector_hold")
        pool_hold = sem("pool_hold")
        ld = sem("weights_in")
        ld_e = sem("experts_in")
        setup_v = sem("setup_vector")
        setup_link = sem("setup_link")
        setup_p = sem("setup_pool")
        setup_a = sem("setup_scalar")
        amax_ready = sem("amax_ready")
        scales_ready = sem("scales_ready")
        skew_out = sem("skew_out")
        dec_in = sem("dec_in")
        pk_ready = sem("package_ready")
        pkh_ready = sem("package_high_ready")
        pk_out = [sem("package_out0"), sem("package_out1")]
        dump_out = sem("dump_rows_out")
        wsplit = sem("weights_high_ready")
        split_ready = sem("weights_split")

        W_S = {"k": 0, "v": 1, "r": 2, "o": 3, "r1": 4, "e1": 5, "e2": 6, "e3": 7}
        S_MIX, S_RW, S_H1, S_H2 = 8, 9, 10, 11
        NS = 12

        def col(t, i):
            return t[:, i:i + 1]

        raw_w = gate[:, :, :].rearrange("p a b -> p (a b)")[:, 0:2048].rearrange("p (m c n) -> p m c n", m=4, c=2)
        raw_r1 = k[:, 0, :].rearrange("p (c n) -> p c n", c=2)
        raw_e = arena[:, IMG * PATCH:].rearrange("p (e m c n) -> p e m c n", e=E, m=3, c=2)
        raw_b = k[:, 1, 0:24]
        raw_b3 = kv[:, 0:E, :]
        filler = xh[:].rearrange("p a b c -> p (a b c)").bitcast(F32)[:, 0:4 * ROW].rearrange("p (j w) -> p j w", j=4)
        zrow = h[:, 0, 4:8, :].rearrange("p a b -> p (a b)")[:, 0:768]
        pack = [h[:, 1, :, :].rearrange("p a b -> p (a b)")[:, 0:EW],
                h[:, 0, :, :].rearrange("p a b -> p (a b)")[:, 0:EW]]
        packm = [t[:, 0:1536].bitcast(F16).rearrange("p (m l c n) -> p m l c n", m=3, l=2, c=2) for t in pack]

        place = [0]

        def carve(words):
            place[0] += words
            assert place[0] <= 2 * IMG * PATCH
            return arena[:, place[0] - words:place[0]]

        def halves(t):
            return t.bitcast(F16).rearrange("p (l c s) -> p l c s", l=2, c=2)

        k_flat, kv_flat = k[:].rearrange("p a b -> p (a b)"), kv[:].rearrange("p a b -> p (a b)")

        packs_b = carve(E * EW).rearrange("p (e w) -> p e w", e=E)
        mats_b = arena[:, 0:E * EW].bitcast(F16).rearrange("p (e w) -> p e w", e=E)
        rows_b = [carve(4 * ROW).rearrange("p (j w) -> p j w", j=4) for _ in range(2)]
        bias_b = [carve(EW - EW_B) for _ in range(2)]
        yt_b = halves(carve(2 * BT))
        hid = [carve(2 * BT).rearrange("p (f s) -> p f s", f=2) for _ in range(2)]
        hid_b = [halves(k_flat[:, i * 2 * BT:(i + 1) * 2 * BT]) for i in range(2)]
        o_b = carve(4 * D).rearrange("p (j w) -> p j w", j=4)
        og_b = [kv_flat[:, i * 4 * D:(i + 1) * 4 * D].rearrange("p (j w) -> p j w", j=4) for i in range(2)]
        num_b = [carve(4) for _ in range(2)]
        gs_b = [carve(4) for _ in range(2)]
        bt_bank = b_tok
        hid_bank = [[b_tr, b_rt], [b_w, b_s]]
        o_bank = b_proj

        half_tiles = btiles // 2
        rows_in = [sig(f"rows_in{j}", 1, 16) for j in range(2)]
        packs_in = sem("packages_in")
        bias_ready = [sig(f"bias_ready{j}", 1) for j in range(2)]
        num_ready = [sig(f"num_ready{j}", 1) for j in range(2)]
        bt_done = [sig(f"bt_done{j}", 1) for j in range(2)]
        yth_ready = [sig(f"yth_ready{j}", 1) for j in range(2)]
        ytl_ready = [sig(f"ytl_ready{j}", 1) for j in range(2)]
        hid_done = [[sig(f"hid{m}_done{j}", 2) for j in range(2)] for m in range(2)]
        hid_ready = [[sig(f"hid{m}_ready{j}", 2) for j in range(2)] for m in range(2)]
        hidh_ready = [[sig(f"hid{m}h_ready{j}", 2) for j in range(2)] for m in range(2)]
        hidl_ready = [[sig(f"hid{m}l_ready{j}", 2) for j in range(2)] for m in range(2)]
        o_done = [sig(f"o_done{j}", 2) for j in range(2)]
        o_ready = [sig(f"o_ready{j}", 2) for j in range(2)]
        gs_ready = [sig(f"gs_ready{j}", 1) for j in range(2)]
        og_ready = [sig(f"og_ready{j}", 4) for j in range(2)]
        adds_out = [sig(f"adds_out{j}", 4, 16) for j in range(2)]
        table_ready = sem("table_ready")
        tails_out = sem("tails_out")
        table_link = sem("table_link")

        def tile_loop(eng, body):
            body(0)
            with eng.Fori(1, half_tiles - 1) as i:
                body(i)
            body(half_tiles - 1)

        def before_tile(i, j):
            return (i, 0) if j else (i - 1, 1)

        def exists(i):
            return not isinstance(i, int) or 0 <= i < half_tiles

        def entry(eng, what, i, j):
            n = 2 * i + j
            return eng.value_load(table[0:1, what, n:n + 1] if isinstance(i, int) else
                                  table[0:1, what, bass.ds(n, 1)], min_val=0, max_val=E - 1 if what else dummy)

        def stage_b_sync(sp):
            sp.wait_ge(table_ready, 2)
            sp.wait_ge(dump_out, 32)
            for e in range(E):
                at = sp.value_load(tails[0:1, e:e + 1], min_val=0, max_val=dummy)
                sp.dma_start(lists[bass.ds(at, BT)], lists[dummy:dummy + BT]).then_inc(tails_out, 16)
            sp.wait_ge(tails_out, 16 * E)
            wait(sp, scat, pairs - 1)

            def body(i):
                for j in range(2):
                    at = entry(sp, 0, i, j)
                    wait(sp, bt_done[j], i - 1)
                    wait(sp, num_ready[j], i - 1)
                    sp.dma_start(rows_b[j], lists[bass.ds(at, BT)].rearrange("(j p) w -> p j w", p=P)).then_inc(
                        rows_in[j].sem, 16)

            tile_loop(sp, body)
            for j in range(2):
                wait(sp, adds_out[j], half_tiles - 1)

        def stage_b_tensor(pe):
            mm = nc.tensor.matmul

            def transposes(i, j):
                wait(pe, rows_in[j], i)
                a, b = before_tile(i, j)
                wait(pe, yth_ready[b], a)
                wait(pe, ytl_ready[b], a)
                for l in range(2):
                    dst = bt_bank[l][:].bitcast(F16)
                    for c in range(2):
                        for t in range(4):
                            src = rows_b[j][:, t, l * P:(l + 1) * P].bitcast(F16)[:, c * P:(c + 1) * P]
                            last = nc.tensor.transpose(dst[:, c * BT + t * P:c * BT + (t + 1) * P], src, id16[:])
                last.then_inc(bt_done[j].sem, 1)

            def matrix(e, m, lw, c, first, n):
                first += ((m * 2 + lw) * 2 + c) * D
                return mats_b[:, bass.ds(e, 1), first:first + n].rearrange("p o n -> p (o n)")

            def hidden(m, i, j, e):
                a, b = before_tile(i, j)
                if m == 0:
                    wait(pe, yth_ready[j], i)
                    wait(pe, ytl_ready[j], i)
                    src = yt_b
                else:
                    wait(pe, hidh_ready[0][j], i)
                    wait(pe, hidl_ready[0][j], i)
                    src = hid_b[0]
                for f in range(2):
                    wait(pe, hid_ready[m][b], a, f)
                    parts = [(matrix(e, m, lw, c, f * P, P), src[:, lx, c, :]) for c in range(2)
                             for lx, lw in ((0, 0), (0, 1), (1, 0))]
                    for n, (l, r) in enumerate(parts):
                        last = mm(hid_bank[m][f][:], l, r, start=(n == 0), stop=(n == 5))
                    last.then_inc(hid_done[m][j].sem, 1)

            def output(i, j, e):
                a, b = before_tile(i, j)
                wait(pe, hidh_ready[1][j], i)
                wait(pe, hidl_ready[1][j], i)
                for u in range(2):
                    wait(pe, o_ready[b], a, u)
                    for t in (2 * u, 2 * u + 1):
                        parts = [(hid_b[1][:, lx, c, t * P:(t + 1) * P], matrix(e, 2, lw, c, 0, D)) for c in range(2)
                                 for lx, lw in ((0, 0), (0, 1), (1, 0))]
                        dst = o_bank[u][:, (t % 2) * D:(t % 2 + 1) * D]
                        for n, (l, r) in enumerate(parts):
                            last = mm(dst, l, r, start=(n == 0), stop=(n == 5))
                    last.then_inc(o_done[j].sem, 1)

            def body(i):
                expert = [entry(pe, 1, i, 0), entry(pe, 1, i, 1)]
                last = entry(pe, 1, i - 1, 1) if exists(i - 1) else None
                for j in range(2):
                    a, b = before_tile(i, j)
                    hidden(0, i, j, expert[j])
                    if exists(a):
                        output(a, b, expert[0] if j else last)
                    if j == 0:
                        transposes(i, 1)
                    elif not isinstance(i, int) or i + 1 < half_tiles:
                        transposes(i + 1, 0)
                    hidden(1, i, j, expert[j])

            wait(pe, pos_ready, pairs - 1)
            wait(pe, rw_ready, pairs - 1)
            wait(pe, h2_ready, pairs - 1)
            pe.wait_ge(table_ready, 2)
            pe.wait_ge(packs_in, 16 * E)
            transposes(0, 0)
            tile_loop(pe, body)
            output(half_tiles - 1, 1, entry(pe, 1, half_tiles - 1, 1))

        def stage_b_scalar(act):
            f_ = nc.scalar.activation

            def copy_high(i, j):
                wait(act, bt_done[j], i)
                a, b = before_tile(i, j)
                wait(act, hid_done[0][b], a)
                f_(yt_b[:, 0], bt_bank[0][:].bitcast(F16).rearrange("p (c s) -> p c s", c=2),
                   ACT.Copy).then_inc(yth_ready[j].sem, 1)

            def relu(m, i, j):
                a, b = before_tile(i, j)
                wait(act, bias_ready[j], i)
                for f in range(2):
                    wait(act, hid_done[m][j], i, f)
                    wait(act, hidl_ready[m][b], a, f)
                    f_(hid[m][:, f, :], hid_bank[m][f][:], ACT.Relu, scale=col(un, 5 + m),
                       bias=bias_b[j][:, 2 * m + f:2 * m + f + 1]).then_inc(hid_ready[m][j].sem, 1)

            def weighted(i, j):
                wait(act, gs_ready[j], i)
                wait(act, adds_out[j], i - 1)
                for t in range(4):
                    wait(act, o_ready[j], i, t // 2)
                    f_(og_b[j][:, t, :], o_b[:, t, :], ACT.Copy, scale=gs_b[j][:, t:t + 1]).then_inc(
                        og_ready[j].sem, 1)

            def body(i):
                for j in range(2):
                    a, b = before_tile(i, j)
                    relu(0, i, j)
                    if exists(a):
                        weighted(a, b)
                    if j == 0:
                        copy_high(i, 1)
                    elif not isinstance(i, int) or i + 1 < half_tiles:
                        copy_high(i + 1, 0)
                    relu(1, i, j)

            wait(act, wkv_done, pairs - 1)
            copy_high(0, 0)
            tile_loop(act, body)
            weighted(half_tiles - 1, 1)

        def stage_b_vector(dve):
            v = nc.vector
            count = [0]

            def link(ins):
                ins.then_inc(table_link, 1)
                count[0] += 1
                dve.wait_ge(table_link, count[0])

            v.tensor_copy(tails[:], base[0:1, 0, :])
            link(v.tensor_tensor(cnt[:], base[:, 0, :], rbase[:], ALU.subtract))
            link(v.tensor_scalar(cnt[:], cnt[:], float(BT - 1), None, ALU.add))
            link(v.tensor_copy(nti[:], cnt[:]))
            link(v.tensor_scalar(nti[:], nti[:], BT.bit_length() - 1, None, ALU.arith_shift_right))
            link(v.tensor_copy(ntf[:], nti[:]))
            link(v.memset(cum[:, 0:1], 0.0))
            for e in range(E):
                link(v.tensor_tensor(cum[:, e + 1:e + 2], cum[:, e:e + 1], ntf[:, e:e + 1], ALU.add))
            link(v.tensor_scalar(cnt[:], ntf[:], -float(BT), float(region), ALU.mult, ALU.add))
            v.memset(texp[:], 0.0)
            link(v.tensor_scalar(toff[:], tk[:], float(BT), None, ALU.mult))
            for e in range(E - 1):
                link(v.tensor_scalar(tge[:], tk[:], cum[0:1, e + 1:e + 2], None, ALU.is_ge))
                v.tensor_tensor(texp[:], texp[:], tge[:], ALU.add)
                link(v.scalar_tensor_tensor(toff[:], tge[:], cnt[0:1, e:e + 1], toff[:], ALU.mult, ALU.add))
            link(v.tensor_scalar(tge[:], tk[:], cum[0:1, E:E + 1], None, ALU.is_ge))
            link(v.tensor_scalar(tk[:], toff[:], -1.0, float(dummy), ALU.mult, ALU.add))
            link(v.tensor_tensor(tk[:], tk[:], tge[:], ALU.mult))
            link(v.tensor_tensor(toff[:], toff[:], tk[:], ALU.add))
            v.tensor_copy(table[:, 1, :], texp[:]).then_inc(table_ready, 1)
            v.tensor_copy(table[:, 0, :], toff[:]).then_inc(table_ready, 1)

            def copy_low(i, j):
                wait(dve, bt_done[j], i)
                a, b = before_tile(i, j)
                wait(dve, hid_done[0][b], a)
                v.tensor_copy(yt_b[:, 1], bt_bank[1][:].bitcast(F16).rearrange("p (c s) -> p c s", c=2)).then_inc(
                    ytl_ready[j].sem, 1)

            def biases(i, j, e):
                wait(dve, hid_ready[1][j], i - 1)
                wait(dve, o_ready[j], i - 1)
                v.tensor_copy(bias_b[j], packs_b[:, bass.ds(e, 1), EW_B:EW].rearrange("p o w -> p (o w)")).then_inc(
                    bias_ready[j].sem, 1)

            def gates(i, j, e):
                wait(dve, rows_in[j], i)
                wait(dve, adds_out[j], i - 1)
                v.tensor_copy(gs_b[j], rows_b[j][:, :, bass.ds(e + D, 1)].rearrange("p j o -> p (j o)")).then_inc(
                    gs_ready[j].sem, 1)
                v.tensor_copy(num_b[j].bitcast(U32), rows_b[j][:, :, D + E].bitcast(U32)).then_inc(
                    num_ready[j].sem, 1)

            def split(m, i, j):
                a, b = before_tile(i, j)
                for f in range(2):
                    wait(dve, hid_ready[m][j], i, f)
                    if m == 0:
                        wait(dve, hid_done[1][b], a)
                    else:
                        wait(dve, o_done[b], a)
                    v.tensor_copy(hid_b[m][:, 0, f, :], hid[m][:, f, :]).then_inc(hidh_ready[m][j].sem, 1)
                    wait(dve, hidh_ready[m][j], i, f)
                    v.tensor_tensor(hid_b[m][:, 1, f, :], hid[m][:, f, :], hid_b[m][:, 0, f, :],
                                    ALU.subtract).then_inc(hidl_ready[m][j].sem, 1)

            def out_bias(i, j):
                a, b = before_tile(i, j)
                for u in range(2):
                    wait(dve, o_done[j], i, u)
                    wait(dve, og_ready[b], a, 2 * u + 1)
                    b3 = bias_b[j][:, EW_B3 - EW_B:].unsqueeze(1).to_broadcast([P, 2, D])
                    v.scalar_tensor_tensor(o_b[:, 2 * u:2 * u + 2, :],
                                           o_bank[u][:].rearrange("p (t w) -> p t w", t=2), col(un, 7), b3,
                                           ALU.mult, ALU.add).then_inc(o_ready[j].sem, 1)

            def body(i):
                more = not isinstance(i, int) or i + 1 < half_tiles
                expert = [entry(dve, 1, i, 0), entry(dve, 1, i, 1)]
                following = entry(dve, 1, i + 1, 0) if more else None
                for j in range(2):
                    a, b = before_tile(i, j)
                    split(0, i, j)
                    if exists(a):
                        out_bias(a, b)
                    gates(i, j, expert[j])
                    if j == 0:
                        biases(i, 1, expert[1])
                        copy_low(i, 1)
                    elif more:
                        biases(i + 1, 0, following)
                        copy_low(i + 1, 0)
                    split(1, i, j)

            wait(dve, sum_done, pairs - 1)
            dve.wait_ge(table_ready, 2)
            dve.sem_inc(dve_hold, 1)
            first = entry(dve, 1, 0, 0)
            dve.wait_ge(packs_in, 16 * E)
            biases(0, 0, first)
            copy_low(0, 0)
            tile_loop(dve, body)
            out_bias(half_tiles - 1, 1)

        def stage_b_pool(pool):
            for s in h2_out:
                wait(pool, s, pairs - 1)
            pool.wait_ge(dump_out, 32)

            def body(i):
                for j in range(2):
                    a, b = before_tile(i, j)
                    wait(pool, num_ready[j], i)
                    wait(pool, adds_out[b], a)
                    for t in range(4):
                        hold(pool, pool_hold, og_ready[j], i, t)
                        nc.gpsimd.indirect_dma_start(
                            out, bass.IndirectOffsetOnAxis(ap=num_b[j][:, t:t + 1].bitcast(U32), axis=0),
                            og_b[j][:, t, :], None, compute_op=ALU.add).then_inc(adds_out[j].sem, 16)

            tile_loop(pool, body)

        block = ctx.enter_context(nc.Block())

        def group_slot(g):
            return slice(g % 2 * GROUP, (g % 2 + 1) * GROUP)

        def rows_of(image):
            if image == 0:
                return [(t, 0, P, P * t) for t in range(4)] + [(4, 0, 64, 512)]
            return [(4, 64, 64, 0)] + [(5 + t, 0, P, 64 + P * t) for t in range(4)]

        def block_of(n):
            return n // 4, (n // 2) % 2, n % 2

        def pieces(n):
            image, half, _ = block_of(n)
            a, b = half * HALF, (half + 1) * HALF
            got = []
            for i, (_, _, size, t0) in enumerate(rows_of(image)):
                lo, hi = max(a, t0), min(b, t0 + size)
                if lo < hi:
                    got.append((i, lo - a, hi - a))
            return got

        def block_cols(n):
            image, half, _ = block_of(n)
            return slice(image * IMG + half * HALF, image * IMG + (half + 1) * HALF)

        @block.sync
        def _(sp):
            def load_image(q, half):
                img = x[2 * q + half] if isinstance(q, int) else x[bass.ds(2 * q + half, 1)].rearrange(
                    "o c h w -> (o c) h w")
                v = img.rearrange("c (n r) w -> c r n w", r=PATCH)
                for g in range(2):
                    for c in range(CH):
                        part = (g * CH + c) * PATCH
                        dst = arena[part:part + PATCH, half * IMG * PATCH:(half + 1) * IMG * PATCH]
                        dst = dst.rearrange("p (n w) -> p n w", n=SIDE)[:, :, 0:SIDE * PATCH - QS * g]
                        sp.dma_start(dst, v[c][:, :, QS * g:]).then_inc(x_in[half].sem, 16)

            load_image(0, 0)
            sp.dma_start(embed_w[:], tok_w).then_inc(ld, 16)
            sp.dma_start(embed_b[:], tok_b).then_inc(ld, 16)
            for i, w in enumerate((wk, wv, wr, wo)):
                sp.dma_start(raw_w[:, i], w.rearrange("(c p) n -> p c n", c=2)).then_inc(ld, 16)
            sp.dma_start(raw_r1, rw1.rearrange("(c p) n -> p c n", c=2)).then_inc(ld, 16)
            sp.dma_start(rw2s[:], rw2).then_inc(ld, 16)
            sp.dma_start(rb1s[:], rb1).then_inc(ld, 16)
            sp.dma_start(rb2s[:], rb2).then_inc(ld, 16)
            sp.dma_start(mixs[:], mix).then_inc(ld, 16)
            sp.dma_start(zrow[:, 128:768], decay).then_inc(ld, 16)
            sp.dma_start(raw_b[:, 0:12], eb1).then_inc(ld_e, 16)
            sp.dma_start(raw_b[:, 12:24], eb2).then_inc(ld_e, 16)
            sp.dma_start(raw_b3, eb3).then_inc(ld_e, 16)
            for i, w in enumerate((ew1, ew2, ew3)):
                for e in range(E):
                    sp.dma_start(raw_e[:, e, i], w[e].rearrange("(c p) n -> p c n", c=2)).then_inc(ld_e, 16)
            sp.wait_ge(ld, 16 * 12)
            sp.wait_ge(setup_v, 1)
            sp.dma_start(skew.rearrange("(p s) -> p s", s=800)[:, 0:768], zrow).then_inc(skew_out, 16)
            sp.wait_ge(skew_out, 16)
            sp.dma_start(dec[:], skew[0:P * 799].rearrange("(p s) -> p s", s=799)[:, 128:768]).then_inc(dec_in, 16)
            for e in range(E):
                sp.wait_ge(pk_ready, e + 1)
                sp.wait_ge(pkh_ready, 4 * (e + 1))
                sp.dma_start(packs[e], pack[e % 2]).then_inc(pk_out[e % 2], 16)
            sp.wait_ge(setup_v, 4)
            sp.wait_ge(setup_p, 6)
            sp.dma_start(lists[dummy:dummy + BT].rearrange("(j p) w -> p j w", p=P), filler[:]).then_inc(dump_out, 16)
            sp.dma_start(out[tokens:tokens + BT].rearrange("(j p) w -> p j w", p=P),
                         filler[:, :, 0:D]).then_inc(dump_out, 16)
            load_image(0, 1)

            outv = out[0:tokens].rearrange("(q t p) w -> q t p w", t=TILES, p=P)

            def body(p):
                for name, n, q in steps(p, pairs):
                    more = not isinstance(q, int) or q + 1 < pairs
                    if name == "tok" and n == 4 and more:
                        wait(sp, tok_done, q, 4)
                        load_image(q + 1, 0)
                    if name == "tok" and n == 8 and more:
                        wait(sp, tok_done, q, 8)
                        load_image(q + 1, 1)
                    if name == "tok" and n == 8 and not more:
                        wait(sp, tok_done, q, 8)
                        sp.wait_ge(pk_out[0], 48)
                        sp.wait_ge(pk_out[1], 48)
                        for e in range(E):
                            sp.dma_start(packs_b[:, e, :], packs[e]).then_inc(packs_in, 16)
                    if name == "wo":
                        wait(sp, h2_ready, q, n)
                        dst = outv[q, n] if isinstance(q, int) else outv[bass.ds(q, 1), n].rearrange(
                            "o p w -> (o p) w")
                        sp.dma_start(dst, h2[:, n % 3, :]).then_inc(h2_out[n % 3].sem, 16)

            iterations(sp, body, pairs, last=2)
            for s in h2_out:
                wait(sp, s, pairs - 1)
            stage_b_sync(sp)

        @block.tensor
        def _(pe):
            mm = nc.tensor.matmul

            def embed(q, t):
                wait(pe, x_in[0 if t < 4 else 1], q)
                if t == 4:
                    wait(pe, x_in[0], q)
                bank_ = b_tok[t % 2]
                if t >= 2:
                    wait(pe, h_ready, q, t - 2)
                else:
                    wait(pe, h_ready, q - 1, 7 if t else 8)
                for j in range(QS):
                    a = t * P * PATCH + j
                    last = mm(bank_[:, 0:D], arena[0:KP, a:a + (P - 1) * PATCH + 1:PATCH], embed_w[:, j, :],
                              start=(j == 0), stop=(j == QS - 1))
                last.then_inc(tok_done.sem, 1)

            def norm1(q, g):
                for t in range(3 * g, 3 * g + 3):
                    wait(pe, y1_ready, q, t)
                    wait(pe, y1t_ready, q if t else q - 1, t - 1 if t else None)
                    for c in range(2):
                        last = nc.tensor.transpose(b_tr[:, c * P:(c + 1) * P], y1[:, t % 3, c * P:(c + 1) * P], id32[:])
                    last.then_inc(tr_done.sem, 1)

            def split_product(dst, parts):
                for i, (l, r) in enumerate(parts):
                    last = mm(dst, l, r, start=(i == 0), stop=(i == len(parts) - 1))
                return last

            def keys_values(q, t):
                g = t // 3
                if t % 3 == 0:
                    wait(pe, xh_ready, q, 3 * g + 1)
                    wait(pe, xl_ready, q, g)
                    wait(pe, xl_pool, q, 2 * g)
                dst = b_proj[t % 2]
                if t >= 2:
                    wait(pe, kv_ready, q, t - 2)
                else:
                    wait(pe, h2_ready, q - 1, 7 + t)
                s = slice(g % 2 * GROUP + t % 3 * P, g % 2 * GROUP + (t % 3 + 1) * P)
                for i in range(2):
                    parts = [(a[:, i, c, s], w[:, i, c, :]) for c in range(2)
                             for a, w in ((xh, wh), (xh, wl), (xl, wh))]
                    last = split_product(dst[:, i * D:(i + 1) * D], parts)
                last.then_inc(kv_done.sem, 1)

            def receptance(q, g):
                wait(pe, xh_ready, q, 3 * g + 2)
                wait(pe, xl_pool, q, 2 * g + 1)
                for f in range(2):
                    dst = (b_w, b_s)[f]
                    if g:
                        wait(pe, rc_ready, q, 2 * (g - 1) + f)
                    else:
                        wait(pe, rw_ready if f == 0 else den_ready, q - 1)
                    s = group_slot(g)
                    parts = [(w[:, 2, c, f * P:(f + 1) * P], a[:, 2, c, s]) for c in range(2)
                             for a, w in ((xh, wh), (xh, wl), (xl, wh))]
                    split_product(dst[:, 0:GROUP], parts).then_inc(r_done.sem, 1)

            def attend(q, n):
                image, half, f = block_of(n)
                rows = rows_of(image)
                a = half * HALF
                fs = slice(f * P, (f + 1) * P)
                mine = pieces(n)
                top = max(i for i, _, _ in mine)
                wait(pe, kv_ready, q, rows[top][0])
                if n:
                    wait(pe, den_ready, q, n - 1)
                else:
                    wait(pe, rc_ready, q, 5)
                for i, lo, hi in mine:
                    t, p0, size, t0 = rows[i]
                    s0 = a + lo - t0 + p0
                    mm(b_s[:, lo:hi], k[p0:p0 + size, t, fs], upto[p0:p0 + size, s0:s0 + hi - lo],
                       start=True, stop=True)
                firsts = [i for i, _, _ in mine]
                for i in range(top):
                    t, p0, size, _ = rows[i]
                    later = sum(1 for j in firsts if j > i)
                    last = mm(b_s[:, HALF:HALF + 3], k[p0:p0 + size, t, fs],
                              carry_w[p0:p0 + size, later - 1:later + 2],
                              start=(i == 0), stop=(i == top - 1))
                last.then_inc(sum_done.sem, 1)
                if n:
                    wait(pe, rw_ready, q, n - 1)
                else:
                    wait(pe, rc_ready, q, 4)
                for i in range(top + 1):
                    t, p0, size, t0 = rows[i]
                    lo = max(t0 - a, 0)
                    s0 = a + lo - t0 + p0
                    last = mm(b_w[:, lo:HALF], kv[p0:p0 + size, t, fs], dec[p0:p0 + size, s0:s0 + HALF - lo],
                              start=(i == 0), stop=(i == top))
                last.then_inc(wkv_done.sem, 1)

            def project(q, t):
                b = (P * t + P - 1) // HALF
                wait(pe, rwh_ready, q, 2 * b + 1)
                wait(pe, rwl_ready, q, 2 * b + 1)
                dst = b_proj[(TILES + t) % 2]
                if t >= 2:
                    wait(pe, h2_ready, q, t - 2)
                else:
                    wait(pe, kv_ready, q, 7 + t)
                s = slice(t * P, (t + 1) * P)
                parts = [(r[:, c, s], w[:, 3, c, :]) for c in range(2) for r, w in ((rwh, wh), (rwh, wl), (rwl, wh))]
                split_product(dst[:, 0:D], parts).then_inc(wo_done.sem, 1)

            def route_transpose(q, t):
                wait(pe, yh_ready, q, t)
                wait(pe, yl_ready, q, t)
                if t % 3:
                    wait(pe, y2t_ready, q, t - 1)
                elif t:
                    wait(pe, lg_ready, q, t // 3 - 1)
                else:
                    wait(pe, pos_ready, q - 1)
                src = row[:, t, 0:D].bitcast(F16)
                dst = b_rt[:, 0:D].bitcast(F16)
                for i in range(4):
                    last = nc.tensor.transpose(dst[:, i * P:(i + 1) * P], src[:, i * P:(i + 1) * P], id16[:])
                last.then_inc(rtt_done.sem, 1)

            def router(q, g):
                wait(pe, y2t_ready, q, 3 * g + 2)
                parts = [(rwa[:, lw, c, :], y2t[:, 2 * lx + c, :]) for c in range(2)
                         for lx, lw in ((0, 0), (0, 1), (1, 0))]
                split_product(b_rt[:, 0:GROUP], parts).then_inc(rh_done.sem, 1)
                wait(pe, rh_ready, q, g)
                for j in range(3):
                    last = mm(b_rt[:, j * E:(j + 1) * E], rh[:, j * P:(j + 1) * P], rw2s[:], start=True, stop=True)
                last.then_inc(lg_done.sem, 1)

            def rank(q):
                wait(pe, sel_ready, q)
                wait(pe, lg_ready, q, 2)
                rhs = sel16[:].rearrange("p t e -> p (t e)")
                mm(b_rt[:, 0:54], before[:], rhs, start=True, stop=True)
                mm(b_rt[:, 64:118], ones16[:], rhs, start=True, stop=True).then_inc(rank_done.sem, 1)

            def body(p):
                for name, n, q in steps(p, pairs):
                    if name == "tok":
                        embed(q, n)
                    elif name == "norm1":
                        norm1(q, n)
                    elif name == "kv":
                        keys_values(q, n)
                    elif name == "r":
                        receptance(q, n)
                    elif name == "att":
                        attend(q, n)
                    elif name == "wo":
                        project(q, n)
                    elif name == "rtt":
                        route_transpose(q, n)
                    elif name == "rh":
                        router(q, n)
                    elif name == "rank":
                        rank(q)

            pe.wait_ge(ld, 16 * 12)
            pe.wait_ge(setup_p, 7)
            pe.wait_ge(split_ready, 5)
            pe.wait_ge(setup_v, 4)
            pe.wait_ge(dec_in, 16)
            iterations(pe, body, pairs)
            stage_b_tensor(pe)

        @block.scalar
        def _(act):
            f = nc.scalar.activation

            def body(p):
                for name, n, q in steps(p, pairs):
                    if name == "norm1":
                        for t in range(3 * n, 3 * n + 3):
                            wait(act, tr_done, q, t)
                            if t % 3 == 0:
                                wait(act, diff_ready, q if n else q - 1, n - 1 if n else None)
                                wait(act, xf_ready, q if n else q - 1, 3 * n - 1 if n else None)
                                if n == 0:
                                    f(y1t[:, :, 0], zero2[:], ACT.Copy)
                                else:
                                    f(y1t[:, :, 0], y1t[:, :, 384 + (n == 2)], ACT.Copy)
                                    if n == 1:
                                        f(y1t[:, :, 193], zero2[:], ACT.Copy)
                            src = b_tr[:, 0:D].rearrange("p (c s) -> p c s", c=2)
                            a = 1 + (t % 3) * P
                            if t == 4:
                                f(y1t[:, :, a:a + 64], src[:, :, 0:64], ACT.Copy)
                                f(y1t[:, :, a + 65:a + 129], src[:, :, 64:128], ACT.Copy).then_inc(y1t_ready.sem, 1)
                            else:
                                a += t == 5
                                f(y1t[:, :, a:a + P], src, ACT.Copy).then_inc(y1t_ready.sem, 1)
                    elif name in ("mix", "mix2"):
                        s = group_slot(n)
                        old, pair = (0, q) if n == 2 else (2 - n, q - 1)
                        for i in range(3):
                            wait(act, xf_ready, q, 3 * n + i)
                            wait(act, kv_done if i < 2 else r_done, pair, 3 * old + 2 if i < 2 else 2 * old + 1)
                            f(xh[:, i, :, s], xf[:, (3 * n + i) % 2], ACT.Copy).then_inc(xh_ready.sem, 1)
                    elif name == "kv":
                        wait(act, kc_ready, q, n)
                        f(k[:, n, :], k[:, n, :], ACT.Exp, scale=col(un, 0)).then_inc(k_ready.sem, 1)
                    elif name == "r":
                        for i in range(2):
                            wait(act, rc_ready, q, 2 * n + i)
                            dst = gate[:, i, n * GROUP:(n + 1) * GROUP]
                            f(dst, dst, ACT.Exp, scale=col(un, 2)).then_inc(e_ready.sem, 1)
                        for i in range(2):
                            dst = gate[:, i, n * GROUP:(n + 1) * GROUP]
                            wait(act, e_ready, q, 2 * n + i)
                            f(dst, dst, ACT.Copy, bias=1.0).then_inc(gate_ready.sem, 1)
                    elif name == "att":
                        if n:
                            split_high(q, n - 1)
                        if n == 7:
                            split_high(q, 7)
                    elif name == "norm2":
                        for t in range(3 * n, 3 * n + 3):
                            wait(act, y2_ready, q, t)
                            if t == 0:
                                wait(act, scat, q - 1)
                            f(row[:, t, 0:P].bitcast(F16), y2[:, t % 3, :], ACT.Copy).then_inc(yh_ready.sem, 1)
                    elif name == "rtt":
                        wait(act, rtt_done, q, n)
                        if n % 3 == 0:
                            wait(act, rh_done, q if n else q - 1, n // 3 - 1 if n else None)
                        src = b_rt[:, 0:D].bitcast(F16).rearrange("p (i s) -> p i s", i=4)
                        f(y2t[:, :, (n % 3) * P:(n % 3 + 1) * P], src, ACT.Copy).then_inc(y2t_ready.sem, 1)
                    elif name == "rh":
                        wait(act, rh_done, q, n)
                        wait(act, lg_done, q if n else q - 1, n - 1 if n else None)
                        f(rh[:], b_rt[:, 0:GROUP], ACT.Relu, bias=rb1s[:], scale=col(un, 4)).then_inc(rh_ready.sem, 1)
                    elif name == "top":
                        wait(act, d_ready, q)
                        f(ex[:], t1[:], ACT.Exp).then_inc(ex_ready.sem, 1)
                        wait(act, q_in, q)
                        f(g2[:], g1[:], ACT.Exp).then_inc(q_ready.sem, 1)

            def split_high(q, n):
                wait(act, rw_ready, q, n)
                if n == 0:
                    wait(act, wo_done, q - 1)
                f(rwh[:, block_of(n)[2], block_cols(n)], gate[:, block_of(n)[2], block_cols(n)],
                  ACT.Copy).then_inc(rwh_ready.sem, 1)

            act.wait_ge(scales_ready, 1)
            for i, s in enumerate(("k", "v", "r", "o")):
                f(wh[:, i], raw_w[:, i], ACT.Copy, scale=col(sc, W_S[s])).then_inc(wsplit, 1)
            f(rwa[:, 0], raw_r1, ACT.Copy, scale=col(sc, 4)).then_inc(wsplit, 1)
            act.wait_ge(skew_out, 16)
            for e in range(E):
                if e >= 2:
                    act.wait_ge(pk_out[e % 2], 16 * (e // 2))
                for i in range(3):
                    f(packm[e % 2][:, i, 0], raw_e[:, e, i], ACT.Copy, scale=col(sc, 5 + i)).then_inc(pkh_ready, 1)
                f(pack[e % 2][:, EW_B:EW_B + 2], raw_b[:, 2 * e:2 * e + 2], ACT.Copy, scale=col(sc, S_H1))
                f(pack[e % 2][:, EW_B + 2:EW_B + 4], raw_b[:, 12 + 2 * e:14 + 2 * e], ACT.Copy, scale=col(sc, S_H2))
                f(pack[e % 2][:, EW_B3:EW_B3 + D], raw_b3[:, e, :], ACT.Copy).then_inc(pkh_ready, 1)
            act.wait_ge(dump_out, 32)
            iterations(act, body, pairs)
            stage_b_scalar(act)

        @block.vector
        def _(dve):
            v = nc.vector

            def tok(q, t):
                wait(dve, tok_done, q, t)
                dst = h[:, q % 2, t, :]
                v.tensor_tensor(dst, b_tok[t % 2][:, 0:D], embed_b[:], ALU.add).then_inc(h_ready.sem, 1)
                hold(dve, dve_hold, h_ready, q, t)
                v.bn_stats(st[:, t % 3, :], dst).then_inc(st1_ready.sem, 1)
                hold(dve, dve_hold, st1_ready, q, t)
                v.bn_aggr(mv1[:, t % 3, :], st[:, t % 3, :]).then_inc(mv1_ready.sem, 1)
                if t % 3 == 2:
                    wait(dve, mv1_ready, q, t)
                    v.tensor_scalar(ve1[:], mv1[:, :, 1], EPS, col(un, 9), ALU.add, ALU.mult).then_inc(ve1_ready.sem, 1)

            def norm1(q, g):
                wait(dve, rs1_ready, q, g)
                for t in range(3 * g, 3 * g + 3):
                    if t >= 3:
                        wait(dve, tr_done, q, t - 3)
                    else:
                        wait(dve, tr_done, q - 1, 6 + t)
                    v.tensor_scalar(y1[:, t % 3, :], h[:, q % 2, t, :], mv1[:, t % 3, 0:1], rs1[:, t % 3:t % 3 + 1],
                                    ALU.subtract, ALU.mult).then_inc(y1_ready.sem, 1)

            def mix_step(q, g):
                wait(dve, y1t_ready, q, 3 * g + 2)
                if g or not isinstance(q, int) or q:
                    wait(dve, xf_ready, q if g else q - 1, 3 * g - 1 if g else None)

                def at(c, first):
                    if g == 1:
                        return y1t[:, c, :].rearrange("p (a s) -> p a s", a=2)[:, :, first:first + 192]
                    return y1t[:, c, first:first + GROUP]

                def out_of(t):
                    return t.rearrange("p (a s) -> p a s", a=2) if g == 1 else t

                for c in range(2):
                    last = v.tensor_tensor(out_of(diff[:, c, :]), at(c, 1), at(c, 0), ALU.subtract)
                last.then_inc(diff_ready.sem, 1)
                wait(dve, diff_ready, q, g)
                for i in range(3):
                    n = 3 * g + i
                    free_xf(q, n)
                    for c in range(2):
                        last = v.scalar_tensor_tensor(out_of(xf[:, n % 2, c, :]), out_of(diff[:, c, :]),
                                                      mixs[:, i, c:c + 1], at(c, 0), ALU.mult, ALU.add)
                    last.then_inc(xf_ready.sem, 1)
                    if i == 1:
                        low_keys(q, g)

            def free_xf(q, n):
                m, pair = (n - 2, q) if n >= 2 else (8 - n, q - 1)
                wait(dve, xh_ready, pair, m)
                if m % 3 == 0:
                    wait(dve, xl_ready, pair, m // 3)
                else:
                    wait(dve, xl_pool, pair, 2 * (m // 3) + m % 3 - 1)

            def low_keys(q, g):
                wait(dve, xh_ready, q, 3 * g)
                s = group_slot(g)
                v.tensor_tensor(xl[:, 0, :, s], xf[:, (3 * g) % 2], xh[:, 0, :, s], ALU.subtract).then_inc(
                    xl_ready.sem, 1)

            def clip_keys(q, t):
                wait(dve, kv_done, q, t)
                if t == 0:
                    wait(dve, sum_done, q - 1)
                    wait(dve, kv_ready, q - 1)
                v.tensor_scalar(k[:, t, :], b_proj[t % 2][:, 0:D], col(un, 10), col(un, 11), ALU.max,
                                ALU.min).then_inc(kc_ready.sem, 1)

            def times_values(q, t):
                wait(dve, k_ready, q, t)
                if t == 0:
                    wait(dve, wkv_done, q - 1)
                v.scalar_tensor_tensor(kv[:, t, :], b_proj[t % 2][:, D:2 * D], col(un, 1), k[:, t, :], ALU.mult,
                                       ALU.mult).then_inc(kv_ready.sem, 1)

            def clip_receptance(q, g):
                for i in range(2):
                    wait(dve, r_done, q, 2 * g + i)
                    if g == 0 and i == 0:
                        wait(dve, rwl_ready, q - 1)
                    v.tensor_scalar(gate[:, i, g * GROUP:(g + 1) * GROUP], (b_w, b_s)[i][:, 0:GROUP], col(un, 13), None,
                                    ALU.max).then_inc(rc_ready.sem, 1)

            def denominators(q, n):
                image, half, f = block_of(n)
                wait(dve, sum_done, q, n)
                wait(dve, gate_ready, q, 5 if n >= 4 else 3)
                dst = gate[:, f, block_cols(n)]
                mine = pieces(n)
                for j, (i, lo, hi) in enumerate(mine):
                    if i == 0:
                        last = v.tensor_tensor(dst[:, lo:hi], b_s[:, lo:hi], dst[:, lo:hi], ALU.mult)
                    else:
                        cc = HALF + 3 - len(mine) + j
                        last = v.scalar_tensor_tensor(dst[:, lo:hi], b_s[:, lo:hi], b_s[:, cc:cc + 1], dst[:, lo:hi],
                                                      ALU.add, ALU.mult)
                last.then_inc(den_ready.sem, 1)

            def weigh(q, n):
                image, half, f = block_of(n)
                dst = gate[:, f, block_cols(n)]
                wait(dve, den_ready, q, n)
                v.reciprocal(dst, dst).then_inc(inv_ready.sem, 1)
                wait(dve, wkv_done, q, n)
                wait(dve, inv_ready, q, n)
                v.scalar_tensor_tensor(dst, b_w[:, 0:HALF], col(sc, S_RW), dst, ALU.mult, ALU.mult).then_inc(
                    rw_ready.sem, 1)

            def residual(q, t):
                wait(dve, wo_done, q, t)
                if t >= 3:
                    wait(dve, h2_out[t % 3], q, t // 3 - 1)
                else:
                    wait(dve, h2_out[t % 3], q - 1)
                    wait(dve, y2_ready, q - 1, 6 + t)
                dst = h2[:, t % 3, :]
                v.scalar_tensor_tensor(dst, b_proj[(TILES + t) % 2][:, 0:D], col(un, 3), h[:, q % 2, t, :], ALU.mult,
                                       ALU.add).then_inc(h2_ready.sem, 1)
                wait(dve, h2_ready, q, t)
                v.bn_stats(st2[:, t % 3, :], dst).then_inc(st2_ready.sem, 1)
                hold(dve, dve_hold, st2_ready, q, t)
                v.bn_aggr(mv2[:, t % 3, :], st2[:, t % 3, :]).then_inc(mv2_ready.sem, 1)
                if t % 3 == 2:
                    wait(dve, mv2_ready, q, t)
                    v.tensor_scalar(ve2[:], mv2[:, :, 1], EPS, LN_SCALE ** -2, ALU.add, ALU.mult).then_inc(
                        ve2_ready.sem, 1)

            def norm2(q, g):
                wait(dve, rs2_ready, q, g)
                for t in range(3 * g, 3 * g + 3):
                    if t >= 3:
                        wait(dve, yh_ready, q, t - 3)
                        wait(dve, yl_ready, q, t - 3)
                    else:
                        wait(dve, yh_ready, q - 1, 6 + t)
                        wait(dve, yl_ready, q - 1, 6 + t)
                    v.tensor_scalar(y2[:, t % 3, :], h2[:, t % 3, :], mv2[:, t % 3, 0:1], rs2[:, t % 3:t % 3 + 1],
                                    ALU.subtract, ALU.mult).then_inc(y2_ready.sem, 1)
                for t in range(3 * g, 3 * g + 3):
                    wait(dve, yh_ready, q, t)
                    v.tensor_tensor(row[:, t, P:D].bitcast(F16), y2[:, t % 3, :], row[:, t, 0:P].bitcast(F16),
                                    ALU.subtract).then_inc(yl_ready.sem, 1)

            def logits(q, g):
                wait(dve, lg_done, q, g)
                if g == 0:
                    wait(dve, pos_ready, q - 1)
                v.tensor_tensor(lg[:, 3 * g:3 * g + 3, :], b_rt[:, 0:3 * E].rearrange("p (t e) -> p t e", e=E),
                                rb2s[:].unsqueeze(1).to_broadcast([P, 3, E]), ALU.add).then_inc(lg_ready.sem, 1)

            def wide(t):
                return t[:].to_broadcast([P, TILES, E])

            def top2(q):
                count = [0]

                def link(ins):
                    ins.then_inc(top_link.sem, 1)
                    wait(dve, top_link, q, count[0])
                    count[0] += 1

                wait(dve, lg_ready, q, 2)
                link(v.tensor_reduce(m1[:], lg[:], AX.X, ALU.max))
                link(v.tensor_tensor(t2[:], lg[:], wide(m1), ALU.subtract))
                v.tensor_scalar(t1[:], t2[:], -87.33654, None, ALU.max).then_inc(d_ready.sem, 1)
                wait(dve, d_ready, q)
                link(v.scalar_tensor_tensor(t2[:], t1[:], 0.0, rev[:], ALU.is_ge, ALU.mult))
                link(v.tensor_reduce(m2[:], t2[:], AX.X, ALU.max))
                link(v.tensor_tensor(oh1[:], t2[:], wide(m2), ALU.is_equal))
                link(v.scalar_tensor_tensor(t2[:], oh1[:], -1e30, t1[:], ALU.mult, ALU.add))
                link(v.tensor_reduce(m1[:], t2[:], AX.X, ALU.max))
                link(v.tensor_tensor(t2[:], t2[:], wide(m1), ALU.is_equal))
                link(v.tensor_tensor(t2[:], t2[:], rev[:], ALU.mult))
                link(v.tensor_reduce(m2[:], t2[:], AX.X, ALU.max))
                link(v.tensor_tensor(oh2[:], t2[:], wide(m2), ALU.is_equal))
                v.tensor_tensor(sel16[:], oh1[:], oh2[:], ALU.add).then_inc(sel_ready.sem, 1)
                wait(dve, ex_ready, q)
                link(v.tensor_reduce(m2[:], ex[:], AX.X, ALU.add))
                link(v.tensor_tensor(t2[:], ex[:], oh2[:], ALU.mult))
                link(v.tensor_reduce(g1[:], t2[:], AX.X, ALU.add))
                link(v.reciprocal(m2[:], m2[:]))
                v.scalar_tensor_tensor(g1[:], g1[:], -1.0, m2[:], ALU.add, ALU.mult).then_inc(q_in.sem, 1)
                wait(dve, q_ready, q)
                link(v.tensor_scalar(m1[:], g2[:], 1.0, None, ALU.add))
                link(v.reciprocal(m1[:], m1[:]))
                link(v.tensor_tensor(g2[:], g2[:], m1[:], ALU.mult))
                link(v.tensor_tensor(t2[:], oh1[:], wide(m1), ALU.mult))
                link(v.tensor_tensor(t1[:], oh2[:], wide(g2), ALU.mult))
                assert count[0] == TOP_LINKS, count
                v.tensor_tensor(row[:, :, D:D + E], t1[:], t2[:], ALU.add).then_inc(gw_ready.sem, 1)

            def positions(q):
                count = [0]

                def link(ins):
                    ins.then_inc(rank_link.sem, 1)
                    wait(dve, rank_link, q, count[0])
                    count[0] += 1

                link(v.tensor_copy(row[:, :, D + E:D + E + 1].bitcast(U32), idf[:].unsqueeze(2)))
                link(v.tensor_scalar(idf[:], idf[:], float(PAIR), None, ALU.add))
                wait(dve, rank_done, q)
                totals = b_rt[:, 64:118].rearrange("p (t e) -> p t e", e=E)
                for t in range(TILES):
                    link(v.tensor_tensor(base[:, t + 1, :], base[:, t, :], totals[:, t, :], ALU.add))
                link(v.tensor_tensor(t1[:], b_rt[:, 0:54].rearrange("p (t e) -> p t e", e=E), base[:, 0:TILES, :],
                                     ALU.add))
                v.tensor_tensor(t2[:], t1[:], oh2[:], ALU.mult)
                link(v.tensor_tensor(t1[:], t1[:], oh1[:], ALU.mult))
                link(v.tensor_copy(base[:, 0, :], base[:, TILES, :]))
                v.tensor_reduce(posf[:, 1, :], t2[:], AX.X, ALU.add)
                link(v.tensor_reduce(posf[:, 0, :], t1[:], AX.X, ALU.add))
                assert count[0] == RANK_LINKS, count
                if not isinstance(q, int) or q:
                    wait(dve, scat, q - 1)
                v.tensor_copy(posu[:], posf[:]).then_inc(pos_ready.sem, 1)

            def body(p):
                for name, n, q in steps(p, pairs):
                    if name == "tok":
                        tok(q, n)
                    elif name == "norm1":
                        norm1(q, n)
                    elif name in ("mix", "mix2"):
                        mix_step(q, n)
                    elif name == "kv":
                        clip_keys(q, n)
                        if n:
                            times_values(q, n - 1)
                    elif name == "r":
                        clip_receptance(q, n)
                        if n == 2:
                            times_values(q, TILES - 1)
                    elif name == "att":
                        denominators(q, n)
                        weigh(q, n)
                    elif name == "wo":
                        residual(q, n)
                    elif name == "norm2":
                        norm2(q, n)
                    elif name == "rh":
                        logits(q, n)
                    elif name == "top":
                        top2(q)
                    elif name == "rank":
                        positions(q)

            chain = [0]

            def link(ins):
                ins.then_inc(setup_link, 1)
                chain[0] += 1
                dve.wait_ge(setup_link, chain[0])

            v.memset(zrow[:, 0:128], 0.0).then_inc(setup_v, 1)
            link(v.memset(mx[:], 0.0))
            v.memset(half3[:], -0.5)
            v.memset(zero2[:], 0.0)
            v.memset(row[:], 0.0).then_inc(setup_v, 1)
            dve.wait_ge(setup_p, 7)
            v.tensor_copy(id16[:], id32[:])
            v.tensor_copy(before[:], upto[:])
            v.tensor_copy(idf[:], idi[:])
            link(v.tensor_copy(tk[:], tki[:]))
            link(v.tensor_tensor(before[:], before[:], id16[:], ALU.subtract))
            for e in range(E):
                v.memset(rev[:, :, e], float(E - e))
                v.memset(rbase[:, e:e + 1], float(e * region))
            link(v.memset(ones16[:], 1.0))
            v.tensor_copy(base[:, 0, :], rbase[:]).then_inc(setup_v, 1)
            dve.wait_ge(ld, 16 * 12)
            dve.wait_ge(ld_e, 16 * 21)

            def largest(i, src, axis):
                link(v.tensor_reduce(mx[:, i:i + 1], src, axis, ALU.max, apply_absolute_value=True))

            for i in range(4):
                largest(i, raw_w[:, i], AX.XY)
            largest(4, raw_r1, AX.XY)
            for i in range(3):
                largest(5 + i, raw_e[:, :, i].rearrange("p e c n -> p e (c n)"), AX.XY)
            largest(8, mixs[:], AX.XY)
            link(v.tensor_scalar(omm[:], mixs[:], -1.0, 1.0, ALU.mult, ALU.add))
            largest(9, omm[:], AX.XY)
            largest(10, zrow[:, 128:768], AX.X)
            largest(11, raw_b[:, 0:12], AX.X)
            v.tensor_reduce(mx[:, 12:13], raw_b[:, 12:24], AX.X, ALU.max, apply_absolute_value=True).then_inc(
                amax_ready, 1)
            dve.wait_ge(setup_p, 8)

            def a(i):
                return mxa[:, i:i + 1]

            link(v.tensor_copy(bd[:, 0:8], mxa[:, 0:8]))
            link(v.tensor_scalar(bd[:, 8:9], a(8), a(9), 16.0, ALU.add, ALU.mult))
            link(v.tensor_scalar(bd[:, 9:10], bd[:, 8:9], a(1), 16.0, ALU.mult, ALU.mult))
            link(v.tensor_scalar(bd[:, 9:10], bd[:, 9:10], a(10), None, ALU.mult))
            link(v.tensor_scalar(bd[:, 10:11], a(5), 256.0, a(11), ALU.mult, ALU.add))
            link(v.tensor_scalar(bd[:, 11:12], bd[:, 10:11], a(6), 256.0, ALU.mult, ALU.mult))
            link(v.tensor_scalar(bd[:, 11:12], bd[:, 11:12], a(12), None, ALU.add))
            link(v.tensor_scalar(bd[:, 0:NS], bd[:, 0:NS], 1e-12, None, ALU.max))
            link(v.tensor_scalar(bd[:, 0:NS].bitcast(U32), bd[:, 0:NS].bitcast(U32), 0x7F800000, None,
                                 ALU.bitwise_and))
            link(v.reciprocal(sc[:, 0:NS], bd[:, 0:NS]))
            link(v.tensor_scalar(sc[:, 0:NS], sc[:, 0:NS], SLACK, None, ALU.mult))
            link(v.tensor_scalar(isc[:, 0:NS], bd[:, 0:NS], 1.0 / SLACK, None, ALU.mult))
            link(v.memset(un[:], 0.0))
            link(v.tensor_scalar(un[:, 0:3], isc[:, 0:3], isc[:, S_MIX:S_MIX + 1], None, ALU.mult))
            link(v.tensor_scalar(un[:, 2:3], un[:, 2:3], -1.0, None, ALU.mult))
            link(v.tensor_scalar(un[:, 3:4], isc[:, 3:4], isc[:, S_RW:S_RW + 1], None, ALU.mult))
            link(v.tensor_scalar(un[:, 4:5], isc[:, 4:5], 1.0 / LN_SCALE, None, ALU.mult))
            link(v.tensor_scalar(un[:, 5:6], isc[:, 5:6], 1.0 / LN_SCALE, sc[:, S_H1:S_H1 + 1], ALU.mult, ALU.mult))
            link(v.tensor_scalar(un[:, 6:7], isc[:, 6:7], isc[:, S_H1:S_H1 + 1], sc[:, S_H2:S_H2 + 1], ALU.mult,
                                 ALU.mult))
            link(v.tensor_scalar(un[:, 7:8], isc[:, 7:8], isc[:, S_H2:S_H2 + 1], None, ALU.mult))
            link(v.tensor_scalar(un[:, 9:10], isc[:, S_MIX:S_MIX + 1], isc[:, S_MIX:S_MIX + 1], None, ALU.mult))
            link(v.tensor_scalar(un[:, 12:13], sc[:, 0:1], sc[:, S_MIX:S_MIX + 1], None, ALU.mult))
            link(v.tensor_scalar(un[:, 10:11], un[:, 12:13], -60.0, None, ALU.mult))
            link(v.tensor_tensor(un[:, 14:15], sc[:, 2:3], sc[:, S_MIX:S_MIX + 1], ALU.mult))
            link(v.tensor_scalar(un[:, 13:14], un[:, 14:15], -50.0, None, ALU.mult))
            v.tensor_scalar(un[:, 11:12], un[:, 12:13], 30.0, None, ALU.mult).then_inc(scales_ready, 1)
            for i in range(4):
                dve.wait_ge(wsplit, i + 1)
                v.scalar_tensor_tensor(wl[:, i], raw_w[:, i], col(sc, i), wh[:, i], ALU.mult,
                                       ALU.subtract).then_inc(split_ready, 1)
            dve.wait_ge(wsplit, 5)
            v.scalar_tensor_tensor(rwa[:, 1], raw_r1, col(sc, 4), rwa[:, 0], ALU.mult, ALU.subtract).then_inc(
                split_ready, 1)
            dve.wait_ge(setup_p, 6)
            v.tensor_copy(filler[:, :, D + E:D + E + 1].bitcast(U32), fill_id[:].unsqueeze(2)).then_inc(setup_v, 1)
            for e in range(E):
                for i in range(3):
                    dve.wait_ge(pkh_ready, 4 * e + i + 1)
                    last = v.scalar_tensor_tensor(packm[e % 2][:, i, 1], raw_e[:, e, i], col(sc, 5 + i),
                                                  packm[e % 2][:, i, 0], ALU.mult, ALU.subtract)
                last.then_inc(pk_ready, 1)
            dve.wait_ge(pk_out[0], 48)
            dve.wait_ge(pk_out[1], 48)
            iterations(dve, body, pairs)
            stage_b_vector(dve)

        @block.gpsimd
        def _(pool):
            g_ = nc.gpsimd

            def low_half(q, n, i):
                s = group_slot(n)
                wait(pool, xh_ready, q, 3 * n + i)
                g_.tensor_tensor(xl[:, i, :, s], xf[:, (3 * n + i) % 2], xh[:, i, :, s], ALU.subtract).then_inc(
                    xl_pool.sem, 1)

            def low_sum(q, n):
                wait(pool, rwh_ready, q, n)
                f, s = block_of(n)[2], block_cols(n)
                g_.tensor_tensor(rwl[:, f, s], gate[:, f, s], rwh[:, f, s], ALU.subtract).then_inc(rwl_ready.sem, 1)

            def body(p):
                for name, n, q in steps(p, pairs):
                    if name == "tok" and n % 3 == 2:
                        wait(pool, ve1_ready, q, n // 3)
                        if n == 2:
                            wait(pool, y1_ready, q - 1)
                        else:
                            wait(pool, y1_ready, q, n - 3)
                        g_.tensor_tensor(rs1[:], ve1[:], half3[:], ALU.pow).then_inc(rs1_ready.sem, 1)
                    elif name == "wo" and n % 3 == 2:
                        wait(pool, ve2_ready, q, n // 3)
                        if n == 2:
                            wait(pool, y2_ready, q - 1)
                        else:
                            wait(pool, y2_ready, q, n - 3)
                        g_.tensor_tensor(rs2[:], ve2[:], half3[:], ALU.pow).then_inc(rs2_ready.sem, 1)
                    elif name in ("mix", "mix2"):
                        low_half(q, n, 1)
                        low_half(q, n, 2)
                    elif name == "att" and n:
                        low_sum(q, n - 1)
                        if n == 7:
                            low_sum(q, 7)
                    elif name == "scat":
                        wait(pool, gw_ready, q)
                        hold(pool, pool_hold, pos_ready, q)
                        for i in range(2):
                            g_.indirect_dma_start(lists, bass.IndirectOffsetOnAxis(ap=posu[:, i, n:n + 1], axis=0),
                                                  row[:, n, :], None).then_inc(scat.sem, 16)

            g_.memset(id32[:], 0.0).then_inc(setup_p, 1)
            g_.memset(upto[:], 1.0).then_inc(setup_p, 1)
            g_.memset(carry_w[:], 1.0).then_inc(setup_p, 1)
            pool.wait_ge(setup_p, 3)
            g_.memset(carry_w[:, 0:2], 0.0).then_inc(setup_p, 1)
            g_.memset(filler[:], 0.0).then_inc(setup_p, 1)
            g_.iota(fill_id[:], pattern=[[P, 4]], base=tokens, channel_multiplier=1).then_inc(setup_p, 1)
            g_.affine_select(out=id32[:], in_=id32[:], compare_op=ALU.not_equal, fill=1.0, base=0, pattern=[[-1, P]],
                             channel_multiplier=1)
            g_.affine_select(out=upto[:], in_=upto[:], compare_op=ALU.is_ge, fill=0.0, base=0, pattern=[[1, P]],
                             channel_multiplier=-1)
            g_.iota(tki[:], pattern=[[1, btiles]], base=0, channel_multiplier=0)
            g_.iota(idi[:], pattern=[[P, TILES]], base=0, channel_multiplier=1).then_inc(setup_p, 1)
            pool.wait_ge(amax_ready, 1)
            g_.partition_all_reduce(mxa[:], mx[:], P, bass.bass_isa.ReduceOp.max).then_inc(setup_p, 1)
            pool.wait_ge(setup_v, 3)
            iterations(pool, body, pairs)
            stage_b_pool(pool)


def kernel(x, L0_tok_W, L0_tok_b, L0_attn_time_w, L0_attn_time_mix_k, L0_attn_time_mix_v, L0_attn_time_mix_r,
           L0_attn_Wk, L0_attn_Wv, L0_attn_Wr, L0_attn_Wo, L0_ffn_router_w1, L0_ffn_router_b1, L0_ffn_router_w2,
           L0_ffn_router_b2, L0_ffn_expert_w1, L0_ffn_expert_b1, L0_ffn_expert_w2, L0_ffn_expert_b2,
           L0_ffn_expert_w3, L0_ffn_expert_b3):
    from concourse import bacc
    from concourse.bass_utils import run_bass_kernel_spmd

    def spread(a):
        a = np.asarray(a).reshape(1, -1)
        return np.broadcast_to(a, (P, a.shape[1]))

    def by_partition(a):
        return np.asarray(a).reshape(-1, 2, P).transpose(2, 0, 1).reshape(P, -1)

    mixes = np.stack([np.asarray(m).reshape(D) for m in (L0_attn_time_mix_k, L0_attn_time_mix_v,
                                                         L0_attn_time_mix_r)])
    arrays = {
        "x": np.asarray(x),
        "tok_w": np.asarray(L0_tok_W).reshape(D, CH, PATCH, 2, QS).transpose(3, 1, 2, 4, 0).reshape(KP, QS, D),
        "tok_b": spread(L0_tok_b),
        "decay": spread(np.asarray(L0_attn_time_w)[::-1][:640]),
        "mix": by_partition(mixes).reshape(P, 3, 2),
        "wk": L0_attn_Wk, "wv": L0_attn_Wv, "wr": L0_attn_Wr, "wo": L0_attn_Wo,
        "rw1": L0_ffn_router_w1, "rb1": np.asarray(L0_ffn_router_b1).reshape(P, 1),
        "rw2": L0_ffn_router_w2, "rb2": spread(L0_ffn_router_b2),
        "ew1": L0_ffn_expert_w1, "eb1": by_partition(L0_ffn_expert_b1),
        "ew2": L0_ffn_expert_w2, "eb2": by_partition(L0_ffn_expert_b2),
        "ew3": L0_ffn_expert_w3,
        "eb3": np.broadcast_to(np.asarray(L0_ffn_expert_b3).reshape(1, E, D), (P, E, D)),
    }
    arrays = {n: np.ascontiguousarray(a) for n, a in arrays.items()}
    images = arrays["x"].shape[0]
    nc = bacc.Bacc("TRN2", target_bir_lowering=False, num_devices=1)
    args = {n: nc.dram_tensor(f"in_{n}", a.shape, mybir.dt.from_np(a.dtype), kind="ExternalInput").ap()
            for n, a in arrays.items()}
    out = nc.dram_tensor("out_rows", (images * IMG + BT, D), F32, kind="ExternalOutput").ap()
    build(nc, out=out, **args)
    r = run_bass_kernel_spmd(nc, [{f"in_{n}": a for n, a in arrays.items()}], core_ids=[0])
    return r.results[0]["out_rows"][:images * IMG].reshape(images, IMG, D)
```

```python
from contextlib import ExitStack

import numpy as np

import concourse.bass as bass
from concourse import mybir

F32, F16 = mybir.dt.float32, mybir.dt.float16
U32, I32 = mybir.dt.uint32, mybir.dt.int32
ALU = mybir.AluOpType
ACT = mybir.ActivationFunctionType
AX = mybir.AxisListType

P = 128
PATCH, SIDE, CH = 16, 24, 3
IMG = SIDE * SIDE
PAIR = 2 * IMG
TILES = PAIR // P
GROUP = 3 * P
D = 256
E = 6
QS = 8
KP = 2 * CH * PATCH
HALF = 288
BT = 512
ROW = 264
SLACK = 8192.0
LN_SCALE = 1024.0
EPS = 1e-5
EW_M, EW_B, EW_B3 = 0, 1536, 1540
EW = 1796
NEXT, THIS, LAST = 1, 0, -1

STEPS = [
    ("embed", 0), ("receptance", 0), ("embed", 1), ("embedded", 0), ("difference2", 2), ("route_transpose", 0),
    ("embedded", 1), ("values", 0), ("route_transposed", 0), ("mixed2", 6), ("values", 1), ("clip_receptance", 0),
    ("route_transpose", 1), ("stats1", 0), ("embed", 2), ("route_transposed", 1), ("clip_keys", 0), ("clip_keys", 1),
    ("exp_keys", 0), ("exp_keys", 1), ("times_values", 0), ("times_values", 1), ("stats1", 1), ("route_transpose", 2),
    ("embedded", 2), ("values", 2), ("route_transposed", 2), ("stats1", 2), ("mean1", 0), ("mean1", 1), ("mean1", 2),
    ("values", 3), ("mixed_high2", 6), ("variance1", 0), ("mixed2", 7), ("root1", 0), ("router", 0), ("low_keys2", 2),
    ("mixed_high2", 7), ("receptance", 1), ("router_relu", 0), ("mixed2", 8), ("low_half2", 4), ("receptance", 2),
    ("norm1", 0), ("mixed_high2", 8), ("norm1", 1), ("transpose", 0), ("logits", 0), ("transposed", 0), ("embed", 3),
    ("add_logit_bias", 0), ("low_half2", 5), ("clip_keys", 2), ("clip_keys", 3), ("exp_keys", 2), ("exp_keys", 3),
    ("times_values", 2), ("exp_receptance", 0), ("clip_receptance", 1), ("times_values", 3), ("norm1", 2),
    ("clip_receptance", 2), ("transpose", 1), ("route_transpose", 3), ("transposed", 1), ("receptance", 3),
    ("embedded", 3), ("exp_receptance", 1), ("values", 4), ("clip_receptance", 3), ("route_transposed", 3),
    ("one_plus", 0), ("transpose", 2), ("exp_receptance", 2), ("clip_keys", 4), ("route_transpose", 4),
    ("receptance", 4), ("stats1", 3), ("exp_keys", 4), ("transposed", 2), ("receptance", 5), ("clip_receptance", 4),
    ("route_transposed", 4), ("times_values", 4), ("one_plus", 1), ("route_transpose", 5), ("clip_receptance", 5),
    ("values", 5), ("route_transposed", 5), ("difference", 0), ("one_plus", 2), ("router", 1), ("exp_receptance", 3),
    ("mixed", 0), ("one_plus", 3), ("sums", 0), ("router_relu", 1), ("mean1", 3), ("clip_keys", 5),
    ("exp_receptance", 4), ("logits", 1), ("denominators", 0), ("decayed", 0), ("exp_keys", 5), ("add_logit_bias", 1),
    ("one_plus", 4), ("invert", 0), ("route_transpose", 6), ("sums", 1), ("route_transposed", 6),
    ("route_transpose", 7), ("denominators", 1), ("values", 6), ("route_transposed", 7), ("weigh", 0), ("invert", 1),
    ("route_transpose", 8), ("sums", 2), ("route_transposed", 8), ("router", 2), ("denominators", 2),
    ("times_values", 5), ("sums", 3), ("router_relu", 2), ("clip_keys", 6), ("mixed", 1), ("exp_keys", 6),
    ("logits", 2), ("values", 7), ("add_logit_bias", 2), ("times_values", 6), ("top2", 0), ("values", 8),
    ("decayed", 1), ("mixed_high", 0), ("mixed_high", 1), ("invert", 2), ("embed", 4), ("exp_logits", 0),
    ("low_half", 0), ("weighed_high", 0), ("weigh", 1), ("clip_keys", 7), ("weighed_high", 1), ("low_keys", 0),
    ("low_sum", 0), ("exp_receptance", 5), ("rank", 0), ("exp_keys", 7), ("second", 0), ("decayed", 2),
    ("low_sum", 1), ("denominators", 3), ("exp_second", 0), ("one_plus", 5), ("gates", 0), ("sums", 4), ("weigh", 2),
    ("embed", 5), ("clip_keys", 8), ("denominators", 4), ("exp_keys", 8), ("weighed_high", 2), ("positions", 0),
    ("embedded", 4), ("low_sum", 2), ("times_values", 7), ("scatter", 0), ("sums", 5), ("times_values", 8),
    ("embedded", 5), ("stats1", 4), ("project", 0), ("stats1", 5), ("denominators", 5), ("decayed", 3),
    ("scatter", 1), ("mixed", 2), ("invert", 3), ("mixed_high", 2), ("sums", 6), ("scatter", 2), ("residual", 0),
    ("project", 1), ("weigh", 3), ("embed", 6), ("mean1", 4), ("mean1", 5), ("stats2", 0), ("scatter", 3),
    ("variance1", 1), ("denominators", 6), ("invert", 4), ("scatter", 4), ("decayed", 4), ("invert", 5),
    ("embedded", 6), ("weighed_high", 3), ("root1", 1), ("embed", 7), ("invert", 6), ("low_sum", 3), ("scatter", 5),
    ("norm1", 3), ("norm1", 4), ("norm1", 5), ("mean2", 0), ("transpose", 3), ("weigh", 4), ("scatter", 6),
    ("project", 2), ("transposed", 3), ("stats1", 6), ("transpose", 4), ("residual", 1), ("sums", 7),
    ("transposed", 4), ("residual", 2), ("embedded", 7), ("stats2", 1), ("scatter", 7), ("stats2", 2),
    ("transpose", 5), ("mean2", 1), ("decayed", 5), ("mean2", 2), ("transposed", 5), ("denominators", 7),
    ("weighed_high", 4), ("difference", 1), ("embed", 8), ("variance2", 0), ("weigh", 5), ("root2", 0), ("invert", 7),
    ("weighed_high", 5), ("scatter", 8), ("norm2", 0), ("mixed", 3), ("low_sum", 4), ("project", 3), ("embedded", 8),
    ("decayed", 6), ("stats1", 7), ("low_sum", 5), ("stats1", 8), ("norm2", 1), ("low_half", 1), ("norm2", 2),
    ("residual", 3), ("mean1", 6), ("stats2", 3), ("norm2_high", 0), ("project", 4), ("weigh", 6), ("mixed_high", 3),
    ("project", 5), ("mean2", 3), ("mean1", 7), ("norm2_low", 0), ("mean1", 8), ("weighed_high", 6), ("residual", 4),
    ("decayed", 7), ("residual", 5), ("norm2_high", 1), ("low_sum", 6), ("stats2", 4), ("norm2_high", 2),
    ("stats2", 5), ("mean2", 4), ("mean2", 5), ("low_keys", 1), ("variance1", 2), ("weigh", 7), ("root1", 2),
    ("mixed", 4), ("weighed_high", 7), ("low_sum", 7), ("variance2", 1), ("norm1", 6), ("mixed", 5), ("root2", 1),
    ("project", 6), ("norm2_low", 1), ("transpose", 6), ("norm2", 3), ("project", 7), ("norm1", 7), ("transposed", 6),
    ("norm2_low", 2), ("residual", 6), ("norm2_high", 3), ("transpose", 7), ("norm1", 8), ("project", 8),
    ("transposed", 7), ("norm2", 4), ("norm2_low", 3), ("norm2", 5), ("transpose", 8), ("norm2_high", 4),
    ("residual", 7), ("norm2_high", 5), ("norm2_low", 4), ("residual", 8), ("mixed_high", 4), ("stats2", 6),
    ("stats2", 7), ("norm2_low", 5), ("mixed_high", 5), ("mean2", 6), ("stats2", 8), ("mean2", 7), ("mean2", 8),
    ("variance2", 2), ("root2", 2), ("norm2", 6), ("norm2", 7), ("norm2_high", 6), ("norm2", 8), ("norm2_high", 7),
    ("norm2_low", 6), ("norm2_high", 8), ("transposed", 8), ("norm2_low", 7), ("low_half", 2), ("norm2_low", 8),
    ("low_half", 3),
]
LEAD = {
    "embed": NEXT, "embedded": NEXT, "stats1": NEXT, "mean1": NEXT, "variance1": NEXT, "root1": NEXT,
    "norm1": NEXT, "transpose": NEXT, "transposed": NEXT, "difference": NEXT, "mixed": NEXT,
    "mixed_high": NEXT, "low_half": NEXT, "low_keys": NEXT,
    "difference2": THIS, "mixed2": THIS, "mixed_high2": THIS, "low_half2": THIS, "low_keys2": THIS,
    "values": THIS, "clip_keys": THIS, "exp_keys": THIS, "times_values": THIS, "receptance": THIS,
    "clip_receptance": THIS, "exp_receptance": THIS, "one_plus": THIS, "sums": THIS, "decayed": THIS,
    "denominators": THIS, "invert": THIS, "weigh": THIS, "weighed_high": THIS, "low_sum": THIS,
    "project": THIS, "residual": THIS, "stats2": THIS, "mean2": THIS, "variance2": THIS, "root2": THIS,
    "norm2": THIS, "norm2_high": THIS, "norm2_low": THIS,
    "route_transpose": LAST, "route_transposed": LAST, "router": LAST, "router_relu": LAST, "logits": LAST,
    "add_logit_bias": LAST, "top2": LAST, "exp_logits": LAST, "second": LAST, "exp_second": LAST,
    "gates": LAST, "rank": LAST, "positions": LAST, "scatter": LAST,
}


class Signal:

    def __init__(self, sem, per, unit=1):
        self.sem, self.per, self.unit = sem, per, unit

    def after(self, pair, n=None):
        return (pair * self.per + (self.per if n is None else n + 1)) * self.unit


def wait(eng, signal, pair, n=None):
    v = signal.after(pair, n)
    if not isinstance(v, int) or v > 0:
        eng.wait_ge(signal.sem, v)


def tile_before(pair, t, n):
    return (pair, t - n) if t >= n else (pair - 1, t - n + TILES)


def group_before(pair, g):
    return (pair, g - 1) if g else (pair - 1, 2)


def hold(eng, spacer, signal, pair, n=None):
    wait(eng, signal, pair, n)
    eng.sem_inc(spacer, 1)


def iterations(eng, body, pairs, last=1):
    body(-1)
    body(0)
    with eng.Fori(1, pairs - last) as p:
        body(p)
    for p in range(pairs - last, pairs + 1):
        body(p)


def steps(p, pairs):
    for name, n in STEPS:
        q = p + LEAD[name]
        if not isinstance(p, int) or 0 <= q < pairs:
            yield name, n, q


def build(nc, x, tok_w, tok_b, decay, mix, wk, wv, wr, wo, rw1, rb1, rw2, rb2, ew1, eb1, ew2, eb2, ew3, eb3,
          out):
    images = x.shape[0]
    pairs = images // 2
    tokens = images * IMG
    region = tokens + BT
    btiles = (2 * tokens + E * (BT - 1)) // BT
    btiles += btiles % 2
    dummy = E * region
    assert pairs >= 4 and region * (E + 1) < 1 << 24

    ctx = ExitStack()
    with ctx:
        def sb(name, shape, dt=F32):
            return ctx.enter_context(nc.sbuf_tensor(name, shape, dt))

        def sem(name):
            return ctx.enter_context(nc.semaphore(name))

        def sig(name, per, unit=1):
            return Signal(sem(name), per, unit)

        lists = nc.dram_tensor("expert_lists", [dummy + BT, ROW], F32, kind="Internal").ap()
        packs = nc.dram_tensor("expert_packages", [E, P, EW], F32, kind="Internal").ap()
        skew = nc.dram_tensor("skewed_decay", [P * 800], F32, kind="Internal").ap()

        arena = sb("arena", [P, 2 * IMG * PATCH])
        embed_w = sb("embed_w", [KP + 1, QS, D])
        h = sb("h", [P, 2, TILES, D])
        y1 = sb("y1", [P, 3, D])
        y1t = sb("y1t", [P, 2, 386])
        diff = sb("diff", [P, 2, GROUP])
        xf = sb("xf", [P, 2, 2, GROUP])
        xh = sb("xh", [P, 3, 2, 2 * GROUP], F16)
        xl = sb("xl", [P, 3, 2, 2 * GROUP], F16)
        k = sb("k", [P, TILES, D])
        kv = sb("kv", [P, TILES, D])
        gate = sb("gate", [P, 2, PAIR])
        rwh = sb("rwh", [P, 2, PAIR], F16)
        rwl = sb("rwl", [P, 2, PAIR], F16)
        h2 = sb("h2", [P, 3, D])
        y2 = sb("y2", [P, 3, D])
        row = sb("row", [P, TILES, ROW])
        y2t = sb("y2t", [P, 4, GROUP], F16)
        rh = sb("rh", [P, GROUP])
        wh = sb("wh", [P, 4, 2, D], F16)
        wl = sb("wl", [P, 4, 2, D], F16)
        rwa = sb("rwa", [P, 2, 2, P], F16)
        rw2s = sb("rw2s", [P, E])
        rb1s = sb("rb1s", [P, 1])
        rb2s = sb("rb2s", [P, E])
        mixs = sb("mixs", [P, 3, 2])
        dec = sb("dec", [P, 640])
        upto = sb("upto", [P, P])
        carry_w = sb("carry_w", [P, 5])
        before = sb("before", [P, P], F16)
        ones16 = sb("ones16", [P, P], F16)
        id16 = sb("id16", [P, P], F16)
        id32 = sb("id32", [P, P])
        half3 = sb("half3", [P, 3])
        zero2 = sb("zero2", [P, 2])
        st = sb("st", [P, 3, 6])
        mv1 = sb("mv1", [P, 3, 2])
        ve1 = sb("ve1", [P, 3])
        rs1 = sb("rs1", [P, 3])
        st2 = sb("st2", [P, 3, 6])
        mv2 = sb("mv2", [P, 3, 2])
        ve2 = sb("ve2", [P, 3])
        rs2 = sb("rs2", [P, 3])
        lg = sb("lg", [P, TILES, E])
        t1 = sb("t1", [P, TILES, E])
        oh1 = sb("oh1", [P, TILES, E])
        oh2 = sb("oh2", [P, TILES, E])
        t2 = sb("t2", [P, TILES, E])
        ex = sb("ex", [P, TILES, E])
        sel16 = sb("sel16", [P, TILES + 1, E], F16)
        base = sb("base", [P, E])
        rev = sb("rev", [P, TILES, E])
        m1 = sb("m1", [P, TILES, 1])
        m2 = sb("m2", [P, TILES, 1])
        g1 = sb("g1", [P, TILES, 1])
        g2 = sb("g2", [P, TILES, 1])
        posf = sb("posf", [P, 2, TILES])
        posu = sb("posu", [P, 2, TILES], U32)
        idf = sb("idf", [P, TILES])
        idi = sb("idi", [P, TILES], I32)
        mx = sb("mx", [P, 20])
        mxa = sb("mxa", [P, 20])
        omm = sb("omm", [P, 3, 2])
        bd = sb("bd", [P, 16])
        sc = sb("sc", [P, 16])
        isc = sb("isc", [P, 16])
        un = sb("un", [P, 16])
        cnt = sb("cnt", [P, E])
        nti = sb("nti", [P, E], I32)
        ntf = sb("ntf", [P, E])
        cum = sb("cum", [P, E + 1])
        tk = sb("tk", [1, btiles])
        tki = sb("tki", [1, btiles], I32)
        tge = sb("tge", [1, btiles])
        toff = sb("toff", [1, btiles])
        texp = sb("texp", [1, btiles])
        table = sb("table", [1, 2, btiles], I32)
        rbase = sb("rbase", [P, E])
        tails = sb("tails", [1, E], I32)
        fill_id = sb("fill_id", [P, 4], I32)

        def bank(name):
            return ctx.enter_context(nc.psum_tensor(name, [P, 512], F32))

        b_tok = [bank("b_tok0"), bank("b_tok1")]
        b_tr = bank("b_tr")
        b_rt = bank("b_rt")
        b_proj = [bank("b_proj0"), bank("b_proj1")]
        b_w = bank("b_w")
        b_s = bank("b_s")

        x_in = [sig("x_in0", 1, 96), sig("x_in1", 1, 96)]
        tok_done = sig("tok_done", TILES)
        h_ready = sig("h_ready", TILES)
        st1_ready = sig("st1_ready", TILES)
        mv1_ready = sig("mv1_ready", TILES)
        ve1_ready = sig("ve1_ready", 3)
        rs1_ready = sig("rs1_ready", 3)
        y1_ready = sig("y1_ready", TILES)
        tr_done = sig("tr_done", TILES)
        y1t_ready = sig("y1t_ready", TILES)
        diff_ready = sig("diff_ready", 3)
        xf_ready = sig("xf_ready", 9)
        xh_ready = sig("xh_ready", 9)
        xl_ready = sig("xl_ready", 3)
        xl_pool = sig("xl_pool", 6)
        kv_done = sig("kv_done", TILES)
        kc_ready = sig("kc_ready", TILES)
        k_ready = sig("k_ready", TILES)
        kv_ready = sig("kv_ready", TILES)
        r_done = sig("r_done", 6)
        rc_ready = sig("rc_ready", 6)
        e_ready = sig("e_ready", 6)
        gate_ready = sig("gate_ready", 6)
        sum_done = sig("sum_done", 8)
        wkv_done = sig("wkv_done", 8)
        den_ready = sig("den_ready", 8)
        inv_ready = sig("inv_ready", 8)
        rw_ready = sig("rw_ready", 8)
        rwh_ready = sig("rwh_ready", 8)
        rwl_ready = sig("rwl_ready", 8)
        wo_done = sig("wo_done", TILES)
        h2_ready = sig("h2_ready", TILES)
        h2_out = [sig(f"h2_out{i}", 3, 16) for i in range(3)]
        st2_ready = sig("st2_ready", TILES)
        mv2_ready = sig("mv2_ready", TILES)
        ve2_ready = sig("ve2_ready", 3)
        rs2_ready = sig("rs2_ready", 3)
        y2_ready = sig("y2_ready", TILES)
        yh_ready = sig("yh_ready", TILES)
        yl_ready = sig("yl_ready", TILES)
        rtt_done = sig("rtt_done", TILES)
        y2t_ready = sig("y2t_ready", TILES)
        rh_done = sig("rh_done", 3)
        rh_ready = sig("rh_ready", 3)
        lg_done = sig("lg_done", 3)
        lg_ready = sig("lg_ready", 3)
        TOP_LINKS = 20
        top_link = sig("top_link", TOP_LINKS)
        d_ready = sig("d_ready", 1)
        ex_ready = sig("ex_ready", 1)
        q_in = sig("q_in", 1)
        q_ready = sig("q_ready", 1)
        sel_ready = sig("sel_ready", 1)
        gw_ready = sig("gw_ready", 1)
        rank_done = sig("rank_done", 1)
        RANK_LINKS = 6
        rank_link = sig("rank_link", RANK_LINKS)
        pos_ready = sig("pos_ready", 1)
        scat = sig("rows_out", 2 * TILES, 16)

        dve_hold = sem("vector_hold")
        pool_hold = sem("pool_hold")
        ld = sem("weights_in")
        ld_e = sem("experts_in")
        setup_v = sem("setup_vector")
        setup_link = sem("setup_link")
        setup_p = sem("setup_pool")
        setup_a = sem("setup_scalar")
        amax_ready = sem("amax_ready")
        scales_ready = sem("scales_ready")
        skew_out = sem("skew_out")
        dec_in = sem("dec_in")
        pk_ready = sem("package_ready")
        pkh_ready = sem("package_high_ready")
        pk_out = [sem("package_out0"), sem("package_out1")]
        ones_ready = sem("ones_ready")
        dump_out = sem("dump_rows_out")
        wsplit = sem("weights_high_ready")
        split_ready = sem("weights_split")

        W_S = {"k": 0, "v": 1, "r": 2, "o": 3, "r1": 4, "e1": 5, "e2": 6, "e3": 7}
        S_MIX, S_RW, S_H1, S_H2 = 8, 9, 10, 11
        NS = 12

        def col(t, i):
            return t[:, i:i + 1]

        raw_w = gate[:, :, :].rearrange("p a b -> p (a b)")[:, 0:2048].rearrange("p (m c n) -> p m c n", m=4, c=2)
        raw_r1 = k[:, 0, :].rearrange("p (c n) -> p c n", c=2)
        raw_e = arena[:, IMG * PATCH:].rearrange("p (e m c n) -> p e m c n", e=E, m=3, c=2)
        raw_b = k[:, 1, 0:24]
        raw_b3 = kv[:, 0:E, :]
        filler = xh[:].rearrange("p a b c -> p (a b c)").bitcast(F32)[:, 0:4 * ROW].rearrange("p (j w) -> p j w", j=4)
        zrow = h[:, 0, 4:8, :].rearrange("p a b -> p (a b)")[:, 0:768]
        pack = [h[:, 1, :, :].rearrange("p a b -> p (a b)")[:, 0:EW],
                h[:, 0, :, :].rearrange("p a b -> p (a b)")[:, 0:EW]]
        packm = [t[:, 0:1536].bitcast(F16).rearrange("p (m l c n) -> p m l c n", m=3, l=2, c=2) for t in pack]

        place = [0]

        def carve(words):
            place[0] += words
            assert place[0] <= 2 * IMG * PATCH
            return arena[:, place[0] - words:place[0]]

        def halves(t):
            return t.bitcast(F16).rearrange("p (l c s) -> p l c s", l=2, c=2)

        k_flat, kv_flat = k[:].rearrange("p a b -> p (a b)"), kv[:].rearrange("p a b -> p (a b)")

        packs_b = carve(E * EW).rearrange("p (e w) -> p e w", e=E)
        mats_b = arena[:, 0:E * EW].bitcast(F16).rearrange("p (e w) -> p e w", e=E)
        rows_b = [carve(4 * ROW).rearrange("p (j w) -> p j w", j=4) for _ in range(2)]
        bias_b = [carve(EW - EW_B) for _ in range(2)]
        yt_b = halves(carve(2 * BT))
        hid = [carve(2 * BT).rearrange("p (f s) -> p f s", f=2) for _ in range(2)]
        hid_b = [halves(k_flat[:, i * 2 * BT:(i + 1) * 2 * BT]) for i in range(2)]
        o_b = carve(4 * D).rearrange("p (j w) -> p j w", j=4)
        og_b = [kv_flat[:, i * 4 * D:(i + 1) * 4 * D].rearrange("p (j w) -> p j w", j=4) for i in range(2)]
        num_b = [carve(4) for _ in range(2)]
        gs_b = [carve(4) for _ in range(2)]
        bt_bank = b_tok
        hid_bank = [[b_tr, b_rt], [b_w, b_s]]
        o_bank = b_proj

        half_tiles = btiles // 2
        rows_in = [sig(f"rows_in{j}", 1, 16) for j in range(2)]
        packs_in = sem("packages_in")
        bias_ready = [sig(f"bias_ready{j}", 1) for j in range(2)]
        num_ready = [sig(f"num_ready{j}", 1) for j in range(2)]
        bt_done = [sig(f"bt_done{j}", 1) for j in range(2)]
        yth_ready = [sig(f"yth_ready{j}", 1) for j in range(2)]
        ytl_ready = [sig(f"ytl_ready{j}", 1) for j in range(2)]
        hid_done = [[sig(f"hid{m}_done{j}", 2) for j in range(2)] for m in range(2)]
        hid_ready = [[sig(f"hid{m}_ready{j}", 2) for j in range(2)] for m in range(2)]
        hidh_ready = [[sig(f"hid{m}h_ready{j}", 2) for j in range(2)] for m in range(2)]
        hidl_ready = [[sig(f"hid{m}l_ready{j}", 2) for j in range(2)] for m in range(2)]
        o_done = [sig(f"o_done{j}", 2) for j in range(2)]
        o_ready = [sig(f"o_ready{j}", 2) for j in range(2)]
        gs_ready = [sig(f"gs_ready{j}", 1) for j in range(2)]
        og_ready = [sig(f"og_ready{j}", 4) for j in range(2)]
        adds_out = [sig(f"adds_out{j}", 4, 16) for j in range(2)]
        table_ready = sem("table_ready")
        tails_out = sem("tails_out")
        table_link = sem("table_link")

        def tile_loop(eng, body):
            body(0)
            with eng.Fori(1, half_tiles - 1) as i:
                body(i)
            body(half_tiles - 1)

        def before_tile(i, j):
            return (i, 0) if j else (i - 1, 1)

        def exists(i):
            return not isinstance(i, int) or 0 <= i < half_tiles

        def entry(eng, what, i, j):
            n = 2 * i + j
            return eng.value_load(table[0:1, what, n:n + 1] if isinstance(i, int) else
                                  table[0:1, what, bass.ds(n, 1)], min_val=0, max_val=E - 1 if what else dummy)

        def stage_b_sync(sp):
            sp.wait_ge(table_ready, 2)
            sp.wait_ge(dump_out, 32)
            for e in range(E):
                at = sp.value_load(tails[0:1, e:e + 1], min_val=0, max_val=dummy)
                sp.dma_start(lists[bass.ds(at, BT)], lists[dummy:dummy + BT]).then_inc(tails_out, 16)
            sp.wait_ge(tails_out, 16 * E)
            wait(sp, scat, pairs - 1)

            def body(i):
                for j in range(2):
                    at = entry(sp, 0, i, j)
                    wait(sp, bt_done[j], i - 1)
                    wait(sp, num_ready[j], i - 1)
                    sp.dma_start(rows_b[j], lists[bass.ds(at, BT)].rearrange("(j p) w -> p j w", p=P)).then_inc(
                        rows_in[j].sem, 16)

            tile_loop(sp, body)
            for j in range(2):
                wait(sp, adds_out[j], half_tiles - 1)

        def stage_b_tensor(pe):
            mm = nc.tensor.matmul

            def transposes(i, j):
                wait(pe, rows_in[j], i)
                a, b = before_tile(i, j)
                wait(pe, yth_ready[b], a)
                wait(pe, ytl_ready[b], a)
                for l in range(2):
                    dst = bt_bank[l][:].bitcast(F16)
                    for c in range(2):
                        for t in range(4):
                            src = rows_b[j][:, t, l * P:(l + 1) * P].bitcast(F16)[:, c * P:(c + 1) * P]
                            last = nc.tensor.transpose(dst[:, c * BT + t * P:c * BT + (t + 1) * P], src, id16[:])
                last.then_inc(bt_done[j].sem, 1)

            def matrix(e, m, lw, c, first, n):
                first += ((m * 2 + lw) * 2 + c) * D
                return mats_b[:, bass.ds(e, 1), first:first + n].rearrange("p o n -> p (o n)")

            def hidden(m, i, j, e):
                a, b = before_tile(i, j)
                if m == 0:
                    wait(pe, yth_ready[j], i)
                    wait(pe, ytl_ready[j], i)
                    src = yt_b
                else:
                    wait(pe, hidh_ready[0][j], i)
                    wait(pe, hidl_ready[0][j], i)
                    src = hid_b[0]
                for f in range(2):
                    wait(pe, hid_ready[m][b], a, f)
                    parts = [(matrix(e, m, lw, c, f * P, P), src[:, lx, c, :]) for c in range(2)
                             for lx, lw in ((0, 0), (0, 1), (1, 0))]
                    for n, (l, r) in enumerate(parts):
                        last = mm(hid_bank[m][f][:], l, r, start=(n == 0), stop=(n == 5))
                    last.then_inc(hid_done[m][j].sem, 1)

            def output(i, j, e):
                a, b = before_tile(i, j)
                wait(pe, hidh_ready[1][j], i)
                wait(pe, hidl_ready[1][j], i)
                for u in range(2):
                    wait(pe, o_ready[b], a, u)
                    for t in (2 * u, 2 * u + 1):
                        parts = [(hid_b[1][:, lx, c, t * P:(t + 1) * P], matrix(e, 2, lw, c, 0, D)) for c in range(2)
                                 for lx, lw in ((0, 0), (0, 1), (1, 0))]
                        dst = o_bank[u][:, (t % 2) * D:(t % 2 + 1) * D]
                        for n, (l, r) in enumerate(parts):
                            last = mm(dst, l, r, start=(n == 0), stop=(n == 5))
                    last.then_inc(o_done[j].sem, 1)

            def body(i):
                expert = [entry(pe, 1, i, 0), entry(pe, 1, i, 1)]
                last = entry(pe, 1, i - 1, 1) if exists(i - 1) else None
                for j in range(2):
                    a, b = before_tile(i, j)
                    hidden(0, i, j, expert[j])
                    if exists(a):
                        output(a, b, expert[0] if j else last)
                    if j == 0:
                        transposes(i, 1)
                    elif not isinstance(i, int) or i + 1 < half_tiles:
                        transposes(i + 1, 0)
                    hidden(1, i, j, expert[j])

            wait(pe, pos_ready, pairs - 1)
            wait(pe, rw_ready, pairs - 1)
            wait(pe, h2_ready, pairs - 1)
            pe.wait_ge(table_ready, 2)
            pe.wait_ge(packs_in, 16 * E)
            transposes(0, 0)
            tile_loop(pe, body)
            output(half_tiles - 1, 1, entry(pe, 1, half_tiles - 1, 1))

        def stage_b_scalar(act):
            f_ = nc.scalar.activation

            def copy_high(i, j):
                wait(act, bt_done[j], i)
                a, b = before_tile(i, j)
                wait(act, hid_done[0][b], a)
                f_(yt_b[:, 0], bt_bank[0][:].bitcast(F16).rearrange("p (c s) -> p c s", c=2),
                   ACT.Copy).then_inc(yth_ready[j].sem, 1)

            def relu(m, i, j):
                a, b = before_tile(i, j)
                wait(act, bias_ready[j], i)
                for f in range(2):
                    wait(act, hid_done[m][j], i, f)
                    wait(act, hidl_ready[m][b], a, f)
                    f_(hid[m][:, f, :], hid_bank[m][f][:], ACT.Relu, scale=col(un, 5 + m),
                       bias=bias_b[j][:, 2 * m + f:2 * m + f + 1]).then_inc(hid_ready[m][j].sem, 1)

            def weighted(i, j):
                wait(act, gs_ready[j], i)
                wait(act, adds_out[j], i - 1)
                for t in range(4):
                    wait(act, o_ready[j], i, t // 2)
                    f_(og_b[j][:, t, :], o_b[:, t, :], ACT.Copy, scale=gs_b[j][:, t:t + 1]).then_inc(
                        og_ready[j].sem, 1)

            def body(i):
                for j in range(2):
                    a, b = before_tile(i, j)
                    relu(0, i, j)
                    if exists(a):
                        weighted(a, b)
                    if j == 0:
                        copy_high(i, 1)
                    elif not isinstance(i, int) or i + 1 < half_tiles:
                        copy_high(i + 1, 0)
                    relu(1, i, j)

            wait(act, wkv_done, pairs - 1)
            copy_high(0, 0)
            tile_loop(act, body)
            weighted(half_tiles - 1, 1)

        def stage_b_vector(dve):
            v = nc.vector
            count = [0]

            def link(ins):
                ins.then_inc(table_link, 1)
                count[0] += 1
                dve.wait_ge(table_link, count[0])

            v.tensor_copy(tails[:], base[0:1, :])
            link(v.tensor_tensor(cnt[:], base[:], rbase[:], ALU.subtract))
            link(v.tensor_scalar(cnt[:], cnt[:], float(BT - 1), None, ALU.add))
            link(v.tensor_copy(nti[:], cnt[:]))
            link(v.tensor_scalar(nti[:], nti[:], BT.bit_length() - 1, None, ALU.arith_shift_right))
            link(v.tensor_copy(ntf[:], nti[:]))
            link(v.memset(cum[:, 0:1], 0.0))
            for e in range(E):
                link(v.tensor_tensor(cum[:, e + 1:e + 2], cum[:, e:e + 1], ntf[:, e:e + 1], ALU.add))
            link(v.tensor_scalar(cnt[:], ntf[:], -float(BT), float(region), ALU.mult, ALU.add))
            v.memset(texp[:], 0.0)
            link(v.tensor_scalar(toff[:], tk[:], float(BT), None, ALU.mult))
            for e in range(E - 1):
                link(v.tensor_scalar(tge[:], tk[:], cum[0:1, e + 1:e + 2], None, ALU.is_ge))
                v.tensor_tensor(texp[:], texp[:], tge[:], ALU.add)
                link(v.scalar_tensor_tensor(toff[:], tge[:], cnt[0:1, e:e + 1], toff[:], ALU.mult, ALU.add))
            link(v.tensor_scalar(tge[:], tk[:], cum[0:1, E:E + 1], None, ALU.is_ge))
            link(v.tensor_scalar(tk[:], toff[:], -1.0, float(dummy), ALU.mult, ALU.add))
            link(v.tensor_tensor(tk[:], tk[:], tge[:], ALU.mult))
            link(v.tensor_tensor(toff[:], toff[:], tk[:], ALU.add))
            v.tensor_copy(table[:, 1, :], texp[:]).then_inc(table_ready, 1)
            v.tensor_copy(table[:, 0, :], toff[:]).then_inc(table_ready, 1)

            def copy_low(i, j):
                wait(dve, bt_done[j], i)
                a, b = before_tile(i, j)
                wait(dve, hid_done[0][b], a)
                v.tensor_copy(yt_b[:, 1], bt_bank[1][:].bitcast(F16).rearrange("p (c s) -> p c s", c=2)).then_inc(
                    ytl_ready[j].sem, 1)

            def biases(i, j, e):
                wait(dve, hid_ready[1][j], i - 1)
                wait(dve, o_ready[j], i - 1)
                v.tensor_copy(bias_b[j], packs_b[:, bass.ds(e, 1), EW_B:EW].rearrange("p o w -> p (o w)")).then_inc(
                    bias_ready[j].sem, 1)

            def gates(i, j, e):
                wait(dve, rows_in[j], i)
                wait(dve, adds_out[j], i - 1)
                v.tensor_copy(gs_b[j], rows_b[j][:, :, bass.ds(e + D, 1)].rearrange("p j o -> p (j o)")).then_inc(
                    gs_ready[j].sem, 1)
                v.tensor_copy(num_b[j].bitcast(U32), rows_b[j][:, :, D + E].bitcast(U32)).then_inc(
                    num_ready[j].sem, 1)

            def split(m, i, j):
                a, b = before_tile(i, j)
                for f in range(2):
                    wait(dve, hid_ready[m][j], i, f)
                    if m == 0:
                        wait(dve, hid_done[1][b], a)
                    else:
                        wait(dve, o_done[b], a)
                    v.tensor_copy(hid_b[m][:, 0, f, :], hid[m][:, f, :]).then_inc(hidh_ready[m][j].sem, 1)
                    wait(dve, hidh_ready[m][j], i, f)
                    v.tensor_tensor(hid_b[m][:, 1, f, :], hid[m][:, f, :], hid_b[m][:, 0, f, :],
                                    ALU.subtract).then_inc(hidl_ready[m][j].sem, 1)

            def out_bias(i, j):
                a, b = before_tile(i, j)
                for u in range(2):
                    wait(dve, o_done[j], i, u)
                    wait(dve, og_ready[b], a, 2 * u + 1)
                    b3 = bias_b[j][:, EW_B3 - EW_B:].unsqueeze(1).to_broadcast([P, 2, D])
                    v.scalar_tensor_tensor(o_b[:, 2 * u:2 * u + 2, :],
                                           o_bank[u][:].rearrange("p (t w) -> p t w", t=2), col(un, 7), b3,
                                           ALU.mult, ALU.add).then_inc(o_ready[j].sem, 1)

            def body(i):
                more = not isinstance(i, int) or i + 1 < half_tiles
                expert = [entry(dve, 1, i, 0), entry(dve, 1, i, 1)]
                following = entry(dve, 1, i + 1, 0) if more else None
                for j in range(2):
                    a, b = before_tile(i, j)
                    split(0, i, j)
                    if exists(a):
                        out_bias(a, b)
                    gates(i, j, expert[j])
                    if j == 0:
                        biases(i, 1, expert[1])
                        copy_low(i, 1)
                    elif more:
                        biases(i + 1, 0, following)
                        copy_low(i + 1, 0)
                    split(1, i, j)

            wait(dve, sum_done, pairs - 1)
            dve.wait_ge(table_ready, 2)
            dve.sem_inc(dve_hold, 1)
            first = entry(dve, 1, 0, 0)
            dve.wait_ge(packs_in, 16 * E)
            biases(0, 0, first)
            copy_low(0, 0)
            tile_loop(dve, body)
            out_bias(half_tiles - 1, 1)

        def stage_b_pool(pool):
            for s in h2_out:
                wait(pool, s, pairs - 1)
            pool.wait_ge(dump_out, 32)

            def body(i):
                for j in range(2):
                    a, b = before_tile(i, j)
                    wait(pool, num_ready[j], i)
                    wait(pool, adds_out[b], a)
                    for t in range(4):
                        hold(pool, pool_hold, og_ready[j], i, t)
                        nc.gpsimd.indirect_dma_start(
                            out, bass.IndirectOffsetOnAxis(ap=num_b[j][:, t:t + 1].bitcast(U32), axis=0),
                            og_b[j][:, t, :], None, compute_op=ALU.add).then_inc(adds_out[j].sem, 16)

            tile_loop(pool, body)

        block = ctx.enter_context(nc.Block())

        def group_slot(g):
            return slice(g % 2 * GROUP, (g % 2 + 1) * GROUP)

        def rows_of(image):
            if image == 0:
                return [(t, 0, P, P * t) for t in range(4)] + [(4, 0, 64, 512)]
            return [(4, 64, 64, 0)] + [(5 + t, 0, P, 64 + P * t) for t in range(4)]

        def block_of(n):
            return n // 4, (n // 2) % 2, n % 2

        def pieces(n):
            image, half, _ = block_of(n)
            a, b = half * HALF, (half + 1) * HALF
            got = []
            for i, (_, _, size, t0) in enumerate(rows_of(image)):
                lo, hi = max(a, t0), min(b, t0 + size)
                if lo < hi:
                    got.append((i, lo - a, hi - a))
            return got

        def block_cols(n):
            image, half, _ = block_of(n)
            return slice(image * IMG + half * HALF, image * IMG + (half + 1) * HALF)

        @block.sync
        def _(sp):
            def load_image(q, half):
                img = x[2 * q + half] if isinstance(q, int) else x[bass.ds(2 * q + half, 1)].rearrange(
                    "o c h w -> (o c) h w")
                v = img.rearrange("c (n r) w -> c r n w", r=PATCH)
                for g in range(2):
                    for c in range(CH):
                        part = (g * CH + c) * PATCH
                        dst = arena[part:part + PATCH, half * IMG * PATCH:(half + 1) * IMG * PATCH]
                        dst = dst.rearrange("p (n w) -> p n w", n=SIDE)[:, :, 0:SIDE * PATCH - QS * g]
                        sp.dma_start(dst, v[c][:, :, QS * g:]).then_inc(x_in[half].sem, 16)

            load_image(0, 0)
            sp.dma_start(embed_w[0:KP], tok_w).then_inc(ld, 16)
            sp.dma_start(embed_w[KP:KP + 1, 0, :], tok_b).then_inc(ld, 16)
            for i, w in enumerate((wk, wv, wr, wo)):
                sp.dma_start(raw_w[:, i], w.rearrange("(c p) n -> p c n", c=2)).then_inc(ld, 16)
            sp.dma_start(raw_r1, rw1.rearrange("(c p) n -> p c n", c=2)).then_inc(ld, 16)
            sp.dma_start(rw2s[:], rw2).then_inc(ld, 16)
            sp.dma_start(rb1s[:], rb1).then_inc(ld, 16)
            sp.dma_start(rb2s[:], rb2).then_inc(ld, 16)
            sp.dma_start(mixs[:], mix).then_inc(ld, 16)
            sp.dma_start(zrow[:, 128:768], decay).then_inc(ld, 16)
            sp.dma_start(raw_b[:, 0:12], eb1).then_inc(ld_e, 16)
            sp.dma_start(raw_b[:, 12:24], eb2).then_inc(ld_e, 16)
            sp.dma_start(raw_b3, eb3).then_inc(ld_e, 16)
            for i, w in enumerate((ew1, ew2, ew3)):
                for e in range(E):
                    sp.dma_start(raw_e[:, e, i], w[e].rearrange("(c p) n -> p c n", c=2)).then_inc(ld_e, 16)
            sp.wait_ge(ld, 16 * 12)
            sp.wait_ge(setup_v, 1)
            sp.dma_start(skew.rearrange("(p s) -> p s", s=800)[:, 0:768], zrow).then_inc(skew_out, 16)
            sp.wait_ge(skew_out, 16)
            sp.dma_start(dec[:], skew[0:P * 799].rearrange("(p s) -> p s", s=799)[:, 128:768]).then_inc(dec_in, 16)
            for e in range(E):
                sp.wait_ge(pk_ready, e + 1)
                sp.wait_ge(pkh_ready, 4 * (e + 1))
                sp.dma_start(packs[e], pack[e % 2]).then_inc(pk_out[e % 2], 16)
            sp.wait_ge(setup_v, 4)
            sp.wait_ge(setup_p, 6)
            sp.dma_start(lists[dummy:dummy + BT].rearrange("(j p) w -> p j w", p=P), filler[:]).then_inc(dump_out, 16)
            sp.dma_start(out[tokens:tokens + BT].rearrange("(j p) w -> p j w", p=P),
                         filler[:, :, 0:D]).then_inc(dump_out, 16)
            load_image(0, 1)

            outv = out[0:tokens].rearrange("(q t p) w -> q t p w", t=TILES, p=P)

            def body(p):
                for name, n, q in steps(p, pairs):
                    more = not isinstance(q, int) or q + 1 < pairs
                    if name == "embed" and n == 4 and more:
                        wait(sp, tok_done, q, 4)
                        load_image(q + 1, 0)
                    if name == "embed" and n == 8 and more:
                        wait(sp, tok_done, q, 8)
                        load_image(q + 1, 1)
                    if name == "embed" and n == 8 and not more:
                        wait(sp, tok_done, q, 8)
                        sp.wait_ge(pk_out[0], 48)
                        sp.wait_ge(pk_out[1], 48)
                        for e in range(E):
                            sp.dma_start(packs_b[:, e, :], packs[e]).then_inc(packs_in, 16)
                    if name == "project":
                        wait(sp, h2_ready, q, n)
                        dst = outv[q, n] if isinstance(q, int) else outv[bass.ds(q, 1), n].rearrange(
                            "o p w -> (o p) w")
                        sp.dma_start(dst, h2[:, n % 3, :]).then_inc(h2_out[n % 3].sem, 16)

            iterations(sp, body, pairs, last=2)
            for s in h2_out:
                wait(sp, s, pairs - 1)
            stage_b_sync(sp)

        @block.tensor
        def _(pe):
            mm = nc.tensor.matmul

            def embed(q, t):
                wait(pe, x_in[0 if t < 4 else 1], q)
                if t == 4:
                    wait(pe, x_in[0], q)
                bank_ = b_tok[t % 2]
                if t >= 2:
                    wait(pe, h_ready, q, t - 2)
                else:
                    wait(pe, h_ready, q - 1, 7 if t else 8)
                for j in range(QS):
                    a = t * P * PATCH + j
                    rows = KP + (j == 0)
                    last = mm(bank_[:, 0:D], arena[0:rows, a:a + (P - 1) * PATCH + 1:PATCH], embed_w[0:rows, j, :],
                              start=(j == 0), stop=(j == QS - 1))
                last.then_inc(tok_done.sem, 1)

            def transpose(q, t):
                wait(pe, y1_ready, q, t)
                wait(pe, y1t_ready, q if t else q - 1, t - 1 if t else None)
                for c in range(2):
                    last = nc.tensor.transpose(b_tr[:, c * P:(c + 1) * P], y1[:, t % 3, c * P:(c + 1) * P], id32[:])
                last.then_inc(tr_done.sem, 1)

            def split_product(dst, parts):
                for i, (l, r) in enumerate(parts):
                    last = mm(dst, l, r, start=(i == 0), stop=(i == len(parts) - 1))
                return last

            def keys_values(q, t):
                g = t // 3
                if t % 3 == 0:
                    wait(pe, xh_ready, q, 3 * g + 1)
                    wait(pe, xl_ready, q, g)
                    wait(pe, xl_pool, q, 2 * g)
                dst = b_proj[t % 2]
                if t >= 2:
                    wait(pe, kv_ready, q, t - 2)
                else:
                    wait(pe, h2_ready, q - 1, 7 + t)
                s = slice(g % 2 * GROUP + t % 3 * P, g % 2 * GROUP + (t % 3 + 1) * P)
                for i in range(2):
                    parts = [(a[:, i, c, s], w[:, i, c, :]) for c in range(2)
                             for a, w in ((xh, wh), (xh, wl), (xl, wh))]
                    last = split_product(dst[:, i * D:(i + 1) * D], parts)
                last.then_inc(kv_done.sem, 1)

            def receptance(q, n):
                g, f = n // 2, n % 2
                if f == 0:
                    wait(pe, xh_ready, q, 3 * g + 2)
                    wait(pe, xl_pool, q, 2 * g + 1)
                dst = (b_w, b_s)[f]
                if g:
                    wait(pe, rc_ready, q, n - 2)
                else:
                    wait(pe, rw_ready if f == 0 else den_ready, q - 1)
                s = group_slot(g)
                parts = [(w[:, 2, c, f * P:(f + 1) * P], a[:, 2, c, s]) for c in range(2)
                         for a, w in ((xh, wh), (xh, wl), (xl, wh))]
                split_product(dst[:, 0:GROUP], parts).then_inc(r_done.sem, 1)

            def sums(q, n):
                image, half, f = block_of(n)
                rows = rows_of(image)
                a = half * HALF
                fs = slice(f * P, (f + 1) * P)
                mine = pieces(n)
                top = max(i for i, _, _ in mine)
                wait(pe, kv_ready, q, rows[top][0])
                if n:
                    wait(pe, den_ready, q, n - 1)
                else:
                    wait(pe, rc_ready, q, 5)
                for i, lo, hi in mine:
                    t, p0, size, t0 = rows[i]
                    s0 = a + lo - t0 + p0
                    mm(b_s[:, lo:hi], k[p0:p0 + size, t, fs], upto[p0:p0 + size, s0:s0 + hi - lo],
                       start=True, stop=True)
                firsts = [i for i, _, _ in mine]
                for i in range(top):
                    t, p0, size, _ = rows[i]
                    later = sum(1 for j in firsts if j > i)
                    last = mm(b_s[:, HALF:HALF + 3], k[p0:p0 + size, t, fs],
                              carry_w[p0:p0 + size, later - 1:later + 2],
                              start=(i == 0), stop=(i == top - 1))
                last.then_inc(sum_done.sem, 1)

            def decayed(q, n):
                image, half, f = block_of(n)
                rows = rows_of(image)
                a = half * HALF
                fs = slice(f * P, (f + 1) * P)
                top = max(i for i, _, _ in pieces(n))
                wait(pe, kv_ready, q, rows[top][0])
                if n:
                    wait(pe, rw_ready, q, n - 1)
                else:
                    wait(pe, rc_ready, q, 4)
                for i in range(top + 1):
                    t, p0, size, t0 = rows[i]
                    lo = max(t0 - a, 0)
                    s0 = a + lo - t0 + p0
                    last = mm(b_w[:, lo:HALF], kv[p0:p0 + size, t, fs], dec[p0:p0 + size, s0:s0 + HALF - lo],
                              start=(i == 0), stop=(i == top))
                last.then_inc(wkv_done.sem, 1)

            def project(q, t):
                b = (P * t + P - 1) // HALF
                wait(pe, rwh_ready, q, 2 * b + 1)
                wait(pe, rwl_ready, q, 2 * b + 1)
                dst = b_proj[(TILES + t) % 2]
                if t >= 2:
                    wait(pe, h2_ready, q, t - 2)
                else:
                    wait(pe, kv_ready, q, 7 + t)
                s = slice(t * P, (t + 1) * P)
                parts = [(r[:, c, s], w[:, 3, c, :]) for c in range(2) for r, w in ((rwh, wh), (rwh, wl), (rwl, wh))]
                split_product(dst[:, 0:D], parts).then_inc(wo_done.sem, 1)

            def route_transpose(q, t):
                wait(pe, yh_ready, q, t)
                wait(pe, yl_ready, q, t)
                if t % 3:
                    wait(pe, y2t_ready, q, t - 1)
                elif t:
                    wait(pe, lg_ready, q, t // 3 - 1)
                else:
                    wait(pe, pos_ready, q - 1)
                src = row[:, t, 0:D].bitcast(F16)
                dst = b_rt[:, 0:D].bitcast(F16)
                for i in range(4):
                    last = nc.tensor.transpose(dst[:, i * P:(i + 1) * P], src[:, i * P:(i + 1) * P], id16[:])
                last.then_inc(rtt_done.sem, 1)

            def router(q, g):
                wait(pe, y2t_ready, q, 3 * g + 2)
                parts = [(rwa[:, lw, c, :], y2t[:, 2 * lx + c, :]) for c in range(2)
                         for lx, lw in ((0, 0), (0, 1), (1, 0))]
                split_product(b_rt[:, 0:GROUP], parts).then_inc(rh_done.sem, 1)

            def logits(q, g):
                wait(pe, rh_ready, q, g)
                for j in range(3):
                    last = mm(b_rt[:, j * E:(j + 1) * E], rh[:, j * P:(j + 1) * P], rw2s[:], start=True, stop=True)
                last.then_inc(lg_done.sem, 1)

            def rank(q, _):
                wait(pe, sel_ready, q)
                wait(pe, lg_ready, q, 2)
                n = TILES * E
                mm(b_rt[:, 0:n + E], before[:], sel16[:].rearrange("p t e -> p (t e)"), start=True, stop=False)
                for t in range(TILES):
                    last = mm(b_rt[:, (t + 1) * E:n + E].rearrange("p (t e) -> p t e", e=E), ones16[:],
                              sel16[:, t:t + 1, :].to_broadcast([P, TILES - t, E]), start=False, stop=(t == TILES - 1))
                last.then_inc(rank_done.sem, 1)

            def body(p):
                for name, n, q in steps(p, pairs):
                    if name in do:
                        do[name](q, n)

            do = {"embed": embed, "transpose": transpose, "values": keys_values, "receptance": receptance,
                  "sums": sums, "decayed": decayed, "project": project, "route_transpose": route_transpose,
                  "router": router, "logits": logits, "rank": rank}
            pe.wait_ge(ld, 16 * 12)
            pe.wait_ge(setup_p, 7)
            pe.wait_ge(ones_ready, 1)
            pe.wait_ge(split_ready, 5)
            pe.wait_ge(setup_v, 4)
            pe.wait_ge(dec_in, 16)
            iterations(pe, body, pairs)
            stage_b_tensor(pe)

        @block.scalar
        def _(act):
            f = nc.scalar.activation

            def embedded(q, t):
                wait(act, tok_done, q, t)
                if t == 0:
                    wait(act, h2_ready, q - 2)
                f(h[:, q % 2, t, :], b_tok[t % 2][:, 0:D], ACT.Copy).then_inc(h_ready.sem, 1)

            def transposed(q, t):
                n = t // 3
                wait(act, tr_done, q, t)
                if t % 3 == 0:
                    wait(act, diff_ready, q if n else q - 1, n - 1 if n else None)
                    wait(act, xf_ready, q if n else q - 1, 3 * n - 1 if n else None)
                    if n == 0:
                        f(y1t[:, :, 0], zero2[:], ACT.Copy)
                    else:
                        f(y1t[:, :, 0], y1t[:, :, 384 + (n == 2)], ACT.Copy)
                        if n == 1:
                            f(y1t[:, :, 193], zero2[:], ACT.Copy)
                src = b_tr[:, 0:D].rearrange("p (c s) -> p c s", c=2)
                a = 1 + (t % 3) * P
                if t == 4:
                    f(y1t[:, :, a:a + 64], src[:, :, 0:64], ACT.Copy)
                    f(y1t[:, :, a + 65:a + 129], src[:, :, 64:128], ACT.Copy).then_inc(y1t_ready.sem, 1)
                else:
                    a += t == 5
                    f(y1t[:, :, a:a + P], src, ACT.Copy).then_inc(y1t_ready.sem, 1)

            def mixed_high(q, m):
                n, i = m // 3, m % 3
                old, pair = (0, q) if n == 2 else (2 - n, q - 1)
                wait(act, xf_ready, q, m)
                wait(act, kv_done if i < 2 else r_done, pair, 3 * old + 2 if i < 2 else 2 * old + 1)
                f(xh[:, i, :, group_slot(n)], xf[:, m % 2], ACT.Copy).then_inc(xh_ready.sem, 1)

            def exp_keys(q, t):
                wait(act, kc_ready, q, t)
                f(k[:, t, :], k[:, t, :], ACT.Exp, scale=col(un, 0)).then_inc(k_ready.sem, 1)

            def part_of_gate(n):
                return gate[:, n % 2, n // 2 * GROUP:(n // 2 + 1) * GROUP]

            def exp_receptance(q, n):
                wait(act, rc_ready, q, n)
                f(part_of_gate(n), part_of_gate(n), ACT.Exp, scale=col(un, 2)).then_inc(e_ready.sem, 1)

            def one_plus(q, n):
                wait(act, e_ready, q, n)
                f(part_of_gate(n), part_of_gate(n), ACT.Copy, bias=1.0).then_inc(gate_ready.sem, 1)

            def weighed_high(q, n):
                wait(act, rw_ready, q, n)
                if n == 0:
                    wait(act, wo_done, q - 1)
                f(rwh[:, block_of(n)[2], block_cols(n)], gate[:, block_of(n)[2], block_cols(n)],
                  ACT.Copy).then_inc(rwh_ready.sem, 1)

            def norm2_high(q, t):
                wait(act, y2_ready, q, t)
                if t == 0:
                    wait(act, scat, q - 1)
                f(row[:, t, 0:P].bitcast(F16), y2[:, t % 3, :], ACT.Copy).then_inc(yh_ready.sem, 1)

            def route_transposed(q, n):
                wait(act, rtt_done, q, n)
                if n % 3 == 0:
                    wait(act, rh_done, q if n else q - 1, n // 3 - 1 if n else None)
                src = b_rt[:, 0:D].bitcast(F16).rearrange("p (i s) -> p i s", i=4)
                f(y2t[:, :, (n % 3) * P:(n % 3 + 1) * P], src, ACT.Copy).then_inc(y2t_ready.sem, 1)

            def router_relu(q, n):
                wait(act, rh_done, q, n)
                wait(act, lg_done, q if n else q - 1, n - 1 if n else None)
                f(rh[:], b_rt[:, 0:GROUP], ACT.Relu, bias=rb1s[:], scale=col(un, 4)).then_inc(rh_ready.sem, 1)

            def exp_logits(q, _):
                wait(act, d_ready, q)
                f(ex[:], t1[:], ACT.Exp).then_inc(ex_ready.sem, 1)

            def exp_second(q, _):
                wait(act, q_in, q)
                f(g2[:], g1[:], ACT.Exp).then_inc(q_ready.sem, 1)

            do = {"embedded": embedded, "transposed": transposed, "mixed_high": mixed_high,
                  "mixed_high2": mixed_high, "exp_keys": exp_keys, "exp_receptance": exp_receptance,
                  "one_plus": one_plus, "weighed_high": weighed_high, "norm2_high": norm2_high,
                  "route_transposed": route_transposed, "router_relu": router_relu, "exp_logits": exp_logits,
                  "exp_second": exp_second}

            def body(p):
                for name, n, q in steps(p, pairs):
                    if name in do:
                        do[name](q, n)

            act.wait_ge(scales_ready, 1)
            for i, s in enumerate(("k", "v", "r", "o")):
                f(wh[:, i], raw_w[:, i], ACT.Copy, scale=col(sc, W_S[s])).then_inc(wsplit, 1)
            f(rwa[:, 0], raw_r1, ACT.Copy, scale=col(sc, 4)).then_inc(wsplit, 1)
            act.wait_ge(skew_out, 16)
            for e in range(E):
                if e >= 2:
                    act.wait_ge(pk_out[e % 2], 16 * (e // 2))
                for i in range(3):
                    f(packm[e % 2][:, i, 0], raw_e[:, e, i], ACT.Copy, scale=col(sc, 5 + i)).then_inc(pkh_ready, 1)
                f(pack[e % 2][:, EW_B:EW_B + 2], raw_b[:, 2 * e:2 * e + 2], ACT.Copy, scale=col(sc, S_H1))
                f(pack[e % 2][:, EW_B + 2:EW_B + 4], raw_b[:, 12 + 2 * e:14 + 2 * e], ACT.Copy, scale=col(sc, S_H2))
                f(pack[e % 2][:, EW_B3:EW_B3 + D], raw_b3[:, e, :], ACT.Copy).then_inc(pkh_ready, 1)
            act.wait_ge(dump_out, 32)
            act.wait_ge(pk_out[0], 48)
            act.wait_ge(pk_out[1], 48)
            iterations(act, body, pairs)
            stage_b_scalar(act)

        @block.vector
        def _(dve):
            v = nc.vector

            def stats1(q, t):
                wait(dve, mv1_ready, *tile_before(q, t, 3))
                hold(dve, dve_hold, h_ready, q, t)
                v.bn_stats(st[:, t % 3, :], h[:, q % 2, t, :]).then_inc(st1_ready.sem, 1)

            def mean1(q, t):
                wait(dve, y1_ready, *tile_before(q, t, 3))
                if t % 3 == 0:
                    wait(dve, ve1_ready, *group_before(q, t // 3))
                hold(dve, dve_hold, st1_ready, q, t)
                v.bn_aggr(mv1[:, t % 3, :], st[:, t % 3, :]).then_inc(mv1_ready.sem, 1)

            def variance1(q, g):
                wait(dve, mv1_ready, q, 3 * g + 2)
                wait(dve, rs1_ready, *group_before(q, g))
                v.tensor_scalar(ve1[:], mv1[:, :, 1], EPS, col(un, 9), ALU.add, ALU.mult).then_inc(ve1_ready.sem, 1)

            def norm1(q, t):
                wait(dve, rs1_ready, q, t // 3)
                if t >= 3:
                    wait(dve, tr_done, q, t - 3)
                else:
                    wait(dve, tr_done, q - 1, 6 + t)
                v.tensor_scalar(y1[:, t % 3, :], h[:, q % 2, t, :], mv1[:, t % 3, 0:1], rs1[:, t % 3:t % 3 + 1],
                                ALU.subtract, ALU.mult).then_inc(y1_ready.sem, 1)

            def at(g, c, first):
                if g == 1:
                    return y1t[:, c, :].rearrange("p (a s) -> p a s", a=2)[:, :, first:first + 192]
                return y1t[:, c, first:first + GROUP]

            def out_of(g, t):
                return t.rearrange("p (a s) -> p a s", a=2) if g == 1 else t

            def difference(q, g):
                wait(dve, y1t_ready, q, 3 * g + 2)
                wait(dve, xf_ready, q if g else q - 1, 3 * g - 1 if g else None)
                for c in range(2):
                    last = v.tensor_tensor(out_of(g, diff[:, c, :]), at(g, c, 1), at(g, c, 0), ALU.subtract)
                last.then_inc(diff_ready.sem, 1)

            def mixed(q, n):
                g, i = n // 3, n % 3
                wait(dve, diff_ready, q, g)
                free_xf(q, n)
                for c in range(2):
                    last = v.scalar_tensor_tensor(out_of(g, xf[:, n % 2, c, :]), out_of(g, diff[:, c, :]),
                                                  mixs[:, i, c:c + 1], at(g, c, 0), ALU.mult, ALU.add)
                last.then_inc(xf_ready.sem, 1)

            def free_xf(q, n):
                m, pair = (n - 2, q) if n >= 2 else (8 - n, q - 1)
                wait(dve, xh_ready, pair, m)
                if m % 3 == 0:
                    wait(dve, xl_ready, pair, m // 3)
                else:
                    wait(dve, xl_pool, pair, 2 * (m // 3) + m % 3 - 1)

            def low_keys(q, g):
                wait(dve, xh_ready, q, 3 * g)
                s = group_slot(g)
                v.tensor_tensor(xl[:, 0, :, s], xf[:, (3 * g) % 2], xh[:, 0, :, s], ALU.subtract).then_inc(
                    xl_ready.sem, 1)

            def clip_keys(q, t):
                wait(dve, kv_done, q, t)
                if t == 0:
                    wait(dve, sum_done, q - 1)
                    wait(dve, kv_ready, q - 1)
                v.tensor_scalar(k[:, t, :], b_proj[t % 2][:, 0:D], col(un, 10), col(un, 11), ALU.max,
                                ALU.min).then_inc(kc_ready.sem, 1)

            def times_values(q, t):
                wait(dve, k_ready, q, t)
                if t == 0:
                    wait(dve, wkv_done, q - 1)
                v.scalar_tensor_tensor(kv[:, t, :], b_proj[t % 2][:, D:2 * D], col(un, 1), k[:, t, :], ALU.mult,
                                       ALU.mult).then_inc(kv_ready.sem, 1)

            def clip_receptance(q, n):
                g, i = n // 2, n % 2
                wait(dve, r_done, q, n)
                if n == 0:
                    wait(dve, rwl_ready, q - 1)
                v.tensor_scalar(gate[:, i, g * GROUP:(g + 1) * GROUP], (b_w, b_s)[i][:, 0:GROUP], col(un, 13), None,
                                ALU.max).then_inc(rc_ready.sem, 1)

            def denominators(q, n):
                image, half, f = block_of(n)
                wait(dve, sum_done, q, n)
                wait(dve, gate_ready, q, 5 if n >= 4 else 3)
                dst = gate[:, f, block_cols(n)]
                mine = pieces(n)
                for j, (i, lo, hi) in enumerate(mine):
                    if i == 0:
                        last = v.tensor_tensor(dst[:, lo:hi], b_s[:, lo:hi], dst[:, lo:hi], ALU.mult)
                    else:
                        cc = HALF + 3 - len(mine) + j
                        last = v.scalar_tensor_tensor(dst[:, lo:hi], b_s[:, lo:hi], b_s[:, cc:cc + 1], dst[:, lo:hi],
                                                      ALU.add, ALU.mult)
                last.then_inc(den_ready.sem, 1)

            def invert(q, n):
                dst = gate[:, block_of(n)[2], block_cols(n)]
                wait(dve, den_ready, q, n)
                v.reciprocal(dst, dst).then_inc(inv_ready.sem, 1)

            def weigh(q, n):
                dst = gate[:, block_of(n)[2], block_cols(n)]
                wait(dve, wkv_done, q, n)
                wait(dve, inv_ready, q, n)
                v.scalar_tensor_tensor(dst, b_w[:, 0:HALF], col(sc, S_RW), dst, ALU.mult, ALU.mult).then_inc(
                    rw_ready.sem, 1)

            def residual(q, t):
                wait(dve, wo_done, q, t)
                if t >= 3:
                    wait(dve, h2_out[t % 3], q, t // 3 - 1)
                else:
                    wait(dve, h2_out[t % 3], q - 1)
                wait(dve, y2_ready, *tile_before(q, t, 3))
                dst = h2[:, t % 3, :]
                v.scalar_tensor_tensor(dst, b_proj[(TILES + t) % 2][:, 0:D], col(un, 3), h[:, q % 2, t, :], ALU.mult,
                                       ALU.add).then_inc(h2_ready.sem, 1)

            def stats2(q, t):
                wait(dve, mv2_ready, *tile_before(q, t, 3))
                hold(dve, dve_hold, h2_ready, q, t)
                v.bn_stats(st2[:, t % 3, :], h2[:, t % 3, :]).then_inc(st2_ready.sem, 1)

            def mean2(q, t):
                wait(dve, y2_ready, *tile_before(q, t, 3))
                if t % 3 == 0:
                    wait(dve, ve2_ready, *group_before(q, t // 3))
                hold(dve, dve_hold, st2_ready, q, t)
                v.bn_aggr(mv2[:, t % 3, :], st2[:, t % 3, :]).then_inc(mv2_ready.sem, 1)

            def variance2(q, g):
                wait(dve, mv2_ready, q, 3 * g + 2)
                wait(dve, rs2_ready, *group_before(q, g))
                v.tensor_scalar(ve2[:], mv2[:, :, 1], EPS, LN_SCALE ** -2, ALU.add, ALU.mult).then_inc(
                    ve2_ready.sem, 1)

            def norm2(q, t):
                wait(dve, rs2_ready, q, t // 3)
                wait(dve, yh_ready, q if t >= 3 else q - 1, (t - 3) % TILES)
                wait(dve, yl_ready, q if t >= 3 else q - 1, (t - 3) % TILES)
                v.tensor_scalar(y2[:, t % 3, :], h2[:, t % 3, :], mv2[:, t % 3, 0:1], rs2[:, t % 3:t % 3 + 1],
                                ALU.subtract, ALU.mult).then_inc(y2_ready.sem, 1)

            def logits(q, g):
                wait(dve, lg_done, q, g)
                if g == 0:
                    wait(dve, pos_ready, q - 1)
                v.tensor_tensor(lg[:, 3 * g:3 * g + 3, :], b_rt[:, 0:3 * E].rearrange("p (t e) -> p t e", e=E),
                                rb2s[:].unsqueeze(1).to_broadcast([P, 3, E]), ALU.add).then_inc(lg_ready.sem, 1)

            def wide(t):
                return t[:].to_broadcast([P, TILES, E])

            count = [0]

            def top_step(q, ins):
                ins.then_inc(top_link.sem, 1)
                wait(dve, top_link, q, count[0])
                count[0] += 1

            def top2(q, _):
                def link(ins):
                    top_step(q, ins)

                count[0] = 0
                wait(dve, lg_ready, q, 2)
                link(v.tensor_reduce(m1[:], lg[:], AX.X, ALU.max))
                link(v.tensor_tensor(t2[:], lg[:], wide(m1), ALU.subtract))
                v.tensor_scalar(t1[:], t2[:], -87.33654, None, ALU.max).then_inc(d_ready.sem, 1)
                wait(dve, d_ready, q)
                link(v.scalar_tensor_tensor(t2[:], t1[:], 0.0, rev[:], ALU.is_ge, ALU.mult))
                link(v.tensor_reduce(m2[:], t2[:], AX.X, ALU.max))
                link(v.tensor_tensor(oh1[:], t2[:], wide(m2), ALU.is_equal))
                link(v.scalar_tensor_tensor(t2[:], oh1[:], -1e30, t1[:], ALU.mult, ALU.add))
                link(v.tensor_reduce(m1[:], t2[:], AX.X, ALU.max))
                link(v.tensor_tensor(t2[:], t2[:], wide(m1), ALU.is_equal))
                link(v.tensor_tensor(t2[:], t2[:], rev[:], ALU.mult))
                link(v.tensor_reduce(m2[:], t2[:], AX.X, ALU.max))
                link(v.tensor_tensor(oh2[:], t2[:], wide(m2), ALU.is_equal))
                v.tensor_tensor(sel16[:, 0:TILES, :], oh1[:], oh2[:], ALU.add).then_inc(sel_ready.sem, 1)

            def second(q, _):
                def link(ins):
                    top_step(q, ins)

                wait(dve, ex_ready, q)
                link(v.tensor_reduce(m2[:], ex[:], AX.X, ALU.add))
                link(v.tensor_tensor(t2[:], ex[:], oh2[:], ALU.mult))
                link(v.tensor_reduce(g1[:], t2[:], AX.X, ALU.add))
                link(v.reciprocal(m2[:], m2[:]))
                v.scalar_tensor_tensor(g1[:], g1[:], -1.0, m2[:], ALU.add, ALU.mult).then_inc(q_in.sem, 1)

            def gates(q, _):
                def link(ins):
                    top_step(q, ins)

                wait(dve, q_ready, q)
                link(v.tensor_scalar(m1[:], g2[:], 1.0, None, ALU.add))
                link(v.reciprocal(m1[:], m1[:]))
                link(v.tensor_tensor(g2[:], g2[:], m1[:], ALU.mult))
                link(v.tensor_tensor(t2[:], oh1[:], wide(m1), ALU.mult))
                link(v.tensor_tensor(t1[:], oh2[:], wide(g2), ALU.mult))
                assert count[0] == TOP_LINKS, count
                v.tensor_tensor(row[:, :, D:D + E], t1[:], t2[:], ALU.add).then_inc(gw_ready.sem, 1)

            def positions(q, _):
                count = [0]

                def link(ins):
                    ins.then_inc(rank_link.sem, 1)
                    wait(dve, rank_link, q, count[0])
                    count[0] += 1

                link(v.tensor_copy(row[:, :, D + E:D + E + 1].bitcast(U32), idf[:].unsqueeze(2)))
                link(v.tensor_scalar(idf[:], idf[:], float(PAIR), None, ALU.add))
                wait(dve, rank_done, q)
                n = TILES * E
                link(v.tensor_tensor(t1[:], b_rt[:, 0:n].rearrange("p (t e) -> p t e", e=E),
                                     base[:].unsqueeze(1).to_broadcast([P, TILES, E]), ALU.add))
                v.tensor_tensor(t2[:], t1[:], oh2[:], ALU.mult)
                link(v.tensor_tensor(base[:], base[:], b_rt[:, n:n + E], ALU.add))
                link(v.tensor_tensor(t1[:], t1[:], oh1[:], ALU.mult))
                v.tensor_reduce(posf[:, 1, :], t2[:], AX.X, ALU.add)
                link(v.tensor_reduce(posf[:, 0, :], t1[:], AX.X, ALU.add))
                assert count[0] == RANK_LINKS, count
                if not isinstance(q, int) or q:
                    wait(dve, scat, q - 1)
                v.tensor_copy(posu[:], posf[:]).then_inc(pos_ready.sem, 1)

            def body(p):
                for name, n, q in steps(p, pairs):
                    if name in do:
                        do[name](q, n)

            do = {"stats1": stats1, "mean1": mean1, "variance1": variance1, "norm1": norm1,
                  "difference": difference, "difference2": difference, "mixed": mixed, "mixed2": mixed,
                  "low_keys": low_keys, "low_keys2": low_keys, "clip_keys": clip_keys, "times_values": times_values,
                  "clip_receptance": clip_receptance, "denominators": denominators, "invert": invert,
                  "weigh": weigh, "residual": residual, "stats2": stats2, "mean2": mean2, "variance2": variance2,
                  "norm2": norm2, "add_logit_bias": logits, "top2": top2, "second": second, "gates": gates,
                  "positions": positions}

            chain = [0]

            def link(ins):
                ins.then_inc(setup_link, 1)
                chain[0] += 1
                dve.wait_ge(setup_link, chain[0])

            v.memset(zrow[:, 0:128], 0.0).then_inc(setup_v, 1)
            link(v.memset(mx[:], 0.0))
            v.memset(half3[:], -0.5)
            v.memset(zero2[:], 0.0)
            v.memset(sel16[:], 0.0)
            v.memset(row[:], 0.0).then_inc(setup_v, 1)
            dve.wait_ge(setup_p, 7)
            v.tensor_copy(id16[:], id32[:])
            v.tensor_copy(before[:], upto[:])
            v.tensor_copy(idf[:], idi[:])
            link(v.tensor_copy(tk[:], tki[:]))
            link(v.tensor_tensor(before[:], before[:], id16[:], ALU.subtract))
            for e in range(E):
                v.memset(rev[:, :, e], float(E - e))
                v.memset(rbase[:, e:e + 1], float(e * region))
            link(v.memset(ones16[:], 1.0))
            v.tensor_copy(base[:], rbase[:]).then_inc(setup_v, 1)
            dve.wait_ge(ld, 16 * 12)
            dve.wait_ge(ld_e, 16 * 21)

            def largest(i, src, axis):
                link(v.tensor_reduce(mx[:, i:i + 1], src, axis, ALU.max, apply_absolute_value=True))

            for i in range(4):
                largest(i, raw_w[:, i], AX.XY)
            largest(4, raw_r1, AX.XY)
            for i in range(3):
                largest(5 + i, raw_e[:, :, i].rearrange("p e c n -> p e (c n)"), AX.XY)
            largest(8, mixs[:], AX.XY)
            link(v.tensor_scalar(omm[:], mixs[:], -1.0, 1.0, ALU.mult, ALU.add))
            largest(9, omm[:], AX.XY)
            largest(10, zrow[:, 128:768], AX.X)
            largest(11, raw_b[:, 0:12], AX.X)
            v.tensor_reduce(mx[:, 12:13], raw_b[:, 12:24], AX.X, ALU.max, apply_absolute_value=True).then_inc(
                amax_ready, 1)
            dve.wait_ge(setup_p, 8)

            def a(i):
                return mxa[:, i:i + 1]

            link(v.tensor_copy(bd[:, 0:8], mxa[:, 0:8]))
            link(v.tensor_scalar(bd[:, 8:9], a(8), a(9), 16.0, ALU.add, ALU.mult))
            link(v.tensor_scalar(bd[:, 9:10], bd[:, 8:9], a(1), 16.0, ALU.mult, ALU.mult))
            link(v.tensor_scalar(bd[:, 9:10], bd[:, 9:10], a(10), None, ALU.mult))
            link(v.tensor_scalar(bd[:, 10:11], a(5), 256.0, a(11), ALU.mult, ALU.add))
            link(v.tensor_scalar(bd[:, 11:12], bd[:, 10:11], a(6), 256.0, ALU.mult, ALU.mult))
            link(v.tensor_scalar(bd[:, 11:12], bd[:, 11:12], a(12), None, ALU.add))
            link(v.tensor_scalar(bd[:, 0:NS], bd[:, 0:NS], 1e-12, None, ALU.max))
            link(v.tensor_scalar(bd[:, 0:NS].bitcast(U32), bd[:, 0:NS].bitcast(U32), 0x7F800000, None,
                                 ALU.bitwise_and))
            link(v.reciprocal(sc[:, 0:NS], bd[:, 0:NS]))
            link(v.tensor_scalar(sc[:, 0:NS], sc[:, 0:NS], SLACK, None, ALU.mult))
            link(v.tensor_scalar(isc[:, 0:NS], bd[:, 0:NS], 1.0 / SLACK, None, ALU.mult))
            link(v.memset(un[:], 0.0))
            link(v.tensor_scalar(un[:, 0:3], isc[:, 0:3], isc[:, S_MIX:S_MIX + 1], None, ALU.mult))
            link(v.tensor_scalar(un[:, 2:3], un[:, 2:3], -1.0, None, ALU.mult))
            link(v.tensor_scalar(un[:, 3:4], isc[:, 3:4], isc[:, S_RW:S_RW + 1], None, ALU.mult))
            link(v.tensor_scalar(un[:, 4:5], isc[:, 4:5], 1.0 / LN_SCALE, None, ALU.mult))
            link(v.tensor_scalar(un[:, 5:6], isc[:, 5:6], 1.0 / LN_SCALE, sc[:, S_H1:S_H1 + 1], ALU.mult, ALU.mult))
            link(v.tensor_scalar(un[:, 6:7], isc[:, 6:7], isc[:, S_H1:S_H1 + 1], sc[:, S_H2:S_H2 + 1], ALU.mult,
                                 ALU.mult))
            link(v.tensor_scalar(un[:, 7:8], isc[:, 7:8], isc[:, S_H2:S_H2 + 1], None, ALU.mult))
            link(v.tensor_scalar(un[:, 9:10], isc[:, S_MIX:S_MIX + 1], isc[:, S_MIX:S_MIX + 1], None, ALU.mult))
            link(v.tensor_scalar(un[:, 12:13], sc[:, 0:1], sc[:, S_MIX:S_MIX + 1], None, ALU.mult))
            link(v.tensor_scalar(un[:, 10:11], un[:, 12:13], -60.0, None, ALU.mult))
            link(v.tensor_tensor(un[:, 14:15], sc[:, 2:3], sc[:, S_MIX:S_MIX + 1], ALU.mult))
            link(v.tensor_scalar(un[:, 13:14], un[:, 14:15], -50.0, None, ALU.mult))
            v.tensor_scalar(un[:, 11:12], un[:, 12:13], 30.0, None, ALU.mult).then_inc(scales_ready, 1)
            for i in range(4):
                dve.wait_ge(wsplit, i + 1)
                v.scalar_tensor_tensor(wl[:, i], raw_w[:, i], col(sc, i), wh[:, i], ALU.mult,
                                       ALU.subtract).then_inc(split_ready, 1)
            dve.wait_ge(wsplit, 5)
            v.scalar_tensor_tensor(rwa[:, 1], raw_r1, col(sc, 4), rwa[:, 0], ALU.mult, ALU.subtract).then_inc(
                split_ready, 1)
            dve.wait_ge(setup_p, 6)
            v.tensor_copy(filler[:, :, D + E:D + E + 1].bitcast(U32), fill_id[:].unsqueeze(2)).then_inc(setup_v, 1)
            for e in range(E):
                for i in range(3):
                    dve.wait_ge(pkh_ready, 4 * e + i + 1)
                    last = v.scalar_tensor_tensor(packm[e % 2][:, i, 1], raw_e[:, e, i], col(sc, 5 + i),
                                                  packm[e % 2][:, i, 0], ALU.mult, ALU.subtract)
                last.then_inc(pk_ready, 1)
            dve.wait_ge(pk_ready, E)
            v.memset(arena[KP:KP + 1, 0:PAIR * PATCH:PATCH], 1.0).then_inc(ones_ready, 1)
            iterations(dve, body, pairs)
            stage_b_vector(dve)

        @block.gpsimd
        def _(pool):
            g_ = nc.gpsimd

            def low_half(q, m):
                n, i = m // 2, 1 + m % 2
                wait(pool, xh_ready, q, 3 * n + i)
                g_.tensor_tensor(xl[:, i, :, group_slot(n)], xf[:, (3 * n + i) % 2], xh[:, i, :, group_slot(n)],
                                 ALU.subtract).then_inc(xl_pool.sem, 1)

            def low_sum(q, n):
                wait(pool, rwh_ready, q, n)
                f, s = block_of(n)[2], block_cols(n)
                g_.tensor_tensor(rwl[:, f, s], gate[:, f, s], rwh[:, f, s], ALU.subtract).then_inc(rwl_ready.sem, 1)

            def root1(q, g):
                wait(pool, ve1_ready, q, g)
                wait(pool, y1_ready, q if g else q - 1, 3 * g - 1 if g else None)
                g_.tensor_tensor(rs1[:], ve1[:], half3[:], ALU.pow).then_inc(rs1_ready.sem, 1)

            def root2(q, g):
                wait(pool, ve2_ready, q, g)
                wait(pool, y2_ready, q if g else q - 1, 3 * g - 1 if g else None)
                g_.tensor_tensor(rs2[:], ve2[:], half3[:], ALU.pow).then_inc(rs2_ready.sem, 1)

            def norm2_low(q, t):
                wait(pool, yh_ready, q, t)
                g_.tensor_tensor(row[:, t, P:D].bitcast(F16), y2[:, t % 3, :], row[:, t, 0:P].bitcast(F16),
                                 ALU.subtract).then_inc(yl_ready.sem, 1)

            def scatter(q, n):
                wait(pool, gw_ready, q)
                hold(pool, pool_hold, pos_ready, q)
                for i in range(2):
                    g_.indirect_dma_start(lists, bass.IndirectOffsetOnAxis(ap=posu[:, i, n:n + 1], axis=0),
                                          row[:, n, :], None).then_inc(scat.sem, 16)

            do = {"low_half": low_half, "low_half2": low_half, "low_sum": low_sum, "root1": root1, "root2": root2,
                  "norm2_low": norm2_low, "scatter": scatter}

            def body(p):
                for name, n, q in steps(p, pairs):
                    if name in do:
                        do[name](q, n)

            g_.memset(id32[:], 0.0).then_inc(setup_p, 1)
            g_.memset(upto[:], 1.0).then_inc(setup_p, 1)
            g_.memset(carry_w[:], 1.0).then_inc(setup_p, 1)
            pool.wait_ge(setup_p, 3)
            g_.memset(carry_w[:, 0:2], 0.0).then_inc(setup_p, 1)
            g_.memset(filler[:], 0.0).then_inc(setup_p, 1)
            g_.iota(fill_id[:], pattern=[[P, 4]], base=tokens, channel_multiplier=1).then_inc(setup_p, 1)
            g_.affine_select(out=id32[:], in_=id32[:], compare_op=ALU.not_equal, fill=1.0, base=0, pattern=[[-1, P]],
                             channel_multiplier=1)
            g_.affine_select(out=upto[:], in_=upto[:], compare_op=ALU.is_ge, fill=0.0, base=0, pattern=[[1, P]],
                             channel_multiplier=-1)
            g_.iota(tki[:], pattern=[[1, btiles]], base=0, channel_multiplier=0)
            g_.iota(idi[:], pattern=[[P, TILES]], base=0, channel_multiplier=1).then_inc(setup_p, 1)
            pool.wait_ge(amax_ready, 1)
            g_.partition_all_reduce(mxa[:], mx[:], P, bass.bass_isa.ReduceOp.max).then_inc(setup_p, 1)
            pool.wait_ge(setup_v, 3)
            iterations(pool, body, pairs)
            stage_b_pool(pool)


def kernel(x, L0_tok_W, L0_tok_b, L0_attn_time_w, L0_attn_time_mix_k, L0_attn_time_mix_v, L0_attn_time_mix_r,
           L0_attn_Wk, L0_attn_Wv, L0_attn_Wr, L0_attn_Wo, L0_ffn_router_w1, L0_ffn_router_b1, L0_ffn_router_w2,
           L0_ffn_router_b2, L0_ffn_expert_w1, L0_ffn_expert_b1, L0_ffn_expert_w2, L0_ffn_expert_b2,
           L0_ffn_expert_w3, L0_ffn_expert_b3):
    from concourse import bacc
    from concourse.bass_utils import run_bass_kernel_spmd

    def spread(a):
        a = np.asarray(a).reshape(1, -1)
        return np.broadcast_to(a, (P, a.shape[1]))

    def by_partition(a):
        return np.asarray(a).reshape(-1, 2, P).transpose(2, 0, 1).reshape(P, -1)

    mixes = np.stack([np.asarray(m).reshape(D) for m in (L0_attn_time_mix_k, L0_attn_time_mix_v,
                                                         L0_attn_time_mix_r)])
    arrays = {
        "x": np.asarray(x),
        "tok_w": np.asarray(L0_tok_W).reshape(D, CH, PATCH, 2, QS).transpose(3, 1, 2, 4, 0).reshape(KP, QS, D),
        "tok_b": np.asarray(L0_tok_b).reshape(1, D),
        "decay": spread(np.asarray(L0_attn_time_w)[::-1][:640]),
        "mix": by_partition(mixes).reshape(P, 3, 2),
        "wk": L0_attn_Wk, "wv": L0_attn_Wv, "wr": L0_attn_Wr, "wo": L0_attn_Wo,
        "rw1": L0_ffn_router_w1, "rb1": np.asarray(L0_ffn_router_b1).reshape(P, 1),
        "rw2": L0_ffn_router_w2, "rb2": spread(L0_ffn_router_b2),
        "ew1": L0_ffn_expert_w1, "eb1": by_partition(L0_ffn_expert_b1),
        "ew2": L0_ffn_expert_w2, "eb2": by_partition(L0_ffn_expert_b2),
        "ew3": L0_ffn_expert_w3,
        "eb3": np.broadcast_to(np.asarray(L0_ffn_expert_b3).reshape(1, E, D), (P, E, D)),
    }
    arrays = {n: np.ascontiguousarray(a) for n, a in arrays.items()}
    images = arrays["x"].shape[0]
    nc = bacc.Bacc("TRN2", target_bir_lowering=False, num_devices=1)
    args = {n: nc.dram_tensor(f"in_{n}", a.shape, mybir.dt.from_np(a.dtype), kind="ExternalInput").ap()
            for n, a in arrays.items()}
    out = nc.dram_tensor("out_rows", (images * IMG + BT, D), F32, kind="ExternalOutput").ap()
    build(nc, out=out, **args)
    r = run_bass_kernel_spmd(nc, [{f"in_{n}": a for n, a in arrays.items()}], core_ids=[0])
    return r.results[0]["out_rows"][:images * IMG].reshape(images, IMG, D)
```

```python
from contextlib import ExitStack

import numpy as np

import concourse.bass as bass
from concourse import mybir

F32, F16 = mybir.dt.float32, mybir.dt.float16
U32, I32 = mybir.dt.uint32, mybir.dt.int32
ALU = mybir.AluOpType
ACT = mybir.ActivationFunctionType
AX = mybir.AxisListType

P = 128
PATCH, SIDE, CH = 16, 24, 3
IMG = SIDE * SIDE
PAIR = 2 * IMG
TILES = PAIR // P
GROUP = 3 * P
D = 256
E = 6
QS = 8
KP = 2 * CH * PATCH
HALF = 288
BT = 512
ROW = 264
SLACK = 8192.0
LN_SCALE = 1024.0
EPS = 1e-5
EW_B, EW_B3 = 1536, 1540
EW = 1796
NEXT, THIS, LAST = 1, 0, -1

STEPS = [
    ("embed", 0), ("embed", 1), ("route_transpose", 0), ("project_late", 6), ("project_late", 7),
    ("residual_late", 6), ("embedded", 0), ("receptance", 0), ("residual_late", 7), ("embedded", 1),
    ("route_transposed", 0), ("project_late", 8), ("clip_receptance", 0), ("route_transpose", 1),
    ("residual_late", 8), ("exp_receptance", 0), ("values", 0), ("stats2_late", 6), ("route_transposed", 1),
    ("stats2_late", 7), ("one_plus", 0), ("mean2_late", 6), ("route_transpose", 2), ("mean2_late", 7), ("values", 1),
    ("clip_keys", 0), ("route_transposed", 2), ("stats2_late", 8), ("mean2_late", 8), ("router", 0),
    ("variance2_late", 2), ("stats1", 0), ("root2_late", 2), ("stats1", 1), ("receptance", 1), ("mean1", 0),
    ("router_relu", 0), ("mean1", 1), ("difference_late", 2), ("clip_keys", 1), ("exp_keys", 0), ("logits", 0),
    ("exp_keys", 1), ("receptance", 2), ("add_logit_bias", 0), ("times_values", 0), ("norm2_late", 6),
    ("norm2_late", 7), ("route_transpose", 3), ("mixed_late", 6), ("norm2_high_late", 6), ("values", 2),
    ("route_transposed", 3), ("norm2_low_late", 6), ("mixed_late", 7), ("route_transpose", 4), ("mixed_high_late", 6),
    ("embed", 2), ("clip_receptance", 1), ("route_transposed", 4), ("low_keys_late", 2), ("clip_keys", 2),
    ("norm2_late", 8), ("times_values", 1), ("norm2_high_late", 7), ("norm2_high_late", 8), ("clip_receptance", 2),
    ("mixed_high_late", 7), ("norm2_low_late", 7), ("mixed_late", 8), ("low_half_late", 4), ("route_transpose", 5),
    ("receptance", 3), ("mixed_high_late", 8), ("values", 3), ("route_transposed", 5), ("clip_receptance", 3),
    ("low_half_late", 5), ("exp_keys", 2), ("embedded", 2), ("times_values", 2), ("router", 1), ("exp_receptance", 1),
    ("stats1", 2), ("exp_receptance", 2), ("clip_keys", 3), ("receptance", 4), ("router_relu", 1),
    ("exp_receptance", 3), ("receptance", 5), ("clip_receptance", 4), ("exp_keys", 3), ("one_plus", 1), ("mean1", 2),
    ("logits", 1), ("variance1", 0), ("one_plus", 2), ("times_values", 3), ("values", 4), ("root1", 0),
    ("clip_receptance", 5), ("one_plus", 3), ("add_logit_bias", 1), ("norm2_low_late", 8), ("norm1", 0), ("sums", 0),
    ("clip_keys", 4), ("route_transpose", 6), ("denominators", 0), ("decayed", 0), ("route_transposed", 6),
    ("invert", 0), ("route_transpose", 7), ("sums", 1), ("route_transposed", 7), ("transpose", 0),
    ("route_transpose", 8), ("transposed", 0), ("values", 5), ("route_transposed", 8), ("denominators", 1),
    ("exp_receptance", 4), ("router", 2), ("exp_receptance", 5), ("weigh", 0), ("invert", 1), ("one_plus", 4),
    ("decayed", 1), ("router_relu", 2), ("norm1", 1), ("logits", 2), ("norm1", 2), ("transpose", 1),
    ("add_logit_bias", 2), ("embed", 3), ("weighed_high", 0), ("top2", 0), ("transposed", 1), ("low_sum", 0),
    ("exp_keys", 4), ("times_values", 4), ("exp_logits", 0), ("rank", 0), ("second", 0), ("values", 6), ("weigh", 1),
    ("exp_second", 0), ("transpose", 2), ("sums", 2), ("gates", 0), ("weighed_high", 1), ("embedded", 3),
    ("embed", 4), ("low_sum", 1), ("transposed", 2), ("difference", 0), ("positions", 0), ("clip_keys", 5),
    ("scatter", 0), ("clip_keys", 6), ("embed", 5), ("exp_keys", 5), ("denominators", 2), ("exp_keys", 6),
    ("embedded", 4), ("times_values", 5), ("mixed", 0), ("scatter", 1), ("times_values", 6), ("mixed", 1),
    ("sums", 3), ("embedded", 5), ("scatter", 2), ("values", 7), ("stats1", 3), ("stats1", 4), ("stats1", 5),
    ("values", 8), ("clip_keys", 7), ("scatter", 3), ("denominators", 3), ("exp_keys", 7), ("decayed", 2),
    ("one_plus", 5), ("invert", 2), ("mixed_high", 0), ("scatter", 4), ("sums", 4), ("mean1", 3), ("embed", 6),
    ("mean1", 4), ("mean1", 5), ("clip_keys", 8), ("denominators", 4), ("scatter", 5), ("times_values", 7),
    ("variance1", 1), ("weigh", 2), ("invert", 3), ("project", 0), ("root1", 1), ("decayed", 3), ("low_keys", 0),
    ("invert", 4), ("norm1", 3), ("weighed_high", 2), ("embedded", 6), ("norm1", 4), ("transpose", 3), ("scatter", 6),
    ("sums", 5), ("exp_keys", 8), ("stats1", 6), ("norm1", 5), ("embed", 7), ("residual", 0), ("times_values", 8),
    ("denominators", 5), ("low_sum", 2), ("stats2", 0), ("scatter", 7), ("mixed", 2), ("weigh", 3), ("sums", 6),
    ("transposed", 3), ("invert", 5), ("transpose", 4), ("decayed", 4), ("transposed", 4), ("scatter", 8),
    ("mixed_high", 1), ("transpose", 5), ("embedded", 7), ("embed", 8), ("denominators", 6), ("weighed_high", 3),
    ("transposed", 5), ("low_half", 0), ("mean1", 6), ("mixed_high", 2), ("weigh", 4), ("invert", 6), ("low_sum", 3),
    ("decayed", 5), ("difference", 1), ("mean2", 0), ("embedded", 8), ("stats1", 7), ("weighed_high", 4),
    ("stats1", 8), ("project", 1), ("mean1", 7), ("mean1", 8), ("weigh", 5), ("low_half", 1), ("project", 2),
    ("variance1", 2), ("mixed", 3), ("weighed_high", 5), ("decayed", 6), ("residual", 1), ("mixed_high", 3),
    ("root1", 2), ("residual", 2), ("stats2", 1), ("low_keys", 1), ("stats2", 2), ("norm1", 6), ("project", 3),
    ("mean2", 1), ("norm1", 7), ("mean2", 2), ("weigh", 6), ("transpose", 6), ("norm1", 8), ("sums", 7),
    ("variance2", 0), ("mixed", 4), ("root2", 0), ("decayed", 7), ("low_sum", 4), ("mixed", 5), ("norm2", 0),
    ("norm2", 1), ("low_sum", 5), ("residual", 3), ("transposed", 6), ("denominators", 7), ("transpose", 7),
    ("project", 4), ("transposed", 7), ("stats2", 3), ("weighed_high", 6), ("project", 5), ("invert", 7),
    ("norm2", 2), ("low_sum", 6), ("transpose", 8), ("norm2_high", 0), ("norm2_high", 1), ("norm2_low", 0),
    ("mixed_high", 4), ("norm2_low", 1), ("residual", 4), ("norm2_high", 2), ("transposed", 8), ("residual", 5),
    ("norm2_low", 2), ("stats2", 4), ("stats2", 5), ("mean2", 3), ("mean2", 4), ("mean2", 5), ("weigh", 7),
    ("variance2", 1), ("weighed_high", 7), ("root2", 1), ("low_sum", 7), ("norm2", 3), ("norm2_high", 3),
    ("norm2", 4), ("norm2_low", 3), ("norm2", 5), ("norm2_high", 4), ("mixed_high", 5), ("norm2_low", 4),
    ("norm2_high", 5), ("low_half", 2), ("low_half", 3), ("norm2_low", 5),
]
LEAD = {
    "embed": NEXT, "embedded": NEXT, "stats1": NEXT, "mean1": NEXT, "variance1": NEXT, "root1": NEXT,
    "norm1": NEXT, "transpose": NEXT, "transposed": NEXT, "difference": NEXT, "mixed": NEXT,
    "mixed_high": NEXT, "low_half": NEXT, "low_keys": NEXT,
    "difference_late": THIS, "mixed_late": THIS, "mixed_high_late": THIS, "low_half_late": THIS,
    "low_keys_late": THIS, "values": THIS, "clip_keys": THIS, "exp_keys": THIS, "times_values": THIS,
    "receptance": THIS, "clip_receptance": THIS, "exp_receptance": THIS, "one_plus": THIS, "sums": THIS,
    "decayed": THIS, "denominators": THIS, "invert": THIS, "weigh": THIS, "weighed_high": THIS,
    "low_sum": THIS, "project": THIS, "residual": THIS, "stats2": THIS, "mean2": THIS, "variance2": THIS,
    "root2": THIS, "norm2": THIS, "norm2_high": THIS, "norm2_low": THIS,
    "route_transpose": LAST, "route_transposed": LAST, "router": LAST, "router_relu": LAST, "logits": LAST,
    "add_logit_bias": LAST, "top2": LAST, "exp_logits": LAST, "second": LAST, "exp_second": LAST,
    "gates": LAST, "rank": LAST, "positions": LAST, "scatter": LAST, "project_late": LAST,
    "residual_late": LAST, "stats2_late": LAST, "mean2_late": LAST, "variance2_late": LAST, "root2_late": LAST,
    "norm2_late": LAST, "norm2_high_late": LAST, "norm2_low_late": LAST,
}


def first_time(pair):
    return isinstance(pair, int) and pair == 0


def base_name(name):
    return name.removesuffix("_late")


class Signal:

    def __init__(self, sem, per, unit=1):
        self.sem, self.per, self.unit = sem, per, unit

    def after(self, pair, n=None):
        return (pair * self.per + (self.per if n is None else n + 1)) * self.unit


def wait(eng, signal, pair, n=None):
    v = signal.after(pair, n)
    if not isinstance(v, int) or v > 0:
        eng.wait_ge(signal.sem, v)


def tile_before(pair, t, n):
    return (pair, t - n) if t >= n else (pair - 1, t - n + TILES)


def group_before(pair, g):
    return (pair, g - 1) if g else (pair - 1, 2)


def hold(eng, spacer, signal, pair, n=None):
    wait(eng, signal, pair, n)
    eng.sem_inc(spacer, 1)


def iterations(eng, body, pairs, last=1):
    body(-1)
    body(0)
    with eng.Fori(1, pairs - last) as p:
        body(p)
    for p in range(pairs - last, pairs + 1):
        body(p)


def steps(p, pairs):
    routing = ("route_transpose", "route_transposed", "router", "router_relu", "logits", "add_logit_bias")
    early = {(name, n) for name in routing for n in range(6 if name.startswith("route_") else 2)}
    for name, n in STEPS:
        q = p + LEAD[name]
        if isinstance(p, int) and p == pairs and (name, n) in early:
            continue
        if not isinstance(p, int) or 0 <= q < pairs:
            yield name, n, q
        if isinstance(p, int) and p == pairs - 1 and name == "norm2_low":
            for step in routing[:2]:
                yield step, n, p
            if n % 3 == 2:
                for step in routing[2:]:
                    yield step, n // 3, p


def build(nc, x, tok_w, tok_b, decay, mix, wk, wv, wr, wo, rw1, rb1, rw2, rb2, ew1, eb1, ew2, eb2, ew3, eb3,
          out):
    images = x.shape[0]
    pairs = images // 2
    tokens = images * IMG
    region = tokens + BT
    btiles = (2 * tokens + E * (BT - 1)) // BT
    dummy = E * region
    assert pairs >= 4 and region * (E + 1) < 1 << 24

    ctx = ExitStack()
    with ctx:
        def sb(name, shape, dt=F32):
            return ctx.enter_context(nc.sbuf_tensor(name, shape, dt))

        def sem(name):
            return ctx.enter_context(nc.semaphore(name))

        def sig(name, per, unit=1):
            return Signal(sem(name), per, unit)

        lists = nc.dram_tensor("expert_lists", [dummy + BT, ROW], F32, kind="Internal").ap()
        packs = nc.dram_tensor("expert_packages", [E, P, EW], F32, kind="Internal").ap()
        skew = nc.dram_tensor("skewed_decay", [P * 800], F32, kind="Internal").ap()

        arena = sb("arena", [P, 2 * IMG * PATCH])
        embed_w = sb("embed_w", [KP + 1, QS, D])
        h = sb("h", [P, 2, TILES, D])
        y1 = sb("y1", [P, 3, D])
        y1t = sb("y1t", [P, 2, 386])
        diff = sb("diff", [P, 2, GROUP])
        xf = sb("xf", [P, 2, 2, GROUP])
        xh = sb("xh", [P, 3, 2, 2 * GROUP], F16)
        xl = sb("xl", [P, 3, 2, 2 * GROUP], F16)
        k = sb("k", [P, TILES, D])
        kv = sb("kv", [P, TILES, D])
        gate = sb("gate", [P, 2, PAIR])
        rwh = sb("rwh", [P, 2, PAIR], F16)
        rwl = sb("rwl", [P, 2, PAIR], F16)
        h2 = sb("h2", [P, 3, D])
        y2 = sb("y2", [P, 3, D])
        row = sb("row", [P, TILES, ROW])
        y2t = sb("y2t", [P, 4, GROUP], F16)
        rh = sb("rh", [P, GROUP])
        wh = sb("wh", [P, 4, 2, D], F16)
        wl = sb("wl", [P, 4, 2, D], F16)
        rwa = sb("rwa", [P, 2, 2, P], F16)
        rw2s = sb("rw2s", [P, E])
        rb1s = sb("rb1s", [P, 1])
        rb2s = sb("rb2s", [P, E])
        mixs = sb("mixs", [P, 3, 2])
        dec = sb("dec", [P, 640])
        upto = sb("upto", [P, P])
        carry = sb("carry", [P, 2, 3])
        minus3 = sb("minus3", [P, 3])
        before = sb("before", [P, P], F16)
        ones16 = sb("ones16", [P, P], F16)
        id16 = sb("id16", [P, P], F16)
        id32 = sb("id32", [P, P])
        half3 = sb("half3", [P, 3])
        zero2 = sb("zero2", [P, 2])
        st = sb("st", [P, 3, 6])
        mv1 = sb("mv1", [P, 3, 2])
        ve1 = sb("ve1", [P, 3])
        rs1 = sb("rs1", [P, 3])
        mm1 = sb("mm1", [P, 3])
        nm1 = sb("nm1", [P, 3])
        st2 = sb("st2", [P, 3, 6])
        mv2 = sb("mv2", [P, 3, 2])
        ve2 = sb("ve2", [P, 3])
        rs2 = sb("rs2", [P, 3])
        mm2 = sb("mm2", [P, 3])
        nm2 = sb("nm2", [P, 3])
        lg = sb("lg", [P, TILES, E])
        t1 = sb("t1", [P, TILES, E])
        oh1 = sb("oh1", [P, TILES, E])
        oh2 = sb("oh2", [P, TILES, E])
        t2 = sb("t2", [P, TILES, E])
        ex = sb("ex", [P, TILES, E])
        sel16 = sb("sel16", [P, TILES + 1, E], F16)
        base = sb("base", [P, E])
        rev = sb("rev", [P, TILES, E])
        m1 = sb("m1", [P, TILES, 1])
        m2 = sb("m2", [P, TILES, 1])
        g1 = sb("g1", [P, TILES, 1])
        g2 = sb("g2", [P, TILES, 1])
        posf = sb("posf", [P, 2, TILES])
        posu = sb("posu", [P, 2, TILES], U32)
        idf = sb("idf", [P, TILES])
        idi = sb("idi", [P, TILES], I32)
        mx = sb("mx", [P, 20])
        mxa = sb("mxa", [P, 20])
        omm = sb("omm", [P, 3, 2])
        bd = sb("bd", [P, 16])
        sc = sb("sc", [P, 16])
        isc = sb("isc", [P, 16])
        un = sb("un", [P, 16])
        cnt = sb("cnt", [P, E])
        nti = sb("nti", [P, E], I32)
        ntf = sb("ntf", [P, E])
        cum = sb("cum", [P, E + 1])
        tk = sb("tk", [1, btiles])
        tki = sb("tki", [1, btiles], I32)
        tge = sb("tge", [1, btiles])
        toff = sb("toff", [1, btiles])
        texp = sb("texp", [1, btiles])
        table = sb("table", [1, 2, btiles], I32)
        rbase = sb("rbase", [P, E])
        tails = sb("tails", [1, E], I32)
        fill_id = sb("fill_id", [P, 4], I32)

        def bank(name):
            return ctx.enter_context(nc.psum_tensor(name, [P, 512], F32))

        b_tok = [bank("b_tok0"), bank("b_tok1")]
        b_tr = bank("b_tr")
        b_rt = bank("b_rt")
        b_proj = [bank("b_proj0"), bank("b_proj1")]
        b_w = bank("b_w")
        b_s = bank("b_s")

        x_in = [sig("x_in0", 1, 96), sig("x_in1", 1, 96)]
        tok_done = sig("tok_done", TILES)
        h_ready = sig("h_ready", TILES)
        st1_ready = sig("st1_ready", TILES)
        mv1_ready = sig("mv1_ready", TILES)
        ve1_ready = sig("ve1_ready", 3)
        rs1_ready = sig("rs1_ready", 3)
        mm1_ready = sig("mm1_ready", 3)
        pow1_ready = sig("pow1_ready", 3)
        y1_ready = sig("y1_ready", TILES)
        tr_done = sig("tr_done", TILES)
        y1t_ready = sig("y1t_ready", TILES)
        diff_ready = sig("diff_ready", 3)
        xf_ready = sig("xf_ready", 9)
        xh_ready = sig("xh_ready", 9)
        xl_ready = sig("xl_ready", 3)
        xl_pool = sig("xl_pool", 6)
        kv_done = sig("kv_done", TILES)
        kc_ready = sig("kc_ready", TILES)
        k_ready = sig("k_ready", TILES)
        kv_ready = sig("kv_ready", TILES)
        r_done = sig("r_done", 6)
        rc_ready = sig("rc_ready", 6)
        e_ready = sig("e_ready", 6)
        gate_ready = sig("gate_ready", 6)
        carry_ready = sig("carry_ready", 12)
        sum_done = sig("sum_done", 8)
        wkv_done = sig("wkv_done", 8)
        den_ready = sig("den_ready", 8)
        inv_ready = sig("inv_ready", 8)
        rw_ready = sig("rw_ready", 8)
        rwh_ready = sig("rwh_ready", 8)
        rwl_ready = sig("rwl_ready", 8)
        wo_done = sig("wo_done", TILES)
        h2_ready = sig("h2_ready", TILES)
        h2_out = [sig(f"h2_out{i}", 3, 16) for i in range(3)]
        st2_ready = sig("st2_ready", TILES)
        mv2_ready = sig("mv2_ready", TILES)
        ve2_ready = sig("ve2_ready", 3)
        rs2_ready = sig("rs2_ready", 3)
        mm2_ready = sig("mm2_ready", 3)
        pow2_ready = sig("pow2_ready", 3)
        y2_ready = sig("y2_ready", TILES)
        yh_ready = sig("yh_ready", TILES)
        yl_ready = sig("yl_ready", TILES)
        rtt_done = sig("rtt_done", TILES)
        y2t_ready = sig("y2t_ready", TILES)
        rh_done = sig("rh_done", 3)
        rh_ready = sig("rh_ready", 3)
        lg_done = sig("lg_done", 3)
        lg_ready = sig("lg_ready", 3)
        TOP_LINKS = 20
        top_link = sig("top_link", TOP_LINKS)
        d_ready = sig("d_ready", 1)
        ex_ready = sig("ex_ready", 1)
        q_in = sig("q_in", 1)
        q_ready = sig("q_ready", 1)
        sel_ready = sig("sel_ready", 1)
        gw_ready = sig("gw_ready", 1)
        rank_done = sig("rank_done", 1)
        RANK_LINKS = 6
        rank_link = sig("rank_link", RANK_LINKS)
        pos_ready = sig("pos_ready", 1)
        scat = sig("rows_out", 2 * TILES, 16)

        dve_hold = sem("vector_hold")
        act_hold = sem("scalar_hold")
        pool_hold = sem("pool_hold")
        ld = sem("weights_in")
        ld_e = sem("expert_biases_in")
        ld_m = [sem(f"expert_matrices_in{i}") for i in range(3)]
        setup_v = sem("setup_vector")
        setup_link = sem("setup_link")
        setup_p = sem("setup_pool")
        setup_a = sem("setup_scalar")
        amax_ready = sem("amax_ready")
        scales_ready = sem("scales_ready")
        skew_out = sem("skew_out")
        dec_in = sem("dec_in")
        pk_ready = sem("package_ready")
        pkh_ready = sem("package_high_ready")
        pk_out = [sem(f"package_out{i}") for i in range(4)]
        ones_ready = sem("ones_ready")
        dump_out = sem("dump_rows_out")
        wsplit = sem("weights_high_ready")
        split_ready = sem("weights_split")

        W_S = {"k": 0, "v": 1, "r": 2, "o": 3, "r1": 4, "e1": 5, "e2": 6, "e3": 7}
        S_MIX, S_RW, S_H1, S_H2 = 8, 9, 10, 11
        NS = 12

        def col(t, i):
            return t[:, i:i + 1]

        raw_w = gate[:, :, :].rearrange("p a b -> p (a b)")[:, 0:2048].rearrange("p (m c n) -> p m c n", m=4, c=2)
        raw_r1 = k[:, 0, :].rearrange("p (c n) -> p c n", c=2)
        raw_e = arena[:, IMG * PATCH:].rearrange("p (e m c n) -> p e m c n", e=E, m=3, c=2)
        raw_b = k[:, 1, 0:24]
        raw_b3 = kv[:, 0:E, :]
        filler = xh[:].rearrange("p a b c -> p (a b c)").bitcast(F32)[:, 0:4 * ROW].rearrange("p (j w) -> p j w", j=4)
        zrow = h2[:].rearrange("p a b -> p (a b)")
        pack = [h[:, 0].rearrange("p a b -> p (a b)")[:, 0:EW], h[:, 1].rearrange("p a b -> p (a b)")[:, 0:EW],
                row[:].rearrange("p a b -> p (a b)")[:, 0:EW],
                xl[:].rearrange("p a b c -> p (a b c)").bitcast(F32)[:, 0:EW]]
        place_of = [0, 1, 2, 3, 1, 2]
        packm = [t[:, 0:1536].bitcast(F16).rearrange("p (m l c n) -> p m l c n", m=3, l=2, c=2) for t in pack]

        place = [0]

        def carve(words):
            place[0] += words
            assert place[0] <= 2 * IMG * PATCH
            return arena[:, place[0] - words:place[0]]

        def halves(t):
            return t.bitcast(F16).rearrange("p (l c s) -> p l c s", l=2, c=2)

        k_flat, kv_flat = k[:].rearrange("p a b -> p (a b)"), kv[:].rearrange("p a b -> p (a b)")

        packs_b = carve(E * EW).rearrange("p (e w) -> p e w", e=E)
        mats_b = arena[:, 0:E * EW].bitcast(F16).rearrange("p (e w) -> p e w", e=E)
        rows_b = [carve(4 * ROW).rearrange("p (j w) -> p j w", j=4) for _ in range(2)]
        bias_b = [carve(EW - EW_B) for _ in range(2)]
        yt_b = halves(carve(2 * BT))
        hid = [carve(2 * BT).rearrange("p (f s) -> p f s", f=2) for _ in range(2)]
        hid_b = [halves(k_flat[:, i * 2 * BT:(i + 1) * 2 * BT]) for i in range(2)]
        o_b = carve(4 * D).rearrange("p (j w) -> p j w", j=4)
        og_b = [kv_flat[:, i * 4 * D:(i + 1) * 4 * D].rearrange("p (j w) -> p j w", j=4) for i in range(2)]
        gs_in = [carve(4) for _ in range(2)]
        num_in = [carve(4) for _ in range(2)]
        num_b = [carve(4) for _ in range(2)]
        gs_b = [carve(4) for _ in range(2)]
        bt_bank = b_tok
        hid_bank = [[b_tr, b_rt], [b_w, b_s]]
        o_bank = b_proj

        half_tiles = (btiles + 1) // 2
        last_tile = ((btiles - 1) // 2, (btiles - 1) % 2)
        rows_in = [sig(f"rows_in{j}", 1, 16) for j in range(2)]
        packs_in = sem("packages_in")
        bias_ready = [sig(f"bias_ready{j}", 1) for j in range(2)]
        gs_got = [sig(f"gs_got{j}", 1) for j in range(2)]
        num_got = [sig(f"num_got{j}", 1) for j in range(2)]
        num_ready = [sig(f"num_ready{j}", 1) for j in range(2)]
        bt_done = [sig(f"bt_done{j}", 1) for j in range(2)]
        yth_ready = [sig(f"yth_ready{j}", 1) for j in range(2)]
        ytl_ready = [sig(f"ytl_ready{j}", 1) for j in range(2)]
        hid_done = [[sig(f"hid{m}_done{j}", 2) for j in range(2)] for m in range(2)]
        hid_ready = [[sig(f"hid{m}_ready{j}", 2) for j in range(2)] for m in range(2)]
        hidh_ready = [[sig(f"hid{m}h_ready{j}", 2) for j in range(2)] for m in range(2)]
        hidl_ready = [[sig(f"hid{m}l_ready{j}", 2) for j in range(2)] for m in range(2)]
        o_done = [sig(f"o_done{j}", 2) for j in range(2)]
        o_ready = [sig(f"o_ready{j}", 2) for j in range(2)]
        gs_ready = [sig(f"gs_ready{j}", 1) for j in range(2)]
        og_ready = [sig(f"og_ready{j}", 4) for j in range(2)]
        adds_out = [sig(f"adds_out{j}", 4, 16) for j in range(2)]
        table_ready = sem("table_ready")
        tails_out = sem("tails_out")
        table_link = sem("table_link")

        def tile_loop(eng, body):
            body(0)
            rounds = (half_tiles - 2) // 3
            with eng.Fori(0, rounds) as i:
                for u in range(3):
                    body(i * 3 + u + 1)
            for i in range(3 * rounds + 1, half_tiles):
                body(i)

        def before_tile(i, j):
            return (i, 0) if j else (i - 1, 1)

        def tile_after(i, j):
            if isinstance(i, int) and (i, j) == last_tile:
                return None
            return (i + 1, 0) if j else (i, 1)

        def tiles_of(i):
            return range(1 if isinstance(i, int) and (i, 0) == last_tile else 2)

        def exists(i):
            return not isinstance(i, int) or 0 <= i < half_tiles

        def last_of(j):
            return last_tile[0] - (j > last_tile[1])

        def entry(eng, what, i, j):
            n = 2 * i + j
            return eng.value_load(table[0:1, what, n:n + 1] if isinstance(i, int) else
                                  table[0:1, what, bass.ds(n, 1)], min_val=0, max_val=E - 1 if what else dummy)

        def stage_b_sync(sp):
            sp.wait_ge(table_ready, 2)
            sp.wait_ge(dump_out, 32)
            for e in range(E):
                at = sp.value_load(tails[0:1, e:e + 1], min_val=0, max_val=dummy)
                sp.dma_start(lists[bass.ds(at, BT)], lists[dummy:dummy + BT]).then_inc(tails_out, 16)
            sp.wait_ge(tails_out, 16 * E)
            wait(sp, scat, pairs - 1)

            def body(i):
                for j in tiles_of(i):
                    at = entry(sp, 0, i, j)
                    wait(sp, bt_done[j], i - 1)
                    wait(sp, num_got[j], i - 1)
                    sp.dma_start(rows_b[j], lists[bass.ds(at, BT)].rearrange("(j p) w -> p j w", p=P)).then_inc(
                        rows_in[j].sem, 16)

            tile_loop(sp, body)
            for j in range(2):
                wait(sp, adds_out[j], last_of(j))

        def stage_b_tensor(pe):
            mm = nc.tensor.matmul

            def transposes(i, j):
                wait(pe, rows_in[j], i)
                a, b = before_tile(i, j)
                wait(pe, yth_ready[b], a)
                wait(pe, ytl_ready[b], a)
                for l in range(2):
                    dst = bt_bank[l][:].bitcast(F16)
                    for c in range(2):
                        for t in range(4):
                            src = rows_b[j][:, t, l * P:(l + 1) * P].bitcast(F16)[:, c * P:(c + 1) * P]
                            last = nc.tensor.transpose(dst[:, c * BT + t * P:c * BT + (t + 1) * P], src, id16[:])
                last.then_inc(bt_done[j].sem, 1)

            def matrix(e, m, lw, c, first, n):
                first += ((m * 2 + lw) * 2 + c) * D
                return mats_b[:, bass.ds(e, 1), first:first + n].rearrange("p o n -> p (o n)")

            def hidden(m, i, j, e):
                a, b = before_tile(i, j)
                if m == 0:
                    wait(pe, yth_ready[j], i)
                    wait(pe, ytl_ready[j], i)
                    src = yt_b
                else:
                    wait(pe, hidh_ready[0][j], i)
                    wait(pe, hidl_ready[0][j], i)
                    src = hid_b[0]
                for f in range(2):
                    wait(pe, hid_ready[m][b], a, f)
                    parts = [(matrix(e, m, lw, c, f * P, P), src[:, lx, c, :]) for c in range(2)
                             for lx, lw in ((0, 0), (0, 1), (1, 0))]
                    for n, (l, r) in enumerate(parts):
                        last = mm(hid_bank[m][f][:], l, r, start=(n == 0), stop=(n == 5))
                    last.then_inc(hid_done[m][j].sem, 1)

            def output(i, j, e):
                a, b = before_tile(i, j)
                wait(pe, hidh_ready[1][j], i)
                wait(pe, hidl_ready[1][j], i)
                for u in range(2):
                    wait(pe, o_ready[b], a, u)
                    for t in (2 * u, 2 * u + 1):
                        parts = [(hid_b[1][:, lx, c, t * P:(t + 1) * P], matrix(e, 2, lw, c, 0, D)) for c in range(2)
                                 for lx, lw in ((0, 0), (0, 1), (1, 0))]
                        dst = o_bank[u][:, (t % 2) * D:(t % 2 + 1) * D]
                        for n, (l, r) in enumerate(parts):
                            last = mm(dst, l, r, start=(n == 0), stop=(n == 5))
                    last.then_inc(o_done[j].sem, 1)

            def body(i):
                expert = [entry(pe, 1, i, j) for j in tiles_of(i)]
                last = entry(pe, 1, i - 1, 1) if exists(i - 1) else None
                for j in tiles_of(i):
                    a, b = before_tile(i, j)
                    hidden(0, i, j, expert[j])
                    if tile_after(i, j):
                        transposes(*tile_after(i, j))
                    if exists(a):
                        output(a, b, expert[0] if j else last)
                    hidden(1, i, j, expert[j])

            wait(pe, pos_ready, pairs - 1)
            wait(pe, rw_ready, pairs - 1)
            wait(pe, h2_ready, pairs - 1)
            pe.wait_ge(table_ready, 2)
            pe.wait_ge(packs_in, 16 * E)
            transposes(0, 0)
            tile_loop(pe, body)
            output(*last_tile, entry(pe, 1, *last_tile))

        def stage_b_scalar(act):
            f_ = nc.scalar.activation

            def copy_high(i, j):
                wait(act, bt_done[j], i)
                a, b = before_tile(i, j)
                wait(act, hid_done[0][b], a)
                f_(yt_b[:, 0], bt_bank[0][:].bitcast(F16).rearrange("p (c s) -> p c s", c=2),
                   ACT.Copy).then_inc(yth_ready[j].sem, 1)

            def relu(m, i, j):
                a, b = before_tile(i, j)
                wait(act, bias_ready[j], i)
                for f in range(2):
                    wait(act, hid_done[m][j], i, f)
                    wait(act, hidl_ready[m][b], a, f)
                    f_(hid[m][:, f, :], hid_bank[m][f][:], ACT.Relu, scale=col(un, 5 + m),
                       bias=bias_b[j][:, 2 * m + f:2 * m + f + 1]).then_inc(hid_ready[m][j].sem, 1)

            def weighted(i, j):
                wait(act, gs_ready[j], i)
                wait(act, adds_out[j], i - 1)
                for t in range(4):
                    wait(act, o_ready[j], i, t // 2)
                    f_(og_b[j][:, t, :], o_b[:, t, :], ACT.Copy, scale=gs_b[j][:, t:t + 1]).then_inc(
                        og_ready[j].sem, 1)

            def body(i):
                for j in tiles_of(i):
                    a, b = before_tile(i, j)
                    relu(0, i, j)
                    if tile_after(i, j):
                        copy_high(*tile_after(i, j))
                    relu(1, i, j)
                    if exists(a):
                        weighted(a, b)

            wait(act, wkv_done, pairs - 1)
            copy_high(0, 0)
            tile_loop(act, body)
            weighted(*last_tile)

        def stage_b_vector(dve):
            v = nc.vector
            count = [0]

            def link(ins):
                ins.then_inc(table_link, 1)
                count[0] += 1
                dve.wait_ge(table_link, count[0])

            v.tensor_copy(tails[:], base[0:1, :])
            link(v.tensor_tensor(cnt[:], base[:], rbase[:], ALU.subtract))
            link(v.tensor_scalar(cnt[:], cnt[:], float(BT - 1), None, ALU.add))
            link(v.tensor_copy(nti[:], cnt[:]))
            link(v.tensor_scalar(nti[:], nti[:], BT.bit_length() - 1, None, ALU.arith_shift_right))
            link(v.tensor_copy(ntf[:], nti[:]))
            link(v.memset(cum[:, 0:1], 0.0))
            for e in range(E):
                link(v.tensor_tensor(cum[:, e + 1:e + 2], cum[:, e:e + 1], ntf[:, e:e + 1], ALU.add))
            link(v.tensor_scalar(cnt[:], ntf[:], -float(BT), float(region), ALU.mult, ALU.add))
            v.memset(texp[:], 0.0)
            link(v.tensor_scalar(toff[:], tk[:], float(BT), None, ALU.mult))
            for e in range(E - 1):
                link(v.tensor_scalar(tge[:], tk[:], cum[0:1, e + 1:e + 2], None, ALU.is_ge))
                v.tensor_tensor(texp[:], texp[:], tge[:], ALU.add)
                link(v.scalar_tensor_tensor(toff[:], tge[:], cnt[0:1, e:e + 1], toff[:], ALU.mult, ALU.add))
            link(v.tensor_scalar(tge[:], tk[:], cum[0:1, E:E + 1], None, ALU.is_ge))
            link(v.tensor_scalar(tk[:], toff[:], -1.0, float(dummy), ALU.mult, ALU.add))
            link(v.tensor_tensor(tk[:], tk[:], tge[:], ALU.mult))
            link(v.tensor_tensor(toff[:], toff[:], tk[:], ALU.add))
            v.tensor_copy(table[:, 1, :], texp[:]).then_inc(table_ready, 1)
            v.tensor_copy(table[:, 0, :], toff[:]).then_inc(table_ready, 1)

            def copy_low(i, j):
                wait(dve, bt_done[j], i)
                a, b = before_tile(i, j)
                wait(dve, hid_done[0][b], a)
                v.tensor_copy(yt_b[:, 1], bt_bank[1][:].bitcast(F16).rearrange("p (c s) -> p c s", c=2)).then_inc(
                    ytl_ready[j].sem, 1)

            def biases(i, j, e):
                wait(dve, hid_ready[1][j], i - 1)
                wait(dve, o_ready[j], i - 1)
                v.tensor_copy(bias_b[j], packs_b[:, bass.ds(e, 1), EW_B:EW].rearrange("p o w -> p (o w)")).then_inc(
                    bias_ready[j].sem, 1)

            def gates(i, j, e):
                wait(dve, rows_in[j], i)
                wait(dve, num_ready[j], i - 1)
                v.tensor_copy(gs_in[j], rows_b[j][:, :, bass.ds(e + D, 1)].rearrange("p j o -> p (j o)")).then_inc(
                    gs_got[j].sem, 1)
                v.tensor_copy(num_in[j].bitcast(U32), rows_b[j][:, :, D + E].bitcast(U32)).then_inc(
                    num_got[j].sem, 1)

            def keep_gates(i, j):
                wait(dve, gs_got[j], i)
                wait(dve, adds_out[j], i - 1)
                v.tensor_copy(gs_b[j], gs_in[j]).then_inc(gs_ready[j].sem, 1)
                wait(dve, num_got[j], i)
                v.tensor_copy(num_b[j].bitcast(U32), num_in[j].bitcast(U32)).then_inc(num_ready[j].sem, 1)

            def split(m, i, j):
                a, b = before_tile(i, j)
                for f in range(2):
                    wait(dve, hid_ready[m][j], i, f)
                    if m == 0:
                        wait(dve, hid_done[1][b], a)
                    else:
                        wait(dve, o_done[b], a)
                    v.tensor_copy(hid_b[m][:, 0, f, :], hid[m][:, f, :]).then_inc(hidh_ready[m][j].sem, 1)
                    wait(dve, hidh_ready[m][j], i, f)
                    v.tensor_tensor(hid_b[m][:, 1, f, :], hid[m][:, f, :], hid_b[m][:, 0, f, :],
                                    ALU.subtract).then_inc(hidl_ready[m][j].sem, 1)

            def out_bias(i, j):
                a, b = before_tile(i, j)
                for u in range(2):
                    wait(dve, o_done[j], i, u)
                    wait(dve, og_ready[b], a, 2 * u + 1)
                    b3 = bias_b[j][:, EW_B3 - EW_B:].unsqueeze(1).to_broadcast([P, 2, D])
                    v.scalar_tensor_tensor(o_b[:, 2 * u:2 * u + 2, :],
                                           o_bank[u][:].rearrange("p (t w) -> p t w", t=2), col(un, 7), b3,
                                           ALU.mult, ALU.add).then_inc(o_ready[j].sem, 1)

            def body(i):
                expert = [entry(dve, 1, i, j) for j in tiles_of(i)]
                if tile_after(i, 1) and len(expert) == 2:
                    expert.append(entry(dve, 1, i + 1, 0))
                for j in tiles_of(i):
                    a, b = before_tile(i, j)
                    split(0, i, j)
                    gates(i, j, expert[j])
                    if tile_after(i, j):
                        copy_low(*tile_after(i, j))
                    if exists(a):
                        out_bias(a, b)
                    if tile_after(i, j):
                        biases(*tile_after(i, j), expert[j + 1])
                    keep_gates(i, j)
                    split(1, i, j)

            wait(dve, sum_done, pairs - 1)
            dve.wait_ge(table_ready, 2)
            dve.sem_inc(dve_hold, 1)
            first = entry(dve, 1, 0, 0)
            dve.wait_ge(packs_in, 16 * E)
            biases(0, 0, first)
            copy_low(0, 0)
            tile_loop(dve, body)
            out_bias(*last_tile)

        def stage_b_pool(pool):
            for s in h2_out:
                wait(pool, s, pairs - 1)
            pool.wait_ge(dump_out, 32)

            def body(i):
                for j in tiles_of(i):
                    a, b = before_tile(i, j)
                    wait(pool, num_ready[j], i)
                    wait(pool, adds_out[b], a)
                    for t in range(4):
                        hold(pool, pool_hold, og_ready[j], i, t)
                        nc.gpsimd.indirect_dma_start(
                            out, bass.IndirectOffsetOnAxis(ap=num_b[j][:, t:t + 1].bitcast(U32), axis=0),
                            og_b[j][:, t, :], None, compute_op=ALU.add).then_inc(adds_out[j].sem, 16)

            tile_loop(pool, body)

        block = ctx.enter_context(nc.Block())

        def group_slot(g):
            return slice(g % 2 * GROUP, (g % 2 + 1) * GROUP)

        def at(g, c, first):
            if g == 1:
                return y1t[:, c, :].rearrange("p (a s) -> p a s", a=2)[:, :, first:first + 192]
            return y1t[:, c, first:first + GROUP]

        def out_of(g, t):
            return t.rearrange("p (a s) -> p a s", a=2) if g == 1 else t

        def rows_of(image):
            if image == 0:
                return [(t, 0, P, P * t) for t in range(4)] + [(4, 0, 64, 512)]
            return [(4, 64, 64, 0)] + [(5 + t, 0, P, 64 + P * t) for t in range(4)]

        def block_of(n):
            return n // 4, (n // 2) % 2, n % 2

        def pieces(n):
            image, half, _ = block_of(n)
            a, b = half * HALF, (half + 1) * HALF
            got = []
            for i, (_, _, size, t0) in enumerate(rows_of(image)):
                lo, hi = max(a, t0), min(b, t0 + size)
                if lo < hi:
                    got.append((i, lo - a, hi - a))
            return got

        def carries_of(n):
            return sum(1 + (m // 2) % 2 for m in range(n))

        def block_cols(n):
            image, half, _ = block_of(n)
            return slice(image * IMG + half * HALF, image * IMG + (half + 1) * HALF)

        @block.sync
        def _(sp):
            def load_image(q, half):
                img = x[2 * q + half] if isinstance(q, int) else x[bass.ds(2 * q + half, 1)].rearrange(
                    "o c h w -> (o c) h w")
                v = img.rearrange("c (n r) w -> c r n w", r=PATCH)
                for g in range(2):
                    for c in range(CH):
                        part = (g * CH + c) * PATCH
                        dst = arena[part:part + PATCH, half * IMG * PATCH:(half + 1) * IMG * PATCH]
                        dst = dst.rearrange("p (n w) -> p n w", n=SIDE)[:, :, 0:SIDE * PATCH - QS * g]
                        sp.dma_start(dst, v[c][:, :, QS * g:]).then_inc(x_in[half].sem, 16)

            sp.dma_start(embed_w[0:KP], tok_w).then_inc(ld, 16)
            sp.dma_start(embed_w[KP:KP + 1, 0, :], tok_b).then_inc(ld, 16)
            for i, w in enumerate((wk, wv, wr, wo)):
                sp.dma_start(raw_w[:, i], w.rearrange("(c p) n -> p c n", c=2)).then_inc(ld, 16)
            sp.dma_start(raw_r1, rw1.rearrange("(c p) n -> p c n", c=2)).then_inc(ld, 16)
            sp.dma_start(rw2s[:], rw2).then_inc(ld, 16)
            sp.dma_start(rb1s[:], rb1).then_inc(ld, 16)
            sp.dma_start(rb2s[:], rb2).then_inc(ld, 16)
            sp.dma_start(mixs[:], mix).then_inc(ld, 16)
            sp.dma_start(zrow[:, 128:768], decay).then_inc(ld, 16)
            for i, w in enumerate((ew1, ew2, ew3)):
                for e in range(E):
                    sp.dma_start(raw_e[:, e, i], w[e].rearrange("(c p) n -> p c n", c=2)).then_inc(ld_m[i], 16)
            sp.dma_start(raw_b[:, 0:12], eb1).then_inc(ld_e, 16)
            sp.dma_start(raw_b[:, 12:24], eb2).then_inc(ld_e, 16)
            sp.dma_start(raw_b3, eb3).then_inc(ld_e, 16)
            load_image(0, 0)
            sp.wait_ge(ld, 16 * 12)
            sp.wait_ge(setup_v, 1)
            sp.dma_start(skew.rearrange("(p s) -> p s", s=800)[:, 0:768], zrow).then_inc(skew_out, 16)
            sp.wait_ge(skew_out, 16)
            sp.dma_start(dec[:], skew[0:P * 799].rearrange("(p s) -> p s", s=799)[:, 128:768]).then_inc(dec_in, 16)
            for e in range(E):
                sp.wait_ge(pk_ready, e + 1)
                sp.wait_ge(pkh_ready, 4 * (e + 1))
                sp.dma_start(packs[e], pack[place_of[e]]).then_inc(pk_out[place_of[e]], 16)
            sp.wait_ge(setup_v, 4)
            sp.wait_ge(setup_p, 5)
            sp.dma_start(lists[dummy:dummy + BT].rearrange("(j p) w -> p j w", p=P), filler[:]).then_inc(dump_out, 16)
            sp.dma_start(out[tokens:tokens + BT].rearrange("(j p) w -> p j w", p=P),
                         filler[:, :, 0:D]).then_inc(dump_out, 16)
            load_image(0, 1)

            outv = out[0:tokens].rearrange("(q t p) w -> q t p w", t=TILES, p=P)

            def body(p):
                for name, n, q in steps(p, pairs):
                    more = not isinstance(q, int) or q + 1 < pairs
                    if name == "embed" and n == 4 and more:
                        wait(sp, tok_done, q, 4)
                        load_image(q + 1, 0)
                    if name == "embed" and n == 8 and more:
                        wait(sp, tok_done, q, 8)
                        load_image(q + 1, 1)
                    if name == "embed" and n == 8 and not more:
                        wait(sp, tok_done, q, 8)
                        for i in range(4):
                            sp.wait_ge(pk_out[i], 16 * place_of.count(i))
                        for e in range(E):
                            sp.dma_start(packs_b[:, e, :], packs[e]).then_inc(packs_in, 16)
                    if base_name(name) == "project":
                        wait(sp, h2_ready, q, n)
                        dst = outv[q, n] if isinstance(q, int) else outv[bass.ds(q, 1), n].rearrange(
                            "o p w -> (o p) w")
                        sp.dma_start(dst, h2[:, n % 3, :]).then_inc(h2_out[n % 3].sem, 16)

            iterations(sp, body, pairs, last=2)
            for s in h2_out:
                wait(sp, s, pairs - 1)
            stage_b_sync(sp)

        @block.tensor
        def _(pe):
            mm = nc.tensor.matmul

            def embed(q, t):
                wait(pe, x_in[0 if t < 4 else 1], q)
                if t == 4:
                    wait(pe, x_in[0], q)
                    if first_time(q):
                        pe.wait_ge(ones_ready, 2)
                bank_ = b_tok[t % 2]
                if t >= 2:
                    wait(pe, h_ready, q, t - 2)
                else:
                    wait(pe, h_ready, q - 1, 7 if t else 8)
                for j in range(QS):
                    a = t * P * PATCH + j
                    rows = KP + (j == 0)
                    last = mm(bank_[:, 0:D], arena[0:rows, a:a + (P - 1) * PATCH + 1:PATCH], embed_w[0:rows, j, :],
                              start=(j == 0), stop=(j == QS - 1))
                last.then_inc(tok_done.sem, 1)

            def transpose(q, t):
                if first_time(q) and t == 0:
                    pe.wait_ge(setup_p, 6)
                wait(pe, y1_ready, q, t)
                wait(pe, y1t_ready, q if t else q - 1, t - 1 if t else None)
                for c in range(2):
                    last = nc.tensor.transpose(b_tr[:, c * P:(c + 1) * P], y1[:, t % 3, c * P:(c + 1) * P], id32[:])
                last.then_inc(tr_done.sem, 1)

            def split_product(dst, parts):
                for i, (l, r) in enumerate(parts):
                    last = mm(dst, l, r, start=(i == 0), stop=(i == len(parts) - 1))
                return last

            def keys_values(q, t):
                g = t // 3
                if t % 3 == 0:
                    wait(pe, xh_ready, q, 3 * g + 1)
                    wait(pe, xl_ready, q, g)
                    wait(pe, xl_pool, q, 2 * g)
                dst = b_proj[t % 2]
                if t >= 2:
                    wait(pe, kv_ready, q, t - 2)
                else:
                    wait(pe, h2_ready, q - 1, 7 + t)
                s = slice(g % 2 * GROUP + t % 3 * P, g % 2 * GROUP + (t % 3 + 1) * P)
                for i in range(2):
                    parts = [(a[:, i, c, s], w[:, i, c, :]) for c in range(2)
                             for a, w in ((xh, wh), (xh, wl), (xl, wh))]
                    last = split_product(dst[:, i * D:(i + 1) * D], parts)
                last.then_inc(kv_done.sem, 1)

            def receptance(q, n):
                g, f = n // 2, n % 2
                if first_time(q) and n == 0:
                    pe.wait_ge(split_ready, 5)
                    pe.wait_ge(setup_v, 4)
                    pe.wait_ge(dec_in, 16)
                if f == 0:
                    wait(pe, xh_ready, q, 3 * g + 2)
                    wait(pe, xl_pool, q, 2 * g + 1)
                dst = (b_w, b_s)[f]
                if g:
                    wait(pe, rc_ready, q, n - 2)
                else:
                    wait(pe, rw_ready if f == 0 else den_ready, q - 1)
                s = group_slot(g)
                parts = [(w[:, 2, c, f * P:(f + 1) * P], a[:, 2, c, s]) for c in range(2)
                         for a, w in ((xh, wh), (xh, wl), (xl, wh))]
                split_product(dst[:, 0:GROUP], parts).then_inc(r_done.sem, 1)

            def sums(q, n):
                image, half, f = block_of(n)
                rows = rows_of(image)
                a = half * HALF
                fs = slice(f * P, (f + 1) * P)
                mine = pieces(n)
                wait(pe, kv_ready, q, rows[mine[-1][0]][0])
                if n:
                    wait(pe, den_ready, q, n - 1)
                else:
                    wait(pe, rc_ready, q, 5)
                for i, lo, hi in mine:
                    t, p0, size, t0 = rows[i]
                    s0 = a + lo - t0 + p0
                    last = mm(b_s[:, lo:hi], k[p0:p0 + size, t, fs], upto[p0:p0 + size, s0:s0 + hi - lo],
                              start=True, stop=True)
                last.then_inc(sum_done.sem, 1)

            def decayed(q, n):
                image, half, f = block_of(n)
                rows = rows_of(image)
                a = half * HALF
                fs = slice(f * P, (f + 1) * P)
                top = max(i for i, _, _ in pieces(n))
                wait(pe, kv_ready, q, rows[top][0])
                if n:
                    wait(pe, rw_ready, q, n - 1)
                else:
                    wait(pe, rc_ready, q, 4)
                for i in range(top + 1):
                    t, p0, size, t0 = rows[i]
                    lo = max(t0 - a, 0)
                    s0 = a + lo - t0 + p0
                    last = mm(b_w[:, lo:HALF], kv[p0:p0 + size, t, fs], dec[p0:p0 + size, s0:s0 + HALF - lo],
                              start=(i == 0), stop=(i == top))
                last.then_inc(wkv_done.sem, 1)

            def project(q, t):
                b = (P * t + P - 1) // HALF
                wait(pe, rwh_ready, q, 2 * b + 1)
                wait(pe, rwl_ready, q, 2 * b + 1)
                dst = b_proj[(TILES + t) % 2]
                if t >= 2:
                    wait(pe, h2_ready, q, t - 2)
                else:
                    wait(pe, kv_ready, q, 7 + t)
                s = slice(t * P, (t + 1) * P)
                parts = [(r[:, c, s], w[:, 3, c, :]) for c in range(2) for r, w in ((rwh, wh), (rwh, wl), (rwl, wh))]
                split_product(dst[:, 0:D], parts).then_inc(wo_done.sem, 1)

            def route_transpose(q, t):
                wait(pe, yh_ready, q, t)
                wait(pe, yl_ready, q, t)
                if t % 3:
                    wait(pe, y2t_ready, q, t - 1)
                elif t:
                    wait(pe, lg_ready, q, t // 3 - 1)
                else:
                    wait(pe, pos_ready, q - 1)
                src = row[:, t, 0:D].bitcast(F16)
                dst = b_rt[:, 0:D].bitcast(F16)
                for i in range(4):
                    last = nc.tensor.transpose(dst[:, i * P:(i + 1) * P], src[:, i * P:(i + 1) * P], id16[:])
                last.then_inc(rtt_done.sem, 1)

            def router(q, g):
                wait(pe, y2t_ready, q, 3 * g + 2)
                parts = [(rwa[:, lw, c, :], y2t[:, 2 * lx + c, :]) for c in range(2)
                         for lx, lw in ((0, 0), (0, 1), (1, 0))]
                split_product(b_rt[:, 0:GROUP], parts).then_inc(rh_done.sem, 1)

            def logits(q, g):
                wait(pe, rh_ready, q, g)
                for j in range(3):
                    last = mm(b_rt[:, j * E:(j + 1) * E], rh[:, j * P:(j + 1) * P], rw2s[:], start=True, stop=True)
                last.then_inc(lg_done.sem, 1)

            def rank(q, _):
                wait(pe, sel_ready, q)
                wait(pe, lg_ready, q, 2)
                n = TILES * E
                mm(b_rt[:, 0:n + E], before[:], sel16[:].rearrange("p t e -> p (t e)"), start=True, stop=False)
                for t in range(TILES):
                    dst = b_rt[:, (t + 1) * E:n + E].rearrange("p (t e) -> p t e", e=E)
                    last = mm(dst, ones16[:], sel16[:, t:t + 1, :].to_broadcast([P, TILES - t, E]), start=False,
                              stop=(t == TILES - 1))
                last.then_inc(rank_done.sem, 1)

            def body(p):
                for name, n, q in steps(p, pairs):
                    if base_name(name) in do:
                        do[base_name(name)](q, n)

            do = {"embed": embed, "transpose": transpose, "values": keys_values, "receptance": receptance,
                  "sums": sums, "decayed": decayed, "project": project, "route_transpose": route_transpose,
                  "router": router, "logits": logits, "rank": rank}
            pe.wait_ge(ld, 16 * 12)
            pe.wait_ge(ones_ready, 1)
            iterations(pe, body, pairs)
            stage_b_tensor(pe)

        @block.scalar
        def _(act):
            f = nc.scalar.activation

            def embedded(q, t):
                wait(act, tok_done, q, t)
                if t in (0, 6):
                    wait(act, h2_ready, q - 2, 8 if t else 5)
                f(h[:, q % 2, t, :], b_tok[t % 2][:, 0:D], ACT.Copy).then_inc(h_ready.sem, 1)

            def norm1(q, t):
                wait(act, tr_done, *tile_before(q, t, 3))
                hold(act, act_hold, rs1_ready, q, t // 3)
                f(y1[:, t % 3, :], h[:, q % 2, t, :], ACT.Identity, scale=rs1[:, t % 3:t % 3 + 1],
                  bias=nm1[:, t % 3:t % 3 + 1]).then_inc(y1_ready.sem, 1)

            def norm2(q, t):
                wait(act, rs2_ready, q, t // 3)
                wait(act, yh_ready, *tile_before(q, t, 3))
                wait(act, yl_ready, *tile_before(q, t, 3))
                f(y2[:, t % 3, :], h2[:, t % 3, :], ACT.Identity, scale=rs2[:, t % 3:t % 3 + 1],
                  bias=nm2[:, t % 3:t % 3 + 1]).then_inc(y2_ready.sem, 1)

            def transposed(q, t):
                n = t // 3
                wait(act, tr_done, q, t)
                if t % 3 == 0:
                    wait(act, diff_ready, q if n else q - 1, n - 1 if n else None)
                    wait(act, xf_ready, q if n else q - 1, 3 * n - 1 if n else None)
                    if n == 0:
                        f(y1t[:, :, 0], zero2[:], ACT.Copy)
                    else:
                        f(y1t[:, :, 0], y1t[:, :, 384 + (n == 2)], ACT.Copy)
                        if n == 1:
                            f(y1t[:, :, 193], zero2[:], ACT.Copy)
                src = b_tr[:, 0:D].rearrange("p (c s) -> p c s", c=2)
                a = 1 + (t % 3) * P
                if t == 4:
                    f(y1t[:, :, a:a + 64], src[:, :, 0:64], ACT.Copy)
                    f(y1t[:, :, a + 65:a + 129], src[:, :, 64:128], ACT.Copy).then_inc(y1t_ready.sem, 1)
                else:
                    a += t == 5
                    f(y1t[:, :, a:a + P], src, ACT.Copy).then_inc(y1t_ready.sem, 1)

            def mixed_high(q, m):
                if first_time(q) and m == 0:
                    for i in range(4):
                        act.wait_ge(pk_out[i], 16 * place_of.count(i))
                    act.wait_ge(dump_out, 32)
                n, i = m // 3, m % 3
                old, pair = (0, q) if n == 2 else (2 - n, q - 1)
                wait(act, xf_ready, q, m)
                wait(act, kv_done if i < 2 else r_done, pair, 3 * old + 2 if i < 2 else 2 * old + 1)
                f(xh[:, i, :, group_slot(n)], xf[:, m % 2], ACT.Copy).then_inc(xh_ready.sem, 1)

            def exp_keys(q, t):
                wait(act, kc_ready, q, t)
                f(k[:, t, :], k[:, t, :], ACT.Exp, scale=col(un, 0)).then_inc(k_ready.sem, 1)

            def part_of_gate(n):
                return gate[:, n % 2, n // 2 * GROUP:(n // 2 + 1) * GROUP]

            def exp_receptance(q, n):
                wait(act, rc_ready, q, n)
                f(part_of_gate(n), part_of_gate(n), ACT.Exp, scale=col(un, 2)).then_inc(e_ready.sem, 1)

            def one_plus(q, n):
                wait(act, e_ready, q, n)
                f(part_of_gate(n), part_of_gate(n), ACT.Copy, bias=1.0).then_inc(gate_ready.sem, 1)

            def weighed_high(q, n):
                wait(act, rw_ready, q, n)
                if n == 0:
                    wait(act, wo_done, q - 1)
                f(rwh[:, block_of(n)[2], block_cols(n)], gate[:, block_of(n)[2], block_cols(n)],
                  ACT.Copy).then_inc(rwh_ready.sem, 1)

            def norm2_high(q, t):
                wait(act, y2_ready, q, t)
                if t == 0:
                    wait(act, scat, q - 1)
                f(row[:, t, 0:P].bitcast(F16), y2[:, t % 3, :], ACT.Copy).then_inc(yh_ready.sem, 1)

            def route_transposed(q, n):
                wait(act, rtt_done, q, n)
                if n % 3 == 0:
                    wait(act, rh_done, q if n else q - 1, n // 3 - 1 if n else None)
                src = b_rt[:, 0:D].bitcast(F16).rearrange("p (i s) -> p i s", i=4)
                f(y2t[:, :, (n % 3) * P:(n % 3 + 1) * P], src, ACT.Copy).then_inc(y2t_ready.sem, 1)

            def router_relu(q, n):
                wait(act, rh_done, q, n)
                wait(act, lg_done, q if n else q - 1, n - 1 if n else None)
                f(rh[:], b_rt[:, 0:GROUP], ACT.Relu, bias=rb1s[:], scale=col(un, 4)).then_inc(rh_ready.sem, 1)

            def exp_logits(q, _):
                wait(act, d_ready, q)
                f(ex[:], t1[:], ACT.Exp).then_inc(ex_ready.sem, 1)

            def exp_second(q, _):
                wait(act, q_in, q)
                f(g2[:], g1[:], ACT.Exp).then_inc(q_ready.sem, 1)

            do = {"embedded": embedded, "norm1": norm1, "norm2": norm2, "transposed": transposed,
                  "mixed_high": mixed_high,
                  "exp_keys": exp_keys, "exp_receptance": exp_receptance,
                  "one_plus": one_plus, "weighed_high": weighed_high, "norm2_high": norm2_high,
                  "route_transposed": route_transposed, "router_relu": router_relu, "exp_logits": exp_logits,
                  "exp_second": exp_second}

            def body(p):
                for name, n, q in steps(p, pairs):
                    if base_name(name) in do:
                        do[base_name(name)](q, n)

            act.wait_ge(scales_ready, 1)
            for i, s in enumerate(("k", "v", "r", "o")):
                f(wh[:, i], raw_w[:, i], ACT.Copy, scale=col(sc, W_S[s])).then_inc(wsplit, 1)
            f(rwa[:, 0], raw_r1, ACT.Copy, scale=col(sc, 4)).then_inc(wsplit, 1)
            for e in range(E):
                at = place_of[e]
                if e >= 4:
                    act.wait_ge(pk_out[at], 16)
                for i in range(3):
                    f(packm[at][:, i, 0], raw_e[:, e, i], ACT.Copy, scale=col(sc, 5 + i)).then_inc(pkh_ready, 1)
                f(pack[at][:, EW_B:EW_B + 2], raw_b[:, 2 * e:2 * e + 2], ACT.Copy, scale=col(sc, S_H1))
                f(pack[at][:, EW_B + 2:EW_B + 4], raw_b[:, 12 + 2 * e:14 + 2 * e], ACT.Copy, scale=col(sc, S_H2))
                f(pack[at][:, EW_B3:EW_B3 + D], raw_b3[:, e, :], ACT.Copy).then_inc(pkh_ready, 1)
            act.wait_ge(pk_out[0], 16)
            iterations(act, body, pairs)
            stage_b_scalar(act)

        @block.vector
        def _(dve):
            v = nc.vector

            def stats1(q, t):
                wait(dve, mv1_ready, *tile_before(q, t, 3))
                hold(dve, dve_hold, h_ready, q, t)
                v.bn_stats(st[:, t % 3, :], h[:, q % 2, t, :]).then_inc(st1_ready.sem, 1)

            def mean1(q, t):
                wait(dve, rs1_ready, *group_before(q, t // 3))
                if t % 3 == 0:
                    wait(dve, ve1_ready, *group_before(q, t // 3))
                hold(dve, dve_hold, st1_ready, q, t)
                v.bn_aggr(mv1[:, t % 3, :], st[:, t % 3, :]).then_inc(mv1_ready.sem, 1)

            def variance1(q, g):
                wait(dve, mv1_ready, q, 3 * g + 2)
                wait(dve, rs1_ready, *group_before(q, g))
                v.tensor_scalar(ve1[:], mv1[:, :, 1], EPS, col(un, 9), ALU.add, ALU.mult).then_inc(ve1_ready.sem, 1)

            def mixed(q, n):
                g, i = n // 3, n % 3
                wait(dve, diff_ready, q, g)
                free_xf(q, n)
                for c in range(2):
                    last = v.scalar_tensor_tensor(out_of(g, xf[:, n % 2, c, :]), out_of(g, diff[:, c, :]),
                                                  mixs[:, i, c:c + 1], at(g, c, 0), ALU.mult, ALU.add)
                last.then_inc(xf_ready.sem, 1)

            def free_xf(q, n):
                m, pair = (n - 2, q) if n >= 2 else (8 - n, q - 1)
                wait(dve, xh_ready, pair, m)
                if m % 3 == 0:
                    wait(dve, xl_ready, pair, m // 3)
                else:
                    wait(dve, xl_pool, pair, 2 * (m // 3) + m % 3 - 1)

            def clip_keys(q, t):
                wait(dve, kv_done, q, t)
                if t == 0:
                    wait(dve, sum_done, q - 1)
                    wait(dve, kv_ready, q - 1)
                v.tensor_scalar(k[:, t, :], b_proj[t % 2][:, 0:D], col(un, 10), col(un, 11), ALU.max,
                                ALU.min).then_inc(kc_ready.sem, 1)

            def times_values(q, t):
                wait(dve, k_ready, q, t)
                if t == 0:
                    wait(dve, wkv_done, q - 1)
                v.scalar_tensor_tensor(kv[:, t, :], b_proj[t % 2][:, D:2 * D], col(un, 1), k[:, t, :], ALU.mult,
                                       ALU.mult).then_inc(kv_ready.sem, 1)

            def clip_receptance(q, n):
                g, i = n // 2, n % 2
                wait(dve, r_done, q, n)
                if n == 0:
                    wait(dve, rwl_ready, q - 1)
                v.tensor_scalar(gate[:, i, g * GROUP:(g + 1) * GROUP], (b_w, b_s)[i][:, 0:GROUP], col(un, 13), None,
                                ALU.max).then_inc(rc_ready.sem, 1)

            def denominators(q, n):
                image, half, f = block_of(n)
                wait(dve, sum_done, q, n)
                wait(dve, gate_ready, q, 5 if n >= 4 else 3)
                dst = gate[:, f, block_cols(n)]
                mine = pieces(n)
                wait(dve, den_ready, q if n else q - 1, n - 1 if n else None)
                ends = [hi for _, _, hi in mine]

                def total(j):
                    return b_s[:, ends[j] - 1:ends[j]]

                if half == 0:
                    v.tensor_reduce(carry[:, f, 0:1], b_s[:, ends[0] - 1:ends[1]:P], AX.X, ALU.add).then_inc(
                        carry_ready.sem, 1)
                    before_ = [None, total(0), carry[:, f, 0:1]]
                else:
                    wait(dve, carry_ready, q, carries_of(n) - 1)
                    v.tensor_tensor(carry[:, f, 1:2], total(0), carry[:, f, 0:1], ALU.add).then_inc(
                        carry_ready.sem, 1)
                    before_ = [carry[:, f, j:j + 1] for j in range(3)]
                for j, (i, lo, hi) in enumerate(mine):
                    if half and j == 1:
                        wait(dve, carry_ready, q, carries_of(n))
                        v.tensor_tensor(carry[:, f, 2:3], total(1), carry[:, f, 1:2], ALU.add).then_inc(
                            carry_ready.sem, 1)
                    if j == 2:
                        wait(dve, carry_ready, q, carries_of(n) + half)
                    if i == 0:
                        last = v.tensor_tensor(dst[:, lo:hi], b_s[:, lo:hi], dst[:, lo:hi], ALU.mult)
                    else:
                        last = v.scalar_tensor_tensor(dst[:, lo:hi], b_s[:, lo:hi], before_[j], dst[:, lo:hi],
                                                      ALU.add, ALU.mult)
                last.then_inc(den_ready.sem, 1)

            def invert(q, n):
                dst = gate[:, block_of(n)[2], block_cols(n)]
                wait(dve, den_ready, q, n)
                v.reciprocal(dst, dst).then_inc(inv_ready.sem, 1)

            def weigh(q, n):
                dst = gate[:, block_of(n)[2], block_cols(n)]
                wait(dve, wkv_done, q, n)
                wait(dve, inv_ready, q, n)
                v.scalar_tensor_tensor(dst, b_w[:, 0:HALF], col(sc, S_RW), dst, ALU.mult, ALU.mult).then_inc(
                    rw_ready.sem, 1)

            def residual(q, t):
                wait(dve, wo_done, q, t)
                if t >= 3:
                    wait(dve, h2_out[t % 3], q, t // 3 - 1)
                else:
                    wait(dve, h2_out[t % 3], q - 1)
                wait(dve, y2_ready, *tile_before(q, t, 3))
                dst = h2[:, t % 3, :]
                v.scalar_tensor_tensor(dst, b_proj[(TILES + t) % 2][:, 0:D], col(un, 3), h[:, q % 2, t, :], ALU.mult,
                                       ALU.add).then_inc(h2_ready.sem, 1)

            def stats2(q, t):
                wait(dve, mv2_ready, *tile_before(q, t, 3))
                hold(dve, dve_hold, h2_ready, q, t)
                v.bn_stats(st2[:, t % 3, :], h2[:, t % 3, :]).then_inc(st2_ready.sem, 1)

            def mean2(q, t):
                wait(dve, rs2_ready, *group_before(q, t // 3))
                if t % 3 == 0:
                    wait(dve, ve2_ready, *group_before(q, t // 3))
                hold(dve, dve_hold, st2_ready, q, t)
                v.bn_aggr(mv2[:, t % 3, :], st2[:, t % 3, :]).then_inc(mv2_ready.sem, 1)

            def variance2(q, g):
                wait(dve, mv2_ready, q, 3 * g + 2)
                wait(dve, rs2_ready, *group_before(q, g))
                v.tensor_scalar(ve2[:], mv2[:, :, 1], EPS, LN_SCALE ** -2, ALU.add, ALU.mult).then_inc(
                    ve2_ready.sem, 1)

            def logits(q, g):
                wait(dve, lg_done, q, g)
                if g == 0:
                    wait(dve, pos_ready, q - 1)
                v.tensor_tensor(lg[:, 3 * g:3 * g + 3, :], b_rt[:, 0:3 * E].rearrange("p (t e) -> p t e", e=E),
                                rb2s[:].unsqueeze(1).to_broadcast([P, 3, E]), ALU.add).then_inc(lg_ready.sem, 1)

            def wide(t):
                return t[:].to_broadcast([P, TILES, E])

            count = [0]

            def top_step(q, ins):
                ins.then_inc(top_link.sem, 1)
                wait(dve, top_link, q, count[0])
                count[0] += 1

            def top2(q, _):
                def link(ins):
                    top_step(q, ins)

                count[0] = 0
                wait(dve, lg_ready, q, 2)
                link(v.tensor_reduce(m1[:], lg[:], AX.X, ALU.max))
                link(v.tensor_tensor(t2[:], lg[:], wide(m1), ALU.subtract))
                v.tensor_scalar(t1[:], t2[:], -87.33654, None, ALU.max).then_inc(d_ready.sem, 1)
                wait(dve, d_ready, q)
                link(v.scalar_tensor_tensor(t2[:], t1[:], 0.0, rev[:], ALU.is_ge, ALU.mult))
                link(v.tensor_reduce(m2[:], t2[:], AX.X, ALU.max))
                link(v.tensor_tensor(oh1[:], t2[:], wide(m2), ALU.is_equal))
                link(v.scalar_tensor_tensor(t2[:], oh1[:], -1e30, t1[:], ALU.mult, ALU.add))
                link(v.tensor_reduce(m1[:], t2[:], AX.X, ALU.max))
                link(v.tensor_tensor(t2[:], t2[:], wide(m1), ALU.is_equal))
                link(v.tensor_tensor(t2[:], t2[:], rev[:], ALU.mult))
                link(v.tensor_reduce(m2[:], t2[:], AX.X, ALU.max))
                link(v.tensor_tensor(oh2[:], t2[:], wide(m2), ALU.is_equal))
                v.tensor_tensor(sel16[:, 0:TILES, :], oh1[:], oh2[:], ALU.add).then_inc(sel_ready.sem, 1)

            def second(q, _):
                def link(ins):
                    top_step(q, ins)

                wait(dve, ex_ready, q)
                link(v.tensor_reduce(m2[:], ex[:], AX.X, ALU.add))
                link(v.tensor_tensor(t2[:], ex[:], oh2[:], ALU.mult))
                link(v.tensor_reduce(g1[:], t2[:], AX.X, ALU.add))
                link(v.reciprocal(m2[:], m2[:]))
                v.scalar_tensor_tensor(g1[:], g1[:], -1.0, m2[:], ALU.add, ALU.mult).then_inc(q_in.sem, 1)

            def gates(q, _):
                def link(ins):
                    top_step(q, ins)

                wait(dve, q_ready, q)
                link(v.tensor_scalar(m1[:], g2[:], 1.0, None, ALU.add))
                link(v.reciprocal(m1[:], m1[:]))
                link(v.tensor_tensor(g2[:], g2[:], m1[:], ALU.mult))
                link(v.tensor_tensor(t2[:], oh1[:], wide(m1), ALU.mult))
                link(v.tensor_tensor(t1[:], oh2[:], wide(g2), ALU.mult))
                assert count[0] == TOP_LINKS, count
                v.tensor_tensor(row[:, :, D:D + E], t1[:], t2[:], ALU.add).then_inc(gw_ready.sem, 1)

            def positions(q, _):
                count = [0]

                def link(ins):
                    ins.then_inc(rank_link.sem, 1)
                    wait(dve, rank_link, q, count[0])
                    count[0] += 1

                link(v.tensor_copy(row[:, :, D + E:D + E + 1].bitcast(U32), idf[:].unsqueeze(2)))
                link(v.tensor_scalar(idf[:], idf[:], float(PAIR), None, ALU.add))
                wait(dve, rank_done, q)
                n = TILES * E
                link(v.tensor_tensor(t1[:], b_rt[:, 0:n].rearrange("p (t e) -> p t e", e=E),
                                     base[:].unsqueeze(1).to_broadcast([P, TILES, E]), ALU.add))
                v.tensor_tensor(t2[:], t1[:], oh2[:], ALU.mult)
                link(v.tensor_tensor(base[:], base[:], b_rt[:, n:n + E], ALU.add))
                link(v.tensor_tensor(t1[:], t1[:], oh1[:], ALU.mult))
                v.tensor_reduce(posf[:, 1, :], t2[:], AX.X, ALU.add)
                link(v.tensor_reduce(posf[:, 0, :], t1[:], AX.X, ALU.add))
                assert count[0] == RANK_LINKS, count
                if not isinstance(q, int) or q:
                    wait(dve, scat, q - 1)
                v.tensor_copy(posu[:], posf[:]).then_inc(pos_ready.sem, 1)

            def body(p):
                for name, n, q in steps(p, pairs):
                    if base_name(name) in do:
                        do[base_name(name)](q, n)

            do = {"stats1": stats1, "mean1": mean1, "variance1": variance1,
                  "mixed": mixed,
                  "clip_keys": clip_keys, "times_values": times_values,
                  "clip_receptance": clip_receptance, "denominators": denominators, "invert": invert,
                  "weigh": weigh, "residual": residual, "stats2": stats2, "mean2": mean2, "variance2": variance2,
                  "add_logit_bias": logits, "top2": top2, "second": second, "gates": gates,
                  "positions": positions}

            chain = [0]

            def link(ins):
                ins.then_inc(setup_link, 1)
                chain[0] += 1
                dve.wait_ge(setup_link, chain[0])

            v.memset(zrow[:, 0:128], 0.0).then_inc(setup_v, 1)
            v.memset(arena[KP:KP + 1, 0:IMG * PATCH:PATCH], 1.0).then_inc(ones_ready, 1)
            link(v.memset(mx[:], 0.0))
            v.memset(half3[:], -0.5)
            v.memset(zero2[:], 0.0)
            v.memset(sel16[:], 0.0).then_inc(setup_v, 1)
            dve.wait_ge(setup_p, 6)
            v.tensor_copy(id16[:], id32[:])
            v.tensor_copy(before[:], upto[:])
            v.tensor_copy(idf[:], idi[:])
            link(v.tensor_copy(tk[:], tki[:]))
            link(v.tensor_tensor(before[:], before[:], id16[:], ALU.subtract))
            for e in range(E):
                v.memset(rev[:, :, e], float(E - e))
                v.memset(rbase[:, e:e + 1], float(e * region))
            link(v.memset(ones16[:], 1.0))
            v.tensor_copy(base[:], rbase[:]).then_inc(setup_v, 1)
            dve.wait_ge(ld, 16 * 12)

            def largest(i, src, axis):
                link(v.tensor_reduce(mx[:, i:i + 1], src, axis, ALU.max, apply_absolute_value=True))

            for i in range(4):
                largest(i, raw_w[:, i], AX.XY)
            largest(4, raw_r1, AX.XY)
            largest(8, mixs[:], AX.XY)
            link(v.tensor_scalar(omm[:], mixs[:], -1.0, 1.0, ALU.mult, ALU.add))
            largest(9, omm[:], AX.XY)
            largest(10, zrow[:, 128:768], AX.X)
            for i in range(3):
                dve.wait_ge(ld_m[i], 16 * E)
                largest(5 + i, raw_e[:, :, i].rearrange("p e c n -> p e (c n)"), AX.XY)
            dve.wait_ge(ld_e, 16 * 3)
            largest(11, raw_b[:, 0:12], AX.X)
            v.tensor_reduce(mx[:, 12:13], raw_b[:, 12:24], AX.X, ALU.max, apply_absolute_value=True).then_inc(
                amax_ready, 1)
            dve.wait_ge(setup_p, 7)

            def a(i):
                return mxa[:, i:i + 1]

            link(v.tensor_copy(bd[:, 0:8], mxa[:, 0:8]))
            link(v.tensor_scalar(bd[:, 8:9], a(8), a(9), 16.0, ALU.add, ALU.mult))
            link(v.tensor_scalar(bd[:, 9:10], bd[:, 8:9], a(1), 16.0, ALU.mult, ALU.mult))
            link(v.tensor_scalar(bd[:, 9:10], bd[:, 9:10], a(10), None, ALU.mult))
            link(v.tensor_scalar(bd[:, 10:11], a(5), 256.0, a(11), ALU.mult, ALU.add))
            link(v.tensor_scalar(bd[:, 11:12], bd[:, 10:11], a(6), 256.0, ALU.mult, ALU.mult))
            link(v.tensor_scalar(bd[:, 11:12], bd[:, 11:12], a(12), None, ALU.add))
            link(v.tensor_scalar(bd[:, 0:NS], bd[:, 0:NS], 1e-12, None, ALU.max))
            link(v.tensor_scalar(bd[:, 0:NS].bitcast(U32), bd[:, 0:NS].bitcast(U32), 0x7F800000, None,
                                 ALU.bitwise_and))
            link(v.reciprocal(sc[:, 0:NS], bd[:, 0:NS]))
            link(v.tensor_scalar(sc[:, 0:NS], sc[:, 0:NS], SLACK, None, ALU.mult))
            link(v.tensor_scalar(isc[:, 0:NS], bd[:, 0:NS], 1.0 / SLACK, None, ALU.mult))
            link(v.memset(un[:], 0.0))
            link(v.tensor_scalar(un[:, 0:3], isc[:, 0:3], isc[:, S_MIX:S_MIX + 1], None, ALU.mult))
            link(v.tensor_scalar(un[:, 2:3], un[:, 2:3], -1.0, None, ALU.mult))
            link(v.tensor_scalar(un[:, 3:4], isc[:, 3:4], isc[:, S_RW:S_RW + 1], None, ALU.mult))
            link(v.tensor_scalar(un[:, 4:5], isc[:, 4:5], 1.0 / LN_SCALE, None, ALU.mult))
            link(v.tensor_scalar(un[:, 5:6], isc[:, 5:6], 1.0 / LN_SCALE, sc[:, S_H1:S_H1 + 1], ALU.mult, ALU.mult))
            link(v.tensor_scalar(un[:, 6:7], isc[:, 6:7], isc[:, S_H1:S_H1 + 1], sc[:, S_H2:S_H2 + 1], ALU.mult,
                                 ALU.mult))
            link(v.tensor_scalar(un[:, 7:8], isc[:, 7:8], isc[:, S_H2:S_H2 + 1], None, ALU.mult))
            link(v.tensor_scalar(un[:, 9:10], isc[:, S_MIX:S_MIX + 1], isc[:, S_MIX:S_MIX + 1], None, ALU.mult))
            link(v.tensor_scalar(un[:, 12:13], sc[:, 0:1], sc[:, S_MIX:S_MIX + 1], None, ALU.mult))
            link(v.tensor_scalar(un[:, 10:11], un[:, 12:13], -60.0, None, ALU.mult))
            link(v.tensor_tensor(un[:, 14:15], sc[:, 2:3], sc[:, S_MIX:S_MIX + 1], ALU.mult))
            link(v.tensor_scalar(un[:, 13:14], un[:, 14:15], -50.0, None, ALU.mult))
            v.tensor_scalar(un[:, 11:12], un[:, 12:13], 30.0, None, ALU.mult).then_inc(scales_ready, 1)
            dve.wait_ge(skew_out, 16)
            for i in range(4):
                dve.wait_ge(wsplit, i + 1)
                v.scalar_tensor_tensor(wl[:, i], raw_w[:, i], col(sc, i), wh[:, i], ALU.mult,
                                       ALU.subtract).then_inc(split_ready, 1)
            dve.wait_ge(wsplit, 5)
            v.scalar_tensor_tensor(rwa[:, 1], raw_r1, col(sc, 4), rwa[:, 0], ALU.mult, ALU.subtract).then_inc(
                split_ready, 1)
            dve.wait_ge(setup_p, 5)
            v.tensor_copy(filler[:, :, D + E:D + E + 1].bitcast(U32), fill_id[:].unsqueeze(2)).then_inc(setup_v, 1)
            for e in range(E):
                for i in range(3):
                    dve.wait_ge(pkh_ready, 4 * e + i + 1)
                    m = packm[place_of[e]]
                    last = v.scalar_tensor_tensor(m[:, i, 1], raw_e[:, e, i], col(sc, 5 + i), m[:, i, 0], ALU.mult,
                                                  ALU.subtract)
                last.then_inc(pk_ready, 1)
            dve.wait_ge(pk_ready, E)
            v.memset(arena[KP:KP + 1, IMG * PATCH:PAIR * PATCH:PATCH], 1.0).then_inc(ones_ready, 1)
            dve.wait_ge(pk_out[2], 32)
            v.memset(row[:, :, ROW - 1:ROW], 0.0)
            iterations(dve, body, pairs)
            stage_b_vector(dve)

        @block.gpsimd
        def _(pool):
            g_ = nc.gpsimd

            def difference(q, g):
                wait(pool, y1t_ready, q, 3 * g + 2)
                wait(pool, xf_ready, q if g else q - 1, 3 * g - 1 if g else None)
                for c in range(2):
                    last = g_.tensor_tensor(out_of(g, diff[:, c, :]), at(g, c, 1), at(g, c, 0), ALU.subtract)
                last.then_inc(diff_ready.sem, 1)

            def low_keys(q, g):
                wait(pool, xh_ready, q, 3 * g)
                s = group_slot(g)
                g_.tensor_tensor(xl[:, 0, :, s], xf[:, (3 * g) % 2], xh[:, 0, :, s], ALU.subtract).then_inc(
                    xl_ready.sem, 1)

            def low_half(q, m):
                n, i = m // 2, 1 + m % 2
                wait(pool, xh_ready, q, 3 * n + i)
                g_.tensor_tensor(xl[:, i, :, group_slot(n)], xf[:, (3 * n + i) % 2], xh[:, i, :, group_slot(n)],
                                 ALU.subtract).then_inc(xl_pool.sem, 1)

            def low_sum(q, n):
                wait(pool, rwh_ready, q, n)
                f, s = block_of(n)[2], block_cols(n)
                g_.tensor_tensor(rwl[:, f, s], gate[:, f, s], rwh[:, f, s], ALU.subtract).then_inc(rwl_ready.sem, 1)

            def root1(q, g):
                wait(pool, ve1_ready, q, g)
                wait(pool, y1_ready, q if g else q - 1, 3 * g - 1 if g else None)
                wait(pool, rs1_ready, *group_before(q, g))
                g_.tensor_tensor(mm1[:], mv1[:, :, 0], minus3[:], ALU.mult).then_inc(mm1_ready.sem, 1)
                g_.tensor_tensor(rs1[:], ve1[:], half3[:], ALU.pow).then_inc(pow1_ready.sem, 1)
                wait(pool, mm1_ready, q, g)
                wait(pool, pow1_ready, q, g)
                g_.tensor_tensor(nm1[:], mm1[:], rs1[:], ALU.mult).then_inc(rs1_ready.sem, 1)

            def root2(q, g):
                wait(pool, ve2_ready, q, g)
                wait(pool, y2_ready, q if g else q - 1, 3 * g - 1 if g else None)
                wait(pool, rs2_ready, *group_before(q, g))
                g_.tensor_tensor(mm2[:], mv2[:, :, 0], minus3[:], ALU.mult).then_inc(mm2_ready.sem, 1)
                g_.tensor_tensor(rs2[:], ve2[:], half3[:], ALU.pow).then_inc(pow2_ready.sem, 1)
                wait(pool, mm2_ready, q, g)
                wait(pool, pow2_ready, q, g)
                g_.tensor_tensor(nm2[:], mm2[:], rs2[:], ALU.mult).then_inc(rs2_ready.sem, 1)

            def norm2_low(q, t):
                wait(pool, yh_ready, q, t)
                g_.tensor_tensor(row[:, t, P:D].bitcast(F16), y2[:, t % 3, :], row[:, t, 0:P].bitcast(F16),
                                 ALU.subtract).then_inc(yl_ready.sem, 1)

            def scatter(q, n):
                wait(pool, gw_ready, q)
                hold(pool, pool_hold, pos_ready, q)
                for i in range(2):
                    g_.indirect_dma_start(lists, bass.IndirectOffsetOnAxis(ap=posu[:, i, n:n + 1], axis=0),
                                          row[:, n, :], None).then_inc(scat.sem, 16)

            do = {"difference": difference, "low_keys": low_keys,
                  "low_half": low_half, "low_sum": low_sum, "root1": root1, "root2": root2,
                  "norm2_low": norm2_low, "scatter": scatter}

            def body(p):
                for name, n, q in steps(p, pairs):
                    if base_name(name) in do:
                        do[base_name(name)](q, n)

            g_.memset(id32[:], 0.0).then_inc(setup_p, 1)
            g_.memset(upto[:], 1.0).then_inc(setup_p, 1)
            g_.memset(minus3[:], -1.0).then_inc(setup_p, 1)
            pool.wait_ge(setup_p, 3)
            g_.memset(filler[:], 0.0).then_inc(setup_p, 1)
            g_.iota(fill_id[:], pattern=[[P, 4]], base=tokens, channel_multiplier=1).then_inc(setup_p, 1)
            g_.affine_select(out=id32[:], in_=id32[:], compare_op=ALU.not_equal, fill=1.0, base=0, pattern=[[-1, P]],
                             channel_multiplier=1)
            g_.affine_select(out=upto[:], in_=upto[:], compare_op=ALU.is_ge, fill=0.0, base=0, pattern=[[1, P]],
                             channel_multiplier=-1)
            g_.iota(tki[:], pattern=[[1, btiles]], base=0, channel_multiplier=0)
            g_.iota(idi[:], pattern=[[P, TILES]], base=0, channel_multiplier=1).then_inc(setup_p, 1)
            pool.wait_ge(amax_ready, 1)
            g_.partition_all_reduce(mxa[:], mx[:], P, bass.bass_isa.ReduceOp.max).then_inc(setup_p, 1)
            pool.wait_ge(setup_v, 3)
            iterations(pool, body, pairs)
            stage_b_pool(pool)


def kernel(x, L0_tok_W, L0_tok_b, L0_attn_time_w, L0_attn_time_mix_k, L0_attn_time_mix_v, L0_attn_time_mix_r,
           L0_attn_Wk, L0_attn_Wv, L0_attn_Wr, L0_attn_Wo, L0_ffn_router_w1, L0_ffn_router_b1, L0_ffn_router_w2,
           L0_ffn_router_b2, L0_ffn_expert_w1, L0_ffn_expert_b1, L0_ffn_expert_w2, L0_ffn_expert_b2,
           L0_ffn_expert_w3, L0_ffn_expert_b3):
    from concourse import bacc
    from concourse.bass_utils import run_bass_kernel_spmd

    def spread(a):
        a = np.asarray(a).reshape(1, -1)
        return np.broadcast_to(a, (P, a.shape[1]))

    def by_partition(a):
        return np.asarray(a).reshape(-1, 2, P).transpose(2, 0, 1).reshape(P, -1)

    mixes = np.stack([np.asarray(m).reshape(D) for m in (L0_attn_time_mix_k, L0_attn_time_mix_v,
                                                         L0_attn_time_mix_r)])
    arrays = {
        "x": np.asarray(x),
        "tok_w": np.asarray(L0_tok_W).reshape(D, CH, PATCH, 2, QS).transpose(3, 1, 2, 4, 0).reshape(KP, QS, D),
        "tok_b": np.asarray(L0_tok_b).reshape(1, D),
        "decay": spread(np.asarray(L0_attn_time_w)[::-1][:640]),
        "mix": by_partition(mixes).reshape(P, 3, 2),
        "wk": L0_attn_Wk, "wv": L0_attn_Wv, "wr": L0_attn_Wr, "wo": L0_attn_Wo,
        "rw1": L0_ffn_router_w1, "rb1": np.asarray(L0_ffn_router_b1).reshape(P, 1),
        "rw2": L0_ffn_router_w2, "rb2": spread(L0_ffn_router_b2),
        "ew1": L0_ffn_expert_w1, "eb1": by_partition(L0_ffn_expert_b1),
        "ew2": L0_ffn_expert_w2, "eb2": by_partition(L0_ffn_expert_b2),
        "ew3": L0_ffn_expert_w3,
        "eb3": np.broadcast_to(np.asarray(L0_ffn_expert_b3).reshape(1, E, D), (P, E, D)),
    }
    arrays = {n: np.ascontiguousarray(a) for n, a in arrays.items()}
    images = arrays["x"].shape[0]
    nc = bacc.Bacc("TRN2", target_bir_lowering=False, num_devices=1)
    args = {n: nc.dram_tensor(f"in_{n}", a.shape, mybir.dt.from_np(a.dtype), kind="ExternalInput").ap()
            for n, a in arrays.items()}
    out = nc.dram_tensor("out_rows", (images * IMG + BT, D), F32, kind="ExternalOutput").ap()
    build(nc, out=out, **args)
    r = run_bass_kernel_spmd(nc, [{f"in_{n}": a for n, a in arrays.items()}], core_ids=[0])
    return r.results[0]["out_rows"][:images * IMG].reshape(images, IMG, D)
```
